# Optimizing a Trainium2 kernel written in Bass

```python
import numpy as np
import jax
import jax.numpy as jnp

def _softmax(x, axis=-1):
    return jax.nn.softmax(x, axis=axis)

def _gelu(x):
    return jax.nn.gelu(x, approximate=True)

def _silu(x):
    return jax.nn.silu(x)

def _sigmoid(x):
    return jax.nn.sigmoid(x)

def _layernorm(x, axis=-1, eps=1e-05):
    m = jnp.mean(x, axis=axis, keepdims=True)
    v = jnp.var(x, axis=axis, keepdims=True)
    return (x - m) / jnp.sqrt(v + eps)

def _scatter_add(tgt, idx, src, axis=0):
    return tgt.at[idx].add(src)

def _segment_sum(src, seg, n):
    return jax.ops.segment_sum(src, seg, n)
kernel_name = 'mk_gnn_preln_d2_gnn_r64_1d6bbd'

def setup_inputs(seed: int=0):
    np.random.seed(seed)
    _w = jnp.asarray

    def _rec_inputs():
        import jax
        import jax.numpy as jnp
        _gk = jax.random.key(seed)
        x = -0.000202 + 1 * jax.random.normal(jax.random.fold_in(_gk, 1), (50000, 128), jnp.float32)
        src = jax.random.randint(jax.random.fold_in(_gk, 2), (12500,), 0, 50000, jnp.int32)
        dst = jnp.minimum((50000 * jax.random.uniform(jax.random.fold_in(_gk, 3), (12500,)) ** 2.0).astype(jnp.int32), 49999)
        _o = jnp.argsort(dst, stable=True)
        src = src[_o]
        dst = dst[_o]
        edge_attr_128 = -8.16379e-05 + 0.999858 * jax.random.normal(jax.random.fold_in(_gk, 12), (12500, 128), jnp.float32)
        return (x, src, dst, edge_attr_128)
    x, src, dst, edge_attr_128 = _rec_inputs()

    def _L0_gnn_setup():
        import jax, jax.numpy as jnp
        import numpy as np
        LN_EPS = 1e-05
        N, E, D = (50000, 12500, 128)
        H = 4 * D
        key = jax.random.key(seed)
        ks = jax.random.split(key, 8)
        h = jax.random.normal(ks[0], (N, D), dtype=jnp.float32)
        e_ij = jax.random.normal(ks[1], (E, D), dtype=jnp.float32)
        src = jax.random.randint(ks[2], (E,), 0, N, dtype=jnp.int32)
        dst = jax.random.randint(ks[3], (E,), 0, N, dtype=jnp.int32)
        W1 = jax.random.normal(ks[4], (D, H), dtype=jnp.float32) / np.sqrt(D)
        b1 = jnp.zeros((H,), dtype=jnp.float32)
        W2 = jax.random.normal(ks[5], (H, D), dtype=jnp.float32) / np.sqrt(H)
        b2 = jnp.zeros((D,), dtype=jnp.float32)
        gamma = jnp.ones((D,), dtype=jnp.float32)
        beta = jnp.zeros((D,), dtype=jnp.float32)
        return {'h': h, 'e_ij': e_ij, 'src': src, 'dst': dst, 'W1': W1, 'b1': b1, 'W2': W2, 'b2': b2, 'gamma': gamma, 'beta': beta}
    _L0_gnn_all = _L0_gnn_setup()
    _L0_gnn_in = {k: v for k, v in _L0_gnn_all.items() if k in ('W1', 'b1', 'W2', 'b2', 'gamma', 'beta')}
    del _L0_gnn_all

    def _L1_gnn_setup():
        import jax, jax.numpy as jnp
        import numpy as np
        N = 625
        E = 10000
        D = 128
        key = jax.random.key(seed)
        ks = jax.random.split(key, 9)
        s2 = 1.0 / np.sqrt(2 * D)
        s1 = 1.0 / np.sqrt(D)
        return {'nodes': jax.random.normal(ks[0], (N, D), jnp.float32), 'edge_index': jax.random.randint(ks[1], (2, E), 0, N, jnp.int32), 'edge_features': jax.random.normal(ks[2], (E, D), jnp.float32), 'mw1': jax.random.uniform(ks[3], (2 * D, D), jnp.float32, -s2, s2), 'mb1': jax.random.uniform(ks[4], (D,), jnp.float32, -s2, s2), 'uw1': jax.random.uniform(ks[5], (2 * D, D), jnp.float32, -s2, s2), 'ub1': jax.random.uniform(ks[6], (D,), jnp.float32, -s2, s2), 'uw2': jax.random.uniform(ks[7], (D, D), jnp.float32, -s1, s1), 'ub2': jax.random.uniform(ks[8], (D,), jnp.float32, -s1, s1)}
    _L1_gnn_all = _L1_gnn_setup()
    _L1_gnn_in = {k: v for k, v in _L1_gnn_all.items() if k in ('mw1', 'mb1', 'uw1', 'ub1', 'uw2', 'ub2')}
    del _L1_gnn_all
    return {'x': x, 'src': src, 'dst': dst, 'edge_attr_128': edge_attr_128, 'L0_gnn_W1': _L0_gnn_in['W1'], 'L0_gnn_b1': _L0_gnn_in['b1'], 'L0_gnn_W2': _L0_gnn_in['W2'], 'L0_gnn_b2': _L0_gnn_in['b2'], 'L0_gnn_gamma': _L0_gnn_in['gamma'], 'L0_gnn_beta': _L0_gnn_in['beta'], 'L1_gnn_mw1': _L1_gnn_in['mw1'], 'L1_gnn_mb1': _L1_gnn_in['mb1'], 'L1_gnn_uw1': _L1_gnn_in['uw1'], 'L1_gnn_ub1': _L1_gnn_in['ub1'], 'L1_gnn_uw2': _L1_gnn_in['uw2'], 'L1_gnn_ub2': _L1_gnn_in['ub2']}

def reference(x, src, dst, edge_attr_128, L0_gnn_W1, L0_gnn_b1, L0_gnn_W2, L0_gnn_b2, L0_gnn_gamma, L0_gnn_beta, L1_gnn_mw1, L1_gnn_mb1, L1_gnn_uw1, L1_gnn_ub1, L1_gnn_uw2, L1_gnn_ub2):
    import jax
    import jax.numpy as jnp

    def _L0_gnn_ref(h, e_ij, src, dst, W1, b1, W2, b2, gamma, beta):
        import jax, jax.numpy as jnp
        import numpy as np
        LN_EPS = 1e-05
        N = h.shape[0]
        neigh = jax.ops.segment_sum(h[src], dst, num_segments=N)
        u_edge = jax.ops.segment_sum(e_ij, dst, num_segments=N)
        u = neigh + u_edge
        hid = jax.nn.relu(u @ W1 + b1)
        out = hid @ W2 + b2 + h
        mean = jnp.mean(out, axis=-1, keepdims=True)
        var = jnp.var(out, axis=-1, keepdims=True)
        normed = (out - mean) * jax.lax.rsqrt(var + LN_EPS)
        return normed * gamma + beta

    def _L1_gnn_ref(nodes, edge_index, edge_features, mw1, mb1, uw1, ub1, uw2, ub2):
        import jax, jax.numpy as jnp
        import numpy as np
        N = 625
        E = 10000
        D = 128
        src, dst = (edge_index[0], edge_index[1])
        msg_in = jnp.concatenate([nodes[src], edge_features], axis=1)
        messages = jax.nn.silu(msg_in @ mw1 + mb1)
        aggregated = jax.ops.segment_sum(messages, dst, num_segments=nodes.shape[0])
        upd_in = jnp.concatenate([nodes, aggregated], axis=1)
        updated = jax.nn.silu(upd_in @ uw1 + ub1) @ uw2 + ub2
        return nodes + updated
    edge_index = jnp.stack([src, dst])
    h = jnp.maximum(_layernorm(x, axis=-1), 0.0)
    x = x + _L0_gnn_ref(h, edge_attr_128, src, dst, L0_gnn_W1, L0_gnn_b1, L0_gnn_W2, L0_gnn_b2, L0_gnn_gamma, L0_gnn_beta)
    h = jnp.maximum(_layernorm(x, axis=-1), 0.0)
    x = x + _L1_gnn_ref(h, edge_index, edge_attr_128, L1_gnn_mw1, L1_gnn_mb1, L1_gnn_uw1, L1_gnn_ub1, L1_gnn_uw2, L1_gnn_ub2)
    return x

_drawn_inputs = setup_inputs


def setup_inputs(seed=0):
    import zlib

    import numpy as np

    out = dict(_drawn_inputs(seed))
    spreads = {'L0_gnn_b1': (0.0, 0.1),
     'L0_gnn_b2': (0.0, 0.1),
     'L0_gnn_gamma': (1.0, 0.2),
     'L0_gnn_beta': (0.0, 0.1)}
    factors = {'L1_gnn_mw1': 8.0, 'L1_gnn_mb1': 58.353, 'L1_gnn_ub1': 8.0, 'L1_gnn_ub2': 2.696}
    for name, (base, spread) in spreads.items():
        noise = np.random.default_rng([zlib.crc32(name.encode()), seed]).standard_normal(out[name].shape)
        drawn = base * np.exp(spread * noise) if base else spread * noise
        out[name] = jnp.asarray(drawn.astype(out[name].dtype))
    for name, factor in factors.items():
        out[name] = (out[name] * factor).astype(out[name].dtype)
    return out
```

```python
from contextlib import ExitStack

import concourse.bass as bass
from concourse import mybir

F32 = mybir.dt.float32
I32 = mybir.dt.int32
BF16 = mybir.dt.bfloat16
ALU = mybir.AluOpType
ACT = mybir.ActivationFunctionType
AX_X = mybir.AxisListType.X

P = 128
G = 7
GR = G * P
BODY = 4
EPS = 1e-5
FAR = 1 << 17
MAGIC = 1597463007.0
CHAIN = 16

SRC, DST, DENSE = "src", "dst", "dense"


def plan(n_edge_groups, n_dense_groups):
    first = [SRC, DENSE] * n_edge_groups
    gap = [DENSE] * 4
    second = [DST, DENSE] * n_edge_groups
    rest = [DENSE] * (n_dense_groups - 2 * n_edge_groups - 4)
    kinds = first + gap + second + rest
    lag, ahead = 8, 3
    loops = []
    start = 0
    for part in (first, gap, second, rest):
        lo, hi = start + lag + (BODY if start == 0 else 0), start + len(part) - ahead
        if hi - lo >= 2 * BODY:
            lo += (start - lo) % BODY
            loops.append((lo, lo + (hi - lo) // BODY * BODY))
        start += len(part)
    return kinds, loops, len(first)


class Tick:

    def __init__(self, s, body=None, bodies=1):
        self.s, self.body, self.bodies = s, body, bodies

    def at(self, f, back=0):
        q = self.s - back
        if self.body is None:
            return f(q)
        step = f(q + BODY) - f(q)
        assert f(q + (self.bodies - 1) * BODY) == f(q) + (self.bodies - 1) * step
        return f(q) + (self.body * step if step else 0)


def gnn_program(nc, x, e, src_t, dst_t, prev_t, keys, after, ident, edge_no, w1, b1, w2, b2, gamma, beta,
                mw1, mb1, uw1, ub1, uw2, ub2, out):
    N, D = x.shape
    NT = src_t.shape[1]
    NE = NT * P
    NG = NT // G
    HID = w1.shape[1]
    HC = HID // P
    ND = -(-N // GR)
    assert D == P and NT % G == 0 and NG % 2 == 0

    kinds, loops, src_span = plan(NG, ND)
    NQ = len(kinds)
    MEET = src_span + 1
    TICKS = NQ + 8

    def is_kind(q, *which):
        return 0 <= q < NQ and kinds[q] in which

    def exists(q):
        return 0 <= q < NQ

    def count(q, *which):
        return sum(k in which for k in kinds[:max(q + 1, 0)])

    def number(q):
        return count(q, kinds[q]) - 1

    def through_dst(q):
        return max([i + 1 for i in range(min(q + 1, NQ)) if kinds[i] == DST], default=0)

    def x_loads(q):
        return sum(16 for i in range(q % 4, q + 1, 4) if kinds[i] == DENSE)

    def x_gathers(q):
        return 16 * G * ((count(q, SRC, DST) - 1) // 2 + 1)

    def wait_x(eng, t, x_loaded, x_gathered, back=0):
        q = t.s - back
        if kinds[q] == DENSE:
            eng.wait_ge(x_loaded[q % 4], t.at(x_loads, back))
        else:
            eng.wait_ge(x_gathered[(count(q, SRC, DST) - 1) % 2], t.at(x_gathers, back))

    def ring(q, each=16):
        return (number(q) // 2 + 1) * each

    def stores(q, *which):
        return sum(16 for i in range(q % 2, min(q + 1, NQ), 2) if kinds[i] in which)

    def dense_row(q):
        n = number(q)
        return 0 if n == 0 else N - GR * (ND - n)

    def run(eng, step, first, ticks, loops, meets={}):
        s = first
        for lo, hi in [*loops, (ticks, ticks)]:
            for s in range(s, lo):
                if s in meets:
                    meets[s]()
                step(Tick(s))
            if hi > lo:
                with eng.Fori(0, (hi - lo) // BODY) as body:
                    for u in range(BODY):
                        step(Tick(lo + u, body, (hi - lo) // BODY))
            s = hi

    ctx = ExitStack()
    with ctx:
        def sb(name, shape, dt=F32):
            return ctx.enter_context(nc.sbuf_tensor(name, shape, dt))

        def sem(name):
            return ctx.enter_context(nc.semaphore(name))

        def sems(name, n):
            return [sem(f"{name}_{i}") for i in range(n)]

        def tiles(name, n):
            return [sb(f"{name}_{i}", [P, G, D]) for i in range(n)]

        v_d = nc.dram_tensor("v_scratch", (NE + P, D), F32).ap()
        m_d = nc.dram_tensor("msg_scratch", (NE + P, D), F32).ap()
        fix_d = nc.dram_tensor("sum_scratch", (NE, D), F32).ap()
        hs_d = nc.dram_tensor("h1_src_scratch", (NE, D), F32).ap()
        hd_d = nc.dram_tensor("h1_dst_scratch", (NE, D), F32).ap()
        zd_d = nc.dram_tensor("x1_h1_dst_scratch", (NE, D), F32).ap()
        slot_d = nc.dram_tensor("slot_of_node_scratch", (N, 1), I32).ap()

        X = tiles("x_in", 4)
        XB = tiles("x_beta", 4)
        W = tiles("work", 4)
        Z = tiles("x1", 4)
        H1 = tiles("h1", 2)
        ZH = tiles("x1_h1", 2)
        Y = tiles("y", 2)
        HT = tiles("h1T", 2)
        S1 = tiles("silu", 2)
        E = tiles("e_in", 2)
        V = tiles("v", 2)
        VG = [sb(f"v_window_{i}", [P, G + 1, D]) for i in range(2)]
        KR = [sb(f"key_row_{i}", [P, GR], I32) for i in range(2)]
        EQ = sb("equal", [P, G + 1, 2 * P])
        KC = sb("key_col_group", [P, G + 1])
        UT = sb("uT", [P, GR])
        HD = sb("hidden", [P, HC, GR])
        IX = [sb(f"gather_index_{i}", [P, G], I32) for i in range(2)]
        MX = [sb(f"map_index_{i}", [P, G], I32) for i in range(2)]
        MV = [sb(f"map_value_{i}", [P, G], I32) for i in range(2)]
        ST = [sb(f"stats_{i}", [P, 3, G, 6]) for i in range(2)]
        RS = [sb(f"rstd_{i}", [P, 3, G]) for i in range(2)]
        NB = [sb(f"minus_mean_rstd_{i}", [P, 3, G]) for i in range(2)]
        CS = sb("chain", [P, 8, 3, G])

        W1 = sb("W1", [P, HID])
        W2 = sb("W2", [P, HC, D])
        B1 = sb("B1", [P, HC])
        RB = sb("relu_b1", [P, HC, P])
        CR = sb("c_row", [P, D])
        GM = sb("gamma_row", [P, D])
        BT = sb("beta_row", [P, D])
        MW = sb("MW1", [P, 2, D])
        UW = sb("UW1", [P, 2, D])
        U2 = sb("UW2", [P, D])
        UB = sb("UB1", [P, 1])
        ID = sb("ident", [P, P])
        BR = sb("bias_rows", [3, 3, D])
        BS = sb("bias_rest", [3, 3, 3, D])
        BH = sb("bias_high", [3, 3, 3, D], BF16)
        B3 = sb("bias_parts", [3, 3, 4, D], BF16)
        ONE3 = sb("ones3", [3, P], BF16)
        ONES = sb("ones", [P, P])
        SRCI = sb("src_index", [P, NT], I32)
        DSTI = sb("dst_key", [P, NT + 1], I32)
        PRVI = sb("prev_key", [P, NT], I32)
        ENO = sb("edge_number", [P, NT], I32)
        KCF = sb("key_col", [P, NT + 1])
        PKF = sb("prev_key_f", [P, NT])
        ENF = sb("edge_number_f", [P, NT])
        LEAD = sb("leader", [P, NT])
        DGI = sb("dst_gather_index", [P, NT], I32)
        LIX = sb("leader_index", [P, NT], I32)
        SLOT = sb("slot_of_src", [P, NT], I32)
        BAD = sb("bad", [P, 4])
        FST = sb("first_of_key", [P, NT])
        FM = sb("first_in_chunk", [P, 1])
        AFT = sb("edges_to_the_end", [P, NT])
        ZERO = sb("zeros", [3, 512], BF16)
        SINK = sb("sink", [1, 1])
        BADI = sb("bad_i", [1, 1], I32)
        FARI = sb("far", [80, N // 80], I32)

        PS = [ctx.enter_context(nc.psum_tensor(f"ps{i}", [P, 1024], F32)) for i in range(4)]
        HALVES = ((0, 512), (512, GR))

        def flat(t):
            return t[:].rearrange("p t d -> p (t d)")

        def each(row):
            return row[:].unsqueeze(1).broadcast_to([P, G, D])

        def edge_rows(d, row, n=G):
            return d[bass.ds(row, n * P), :].rearrange("(t p) d -> p t d", p=P)

        def node_rows(d, row):
            return d[bass.ds(row, GR), :].rearrange("(p t) d -> p t d", t=G)

        consts_in = sem("consts_in")
        tables_in = sem("tables_in")
        filled = sem("filled")
        prep = sem("prep")
        prep_pe = sem("prep_pe")
        slots_cleared = sem("slots_cleared")
        ready = sem("ready")
        flag_ready = sem("order_flag_ready")
        first_in = sem("first_keys_loaded")
        first_key = sem("first_key_col_done")
        first_done = sem("first_of_key_steps")
        first_ends = sem("first_of_key_ends")
        targets = sems("sums_keys_loaded_and_sums_stored", 2)
        source_in = sems("sums_source_loaded", 2)
        sums_mm = sems("sums_mm", 2)
        sums_equal = sems("sums_equal_done", 2)
        sums_key = sems("sums_key_col_done", 2)
        sums_done = sems("sums_done", 2)
        sums_moved = sems("sums_moved", 2)
        x_loaded = sems("x_loaded", 4)
        x_gathered = sems("x_gathered", 2)
        x_beta = sem("x_beta_done")
        h_done = sem("h_done")
        g_done = sem("g_done")
        n_done = sem("n_done")
        mul_done = sem("mul_done")
        z_done = sem("z_done")
        st_done = sem("st_done")
        chain_done = sem("chain_done")
        h1_done = sem("h1_done")
        zh_done = sem("zh_done")
        e_loaded = sems("e_loaded", 2)
        v_done = sem("v_done")
        v_stored = sems("v_stored", 2)
        window_loaded = sems("window_loaded", 2)
        kc_done = sem("kc_done")
        eq_done = sem("eq_done")
        seg_done = sem("seg_done")
        ut_done = sem("ut_done")
        hid_mm = sem("hid_mm")
        hid_act = sem("hid_act")
        m_done = sem("m_done")
        t_done = sem("t_done")
        ht_done = sem("ht_done")
        u_done = sem("u_done")
        silu_done = sem("silu_done")
        y_mm = sem("y_mm")
        y_done = sem("y_done")
        y_stored = sems("y_stored", 2)
        h1_stored = sems("h1_stored", 2)
        zh_stored = sems("zh_stored", 2)
        index_done = sem("index_done")
        map_index_done = sem("map_index_done")
        slots_set = sems("slots_set", 2)
        slots_got = sems("slots_got", 2)
        slot_kept = sem("slot_kept")

        hs_in = sems("msg_h_loaded", 2)
        ms_in = sems("msg_e_loaded", 2)
        over = sems("msg_h_replaced", 2)
        mi_done = sem("msg_index_done")
        mt_done = sem("msg_transposed")
        mh_done = sem("msg_hT_done")
        me_done = sem("msg_eT_done")
        mm_done = sem("msg_mm")
        msg_done = sem("msg_done")
        msg_stored = sems("msg_stored", 2)
        up_in = sems("upd_window_loaded", 2)
        uh_in = sems("upd_h1_loaded", 2)
        uz_in = sems("upd_x1_h1_loaded", 4)
        uk_done = sem("upd_key_col_done")
        uq_done = sem("upd_equal_done")
        us_done = sem("upd_sums")
        ut2_done = sem("upd_transposed")
        ua_done = sem("upd_aT_done")
        uh_done = sem("upd_hT_done")
        um_done = sem("upd_u_mm")
        usilu_done = sem("upd_silu_done")
        uy_mm = sem("upd_y_mm")
        uy_done = sem("upd_y_done")
        ui_done = sem("upd_index_done")
        scattered = sems("upd_scattered", 2)

        def equal_tiles(dve, row):
            for j in range(G + 1):
                lo, hi = max(j - 1, 0) * P, min(j + 1, G) * P
                at = P if j == 0 else 0
                ins = dve.tensor_scalar(EQ[:, j, at:at + hi - lo], row[:, lo:hi], KC[:, j:j + 1], None, ALU.is_equal)
            return ins

        def neighbour_sums(pe, ps, rows):
            for u in range(G):
                own = u * P, (u + 1) * P
                pe.matmul(ps[:, own[0]:own[1]], rows[:, u, :], EQ[:, u, P:2 * P],
                          start=(u * P % 512 == 0), stop=False, skip_group_check=True)
                ins = pe.matmul(ps[:, own[0]:own[1]], rows[:, u + 1, :], EQ[:, u + 1, 0:P],
                                start=False, stop=True, skip_group_check=True)
            return ins

        def bias(pe, ps, which):
            for lo, hi in HALVES:
                pe.matmul(ps[:, lo:hi], ONE3[:], B3[:, which].rearrange("k t d -> k (t d)")[:, 0:hi - lo],
                          start=True, stop=False, skip_group_check=True)

        def take_waits(pool):
            pool.tensor_tensor(SINK[:], ONES[0:1, 0:1], ONES[0:1, 0:1], ALU.mult)

        EDGE_TICKS = NG + 3
        edge_loops = [(4, 4 + (NG - 4) // BODY * BODY)]

        def group(t, back=0):
            return t.at(lambda q: q, back), 0 <= t.s - back < NG

        def messages_sync(sp):
            sp.wait_ge(h_done, NQ)
            sp.wait_ge(x_beta, NQ)
            sp.wait_ge(v_done, NG)

            def step(t):
                s = t.s
                i, there = group(t)
                if there:
                    k = s % 2
                    if s >= 2:
                        sp.wait_ge(mt_done, i - 1)
                    sp.dma_start(X[k][:], edge_rows(hs_d, i * GR)).then_inc(hs_in[k], 16)
                    sp.dma_start(E[k][:], edge_rows(e, i * GR)).then_inc(ms_in[k], 16)
                i, there = group(t, 2)
                if there:
                    sp.wait_ge(msg_done, i + 1)
                    sp.dma_start(edge_rows(m_d, i * GR), Y[s % 2][:]).then_inc(msg_stored[s % 2], 16)

            run(sp, step, 0, EDGE_TICKS, edge_loops)
            for k in range(2):
                sp.wait_ge(msg_stored[k], 16 * (NG // 2))

        def messages_pool(pool, last_edge):
            pool.wait_ge(h1_stored[0], stores(NQ, SRC, DST))
            pool.wait_ge(slot_kept, NG)

            def step(t):
                s = t.s
                i, there = group(t)
                if there:
                    k = s % 2
                    if s >= 2:
                        pool.wait_ge(over[k], t.at(lambda q: 16 * G * (q // 2)))
                    pool.tensor_copy(IX[k][:], SLOT[:, bass.ds(i * G, G)]).then_inc(mi_done, 1)
                    pool.wait_ge(mi_done, i + 1)
                    pool.wait_ge(hs_in[k], t.at(lambda q: 16 * (q // 2 + 1)))
                    take_waits(pool)
                    for u in range(G):
                        pool.indirect_dma_start(
                            out=X[k][:, u, :], out_offset=None, in_=hd_d,
                            in_offset=bass.IndirectOffsetOnAxis(ap=IX[k][:, u:u + 1], axis=0),
                            bounds_check=last_edge, oob_is_err=False).then_inc(over[k], 16)

            run(pool, step, 0, EDGE_TICKS, edge_loops)

        def messages_pe(pe):
            pe.wait_ge(ht_done, ND)
            pe.wait_ge(hid_act, HC * NG)
            pe.wait_ge(silu_done, ND)
            pe.wait_ge(y_done, ND)
            pe.wait_ge(g_done, NQ)

            def step(t):
                s = t.s
                i, there = group(t)
                if there:
                    k = s % 2
                    pe.wait_ge(over[k], t.at(lambda q: 16 * G * (q // 2 + 1)))
                    pe.wait_ge(ms_in[k], t.at(lambda q: 16 * (q // 2 + 1)))
                    if s >= 1:
                        pe.wait_ge(mh_done, i)
                    for u in range(G):
                        pe.transpose(PS[0][:, u * P:(u + 1) * P], X[k][:, u, :], ID[:])
                    if s >= 1:
                        pe.wait_ge(me_done, i)
                    for u in range(G):
                        ins = pe.transpose(PS[1][:, u * P:(u + 1) * P], E[k][:, u, :], ID[:])
                    ins.then_inc(mt_done, 1)
                i, there = group(t, 1)
                if there:
                    k = (s - 1) % 2
                    if s >= 3:
                        pe.wait_ge(msg_done, i - 1)
                    bias(pe, PS[2 + k], 1)
                    pe.wait_ge(mh_done, i + 1)
                    pe.wait_ge(me_done, i + 1)
                    for u in range(G):
                        own = PS[2 + k][:, u * P:(u + 1) * P]
                        pe.matmul(own, HT[k][:, u, :], MW[:, 0, :], start=False, stop=False, skip_group_check=True)
                        ins = pe.matmul(own, S1[k][:, u, :], MW[:, 1, :], start=False, stop=True, skip_group_check=True)
                    ins.then_inc(mm_done, 1)

            run(pe, step, 0, EDGE_TICKS, edge_loops)

        def messages_act(act):
            act.wait_ge(u_done, ND)
            for k in range(2):
                act.wait_ge(y_stored[k], 16 * (ND // 2))

            def step(t):
                s = t.s
                i, there = group(t)
                if there:
                    act.wait_ge(mt_done, i + 1)
                    if s >= 2:
                        act.wait_ge(mm_done, i - 1)
                    act.copy(flat(HT[s % 2]), PS[0][:, 0:GR]).then_inc(mh_done, 1)
                i, there = group(t, 2)
                if there:
                    act.wait_ge(mm_done, i + 1)
                    if s >= 4:
                        act.wait_ge(msg_stored[s % 2], t.at(lambda q: 16 * (q // 2), 2))
                    act.activation(flat(Y[s % 2]), PS[2 + s % 2][:, 0:GR], ACT.Silu).then_inc(msg_done, 1)

            run(act, step, 0, EDGE_TICKS, edge_loops)

        def messages_vector(dve):
            dve.wait_ge(y_mm, ND)

            def step(t):
                s = t.s
                i, there = group(t)
                if there:
                    dve.wait_ge(mt_done, i + 1)
                    if s >= 2:
                        dve.wait_ge(mm_done, i - 1)
                    dve.tensor_copy(flat(S1[s % 2]), PS[1][:, 0:GR]).then_inc(me_done, 1)

            run(dve, step, 0, EDGE_TICKS, edge_loops)

        def update_sync(sp):
            sp.wait_ge(seg_done, NG)
            sp.wait_ge(eq_done, NG)
            sp.wait_ge(h1_done, NQ)

            def step(t):
                s = t.s
                i, there = group(t)
                if there:
                    k = s % 2
                    if s >= 2:
                        sp.wait_ge(us_done, i - 1)
                        sp.wait_ge(ut2_done, i - 1)
                    sp.dma_start(VG[k][:], edge_rows(m_d, i * GR, G + 1)).then_inc(up_in[k], 16)
                    sp.dma_start(KR[k][:], keys[bass.ds(i * GR, GR)].partition_broadcast(P)).then_inc(up_in[k], 16)
                    sp.dma_start(X[2 + k][:], edge_rows(hd_d, i * GR)).then_inc(uh_in[k], 16)
                    if s >= 4:
                        sp.wait_ge(uy_done, i - 3)
                    sp.dma_start(Z[s % 4][:], edge_rows(zd_d, i * GR)).then_inc(uz_in[s % 4], 16)

            run(sp, step, 0, EDGE_TICKS, edge_loops)

        def update_vector(dve):
            def step(t):
                s = t.s
                i, there = group(t)
                if there:
                    k = s % 2
                    if s >= 1:
                        dve.wait_ge(uq_done, i)
                    dve.tensor_copy(KC[:], KCF[:, bass.ds(i * G, G + 1)]).then_inc(uk_done, 1)
                    dve.wait_ge(up_in[k], t.at(lambda q: 32 * (q // 2 + 1)))
                    if s >= 1:
                        dve.wait_ge(us_done, i)
                    dve.wait_ge(uk_done, i + 1)
                    equal_tiles(dve, KR[k]).then_inc(uq_done, 1)
                    dve.wait_ge(ut2_done, i + 1)
                    if s >= 2:
                        dve.wait_ge(um_done, i - 1)
                    dve.tensor_copy(flat(HT[k]), PS[1][:, 0:GR]).then_inc(uh_done, 1)
                i, there = group(t, 2)
                if there:
                    k = s % 2
                    dve.wait_ge(uy_mm, i + 1)
                    dve.wait_ge(uz_in[(s - 2) % 4], t.at(lambda q: 16 * (q // 4 + 1), 2))
                    if s >= 4:
                        dve.wait_ge(scattered[k], t.at(lambda q: 16 * G * (q // 2), 2))
                    dve.tensor_tensor(flat(Y[k]), PS[3][:, 0:GR], flat(Z[(s - 2) % 4]), ALU.add).then_inc(uy_done, 1)

            run(dve, step, 0, EDGE_TICKS, edge_loops)

        def update_act(act):
            def step(t):
                s = t.s
                i, there = group(t)
                if there:
                    k = s % 2
                    act.wait_ge(us_done, i + 1)
                    if s >= 2:
                        act.wait_ge(um_done, i - 1)
                    act.copy(flat(W[k]), PS[0][:, 0:GR]).then_inc(ua_done, 1)
                i, there = group(t, 1)
                if there:
                    k = (s - 1) % 2
                    act.wait_ge(um_done, i + 1)
                    if s >= 3:
                        act.wait_ge(uy_mm, i - 1)
                    act.activation(flat(S1[k]), PS[2][:, 0:GR], ACT.Silu, bias=UB[:, 0:1], scale=1.0).then_inc(usilu_done, 1)

            run(act, step, 0, EDGE_TICKS, edge_loops)

        def update_pe(pe):
            def step(t):
                s = t.s
                i, there = group(t)
                if there:
                    k = s % 2
                    pe.wait_ge(up_in[k], t.at(lambda q: 32 * (q // 2 + 1)))
                    pe.wait_ge(uq_done, i + 1)
                    if s >= 1:
                        pe.wait_ge(ua_done, i)
                    neighbour_sums(pe, PS[0], VG[k]).then_inc(us_done, 1)
                    pe.wait_ge(uh_in[k], t.at(lambda q: 16 * (q // 2 + 1)))
                    if s >= 1:
                        pe.wait_ge(uh_done, i)
                    for u in range(G):
                        ins = pe.transpose(PS[1][:, u * P:(u + 1) * P], X[2 + k][:, u, :], ID[:])
                    ins.then_inc(ut2_done, 1)
                i, there = group(t, 2)
                if there:
                    k = s % 2
                    if s >= 3:
                        pe.wait_ge(uy_done, i)
                    bias(pe, PS[3], 2)
                    pe.wait_ge(usilu_done, i + 1)
                    for u in range(G):
                        ins = pe.matmul(PS[3][:, u * P:(u + 1) * P], S1[k][:, u, :], U2[:],
                                        start=False, stop=True, skip_group_check=True)
                    ins.then_inc(uy_mm, 1)
                i, there = group(t, 1)
                if there:
                    k = (s - 1) % 2
                    if s >= 2:
                        pe.wait_ge(usilu_done, i)
                    pe.wait_ge(uh_done, i + 1)
                    pe.wait_ge(ua_done, i + 1)
                    for lo, hi in HALVES:
                        pe.matmul(PS[2][:, lo:hi], UW[:, 0, :], flat(HT[k])[:, lo:hi], start=True, stop=False)
                        ins = pe.matmul(PS[2][:, lo:hi], UW[:, 1, :], flat(W[k])[:, lo:hi], start=False, stop=True)
                    ins.then_inc(um_done, 1)

            pe.wait_ge(msg_done, NG)
            run(pe, step, 0, EDGE_TICKS, edge_loops)

        def update_pool(pool, last_node):
            for k in range(2):
                pool.wait_ge(y_stored[k], 16 * (ND // 2))
                pool.wait_ge(over[k], 16 * G * (NG // 2))

            def step(t):
                s = t.s
                i, there = group(t, 2)
                if there:
                    k = s % 2
                    if s >= 4:
                        pool.wait_ge(scattered[k], t.at(lambda q: 16 * G * (q // 2), 2))
                    pool.tensor_copy(IX[k][:], LIX[:, bass.ds(i * G, G)]).then_inc(ui_done, 1)
                    pool.wait_ge(ui_done, i + 1)
                    pool.wait_ge(uy_done, i + 1)
                    take_waits(pool)
                    for u in range(G):
                        pool.indirect_dma_start(
                            out=out, out_offset=bass.IndirectOffsetOnAxis(ap=IX[k][:, u:u + 1], axis=0),
                            in_=Y[k][:, u, :], in_offset=None,
                            bounds_check=last_node, oob_is_err=False).then_inc(scattered[k], 16)

            run(pool, step, 0, EDGE_TICKS, edge_loops)
            for k in range(2):
                pool.wait_ge(scattered[k], 16 * G * (NG // 2))


        def flagged(eng):
            return eng.value_load(BADI[0:1, 0:1])

        SETS = 1 + NT

        def leaders_sync(sp):
            sp.wait_ge(flag_ready, 1)
            with sp.If(flagged(sp)):
                with sp.Fori(0, NG) as c:
                    sp.wait_ge(first_done, c * (3 * NT) + 1)
                    sp.dma_start(KR[0][:], keys[bass.ds(c * GR, GR)].partition_broadcast(P)).then_inc(first_in, 16)
                    sp.dma_start(UT[:], after[bass.ds(c * GR, GR)].partition_broadcast(P)).then_inc(first_in, 16)

        def leaders_vector(dve):
            product = flat(EQ)[:, 0:GR]
            with dve.If(flagged(dve)):
                dve.memset(FST[:], 0.0).then_inc(first_done, 1)
                dve.wait_ge(first_done, 1)
                with dve.Fori(0, NG) as c:
                    with dve.Fori(0, NT) as i:
                        n = c * (3 * NT) + i * 3 + 1
                        dve.wait_ge(first_in, (c + 1) * 32)
                        dve.tensor_copy(KC[:, 0:1], KCF[:, bass.ds(i, 1)]).then_inc(first_key, 1)
                        dve.wait_ge(first_key, c * NT + i + 1)
                        dve.scalar_tensor_tensor(out=product, in0=KR[0][:], scalar=KC[:, 0:1], in1=UT[:],
                                                 op0=ALU.is_equal, op1=ALU.mult).then_inc(first_done, 1)
                        dve.wait_ge(first_done, n + 1)
                        dve.tensor_reduce(out=FM[:], in_=product, axis=AX_X, op=ALU.max).then_inc(first_done, 1)
                        dve.wait_ge(first_done, n + 2)
                        dve.tensor_tensor(FST[:, bass.ds(i, 1)], FST[:, bass.ds(i, 1)], FM[:], ALU.max).then_inc(first_done, 1)
                        dve.wait_ge(first_done, n + 3)
                dve.tensor_scalar(AFT[:], ENO[:], -1.0, float(NE), ALU.mult, ALU.add).then_inc(first_ends, 1)
                dve.wait_ge(first_ends, 1)
                dve.tensor_tensor(LEAD[:], AFT[:], FST[:], ALU.is_equal).then_inc(first_ends, 1)
                dve.wait_ge(first_ends, 2)

        def sums_sync(sp, layer):
            rows = (v_d, m_d)[layer]
            with sp.If(flagged(sp)):
                with sp.Fori(0, NG) as i:
                    sp.dma_start(KR[0][:], keys[bass.ds(i * GR, GR)].partition_broadcast(P)).then_inc(targets[layer], 16)
                    with sp.Fori(0, NG) as j:
                        sp.wait_ge(targets[layer], i * 32 + 16)
                        sp.wait_ge(sums_mm[layer], i * SETS + j * G + 1)
                        sp.dma_start(VG[0][:, 0:G, :], edge_rows(rows, j * GR)).then_inc(source_in[layer], 16)
                    sp.wait_ge(sums_done[layer], i + 1)
                    sp.dma_start(edge_rows(fix_d, i * GR), V[0][:]).then_inc(targets[layer], 16)
                sp.wait_ge(targets[layer], NG * 32)
                sp.dma_start(rows[0:NE, :], fix_d).then_inc(sums_moved[layer], 16)
                sp.wait_ge(sums_moved[layer], 16)

        def sums_pe(pe, layer):
            with pe.If(flagged(pe)):
                with pe.Fori(0, NG) as i:
                    pe.wait_ge(targets[layer], i * 32 + 16)
                    for lo, hi in HALVES:
                        ins = pe.matmul(PS[1][:, lo:hi], ONE3[:], ZERO[:, 0:hi - lo], start=True, stop=False,
                                        skip_group_check=True)
                    ins.then_inc(sums_mm[layer], 1)
                    with pe.Fori(0, NG) as j:
                        pe.wait_ge(source_in[layer], (i * NG + j + 1) * 16)
                        for v in range(G):
                            pe.wait_ge(sums_equal[layer], i * NT + j * G + v + 1)
                            for u in range(G):
                                ins = pe.matmul(PS[1][:, u * P:(u + 1) * P], HD[:, 0, u * P:(u + 1) * P], VG[0][:, v, :],
                                                start=False, stop=True, skip_group_check=True)
                            ins.then_inc(sums_mm[layer], 1)
                    pe.wait_ge(sums_done[layer], i + 1)

        def sums_vector(dve, layer):
            with dve.If(flagged(dve)):
                with dve.Fori(0, NG) as i:
                    with dve.Fori(0, NG) as j:
                        dve.wait_ge(targets[layer], i * 32 + 16)
                        dve.wait_ge(sums_mm[layer], i * SETS + j * G + 1)
                        dve.tensor_copy(KC[:], KCF[:, bass.ds(j * G, G + 1)]).then_inc(sums_key[layer], 1)
                        dve.wait_ge(sums_key[layer], i * (NG + 1) + j + 1)
                        for v in range(G):
                            dve.wait_ge(sums_mm[layer], i * SETS + j * G + v + 1)
                            dve.tensor_scalar(HD[:, 0, :], KR[0][:], KC[:, v:v + 1], None,
                                              ALU.is_equal).then_inc(sums_equal[layer], 1)
                    dve.wait_ge(sums_mm[layer], (i + 1) * SETS)
                    dve.wait_ge(sums_equal[layer], (i + 1) * NT)
                    dve.tensor_copy(KC[:, 0:G], LEAD[:, bass.ds(i * G, G)]).then_inc(sums_key[layer], 1)
                    dve.wait_ge(sums_key[layer], (i + 1) * (NG + 1))
                    for u in range(G):
                        ins = dve.tensor_scalar(V[0][:, u, :], PS[1][:, u * P:(u + 1) * P], KC[:, u:u + 1], None, ALU.mult)
                    ins.then_inc(sums_done[layer], 1)
                dve.wait_ge(sums_done[layer], NG)

        def setup_vector(dve):
            done = [0]

            def then(ins):
                done[0] += 1
                ins.then_inc(prep, 1)
                dve.wait_ge(prep, done[0])

            dve.wait_ge(tables_in, 16 * len(TABLES))
            dve.wait_ge(filled, 1)
            dve.tensor_copy(KCF[:], DSTI[:])
            then(dve.tensor_copy(PKF[:], PRVI[:]))
            key = KCF[:, 0:NT]
            tmp = flat(W[0])[:, 0:NT]
            tmp2 = flat(W[1])[:, 0:NT]
            dve.tensor_scalar(DGI[:], key, float(N - 1), None, ALU.min)
            dve.tensor_tensor(LEAD[:], PKF[:], key, ALU.not_equal)
            dve.tensor_tensor(tmp, PKF[:], key, ALU.is_gt)
            then(dve.tensor_tensor(tmp2, KCF[:, 1:NT + 1], key, ALU.is_le))
            then(dve.tensor_tensor(tmp, tmp, tmp2, ALU.add))
            then(dve.reduce_sum(BAD[:, 0:1], tmp, AX_X))
            dve.wait_ge(consts_in, 16 * len(CONSTS))
            for c in range(HC):
                dve.tensor_scalar(RB[:, c, :], ONES[:], B1[:, c:c + 1], 0.0, ALU.mult, ALU.max)
            then(dve.tensor_copy(BH[:, 0], BR[:]))
            then(dve.tensor_tensor(BS[:, 0], BR[:], BH[:, 0], ALU.subtract))
            then(dve.tensor_copy(BH[:, 1], BS[:, 0]))
            then(dve.tensor_tensor(BS[:, 1], BS[:, 0], BH[:, 1], ALU.subtract))
            then(dve.tensor_copy(BH[:, 2], BS[:, 1]))
            then(dve.tensor_scalar(BS[:, 0], BH[:, 0], ID[0:3, 0:1], None, ALU.mult))
            then(dve.scalar_tensor_tensor(out=BS[:, 1], in0=BH[:, 1], scalar=ID[0:3, 1:2], in1=BS[:, 0],
                                          op0=ALU.mult, op1=ALU.add))
            then(dve.scalar_tensor_tensor(out=BS[:, 2], in0=BH[:, 2], scalar=ID[0:3, 2:3], in1=BS[:, 1],
                                          op0=ALU.mult, op1=ALU.add))
            then(dve.tensor_copy(B3[:], BS[:, 2].unsqueeze(2).broadcast_to([3, 3, 4, D])))
            assert done[0] == SETUP_STEPS
            dve.wait_ge(prep_pe, 1)
            dve.tensor_copy(CR[:], PS[2][:, 0:D])
            dve.tensor_copy(BADI[:], PS[1][0:1, 0:1]).then_inc(flag_ready, 1)
            dve.wait_ge(flag_ready, 1)
            leaders_vector(dve)
            tmp3 = flat(W[2])[:, 0:NT]
            then(dve.tensor_scalar(tmp3, LEAD[:], -float(FAR), float(FAR), ALU.mult, ALU.add))
            dve.tensor_tensor(LIX[:], tmp3, KCF[:, 0:NT], ALU.add).then_inc(ready, 1)

        SETUP_STEPS = 13

        block = ctx.enter_context(nc.Block())
        CONSTS = [(W1[:], w1), (W2[:], w2.rearrange("(c p) d -> p c d", p=P)),
                  (B1[:], b1),
                  (GM[:], gamma.partition_broadcast(P)), (BT[:], beta.partition_broadcast(P)),
                  (MW[:], mw1.rearrange("(c p) d -> p c d", p=P)), (UW[:], uw1.rearrange("(c p) d -> p c d", p=P)),
                  (U2[:], uw2), (UB[:], ub1.rearrange("(p a) -> p a", a=1)), (ID[:], ident),
                  (BR[:, 0, :], b2.partition_broadcast(3)), (BR[:, 1, :], mb1.partition_broadcast(3)),
                  (BR[:, 2, :], ub2.partition_broadcast(3))]
        TABLES = [(DSTI[:], dst_t), (PRVI[:], prev_t), (SRCI[:], src_t), (ENO[:], edge_no)]

        @block.sync
        def _(sp):
            for t, a in TABLES:
                sp.dma_start(t, a).then_inc(tables_in, 16)
            for t, a in CONSTS:
                sp.dma_start(t, a).then_inc(consts_in, 16)
            sp.wait_ge(filled, 1)
            sp.dma_start(slot_d.rearrange("(p n) a -> p (n a)", p=80), FARI[:]).then_inc(slots_cleared, 16)
            sp.dma_start(v_d[NE:NE + P, :], Z[0][:, 0, :]).then_inc(slots_cleared, 16)
            sp.dma_start(m_d[NE:NE + P, :], Z[0][:, 0, :]).then_inc(slots_cleared, 16)

            def step(t):
                s = t.s
                if is_kind(s + 3, DENSE):
                    if s >= 1:
                        sp.wait_ge(h_done, t.at(lambda q: q + 1, 1))
                        sp.wait_ge(x_beta, t.at(lambda q: q + 1, 1))
                    sp.dma_start(X[(s + 3) % 4][:], node_rows(x, t.at(dense_row, -3))).then_inc(x_loaded[(s + 3) % 4], 16)
                if is_kind(s + 3, SRC):
                    n = number(s + 3)
                    if n >= 2:
                        sp.wait_ge(v_done, t.at(lambda q: number(q) - 1, -3))
                    sp.dma_start(E[n % 2][:], edge_rows(e, t.at(lambda q: number(q) * GR, -3))).then_inc(e_loaded[n % 2], 16)
                if is_kind(s + 3, DST):
                    n = number(s + 3)
                    if n >= 2:
                        sp.wait_ge(seg_done, t.at(lambda q: number(q) - 1, -3))
                    row = t.at(lambda q: number(q) * GR, -3)
                    sp.dma_start(VG[n % 2][:], edge_rows(v_d, row, G + 1)).then_inc(window_loaded[n % 2], 16)
                    sp.dma_start(KR[n % 2][:], keys[bass.ds(row, GR)].partition_broadcast(P)).then_inc(window_loaded[n % 2], 16)
                if is_kind(s - 2, SRC):
                    n = number(s - 2)
                    sp.wait_ge(v_done, t.at(lambda q: number(q) + 1, 2))
                    sp.dma_start(edge_rows(v_d, t.at(lambda q: number(q) * GR, 2)), V[n % 2][:]).then_inc(v_stored[n % 2], 16)
                if is_kind(s - 5, SRC, DST):
                    sp.wait_ge(h1_done, t.at(lambda q: q + 1, 5))
                    to = hs_d if kinds[s - 5] == SRC else hd_d
                    sp.dma_start(edge_rows(to, t.at(lambda q: number(q) * GR, 5)), H1[(s - 5) % 2][:]).then_inc(h1_stored[(s - 5) % 2], 16)
                if is_kind(s - 6, DST):
                    sp.wait_ge(zh_done, t.at(lambda q: count(q, DST, DENSE), 6))
                    sp.dma_start(edge_rows(zd_d, t.at(lambda q: number(q) * GR, 6)), ZH[(s - 6) % 2][:]).then_inc(zh_stored[(s - 6) % 2], 16)
                if is_kind(s - 8, DENSE):
                    n = number(s - 8)
                    sp.wait_ge(y_done, t.at(lambda q: number(q) + 1, 8))
                    if n == 1:
                        sp.wait_ge(y_stored[0], 16)
                    sp.dma_start(node_rows(out, t.at(dense_row, 8)), Y[n % 2][:]).then_inc(y_stored[n % 2], 16)

            def meet():
                for n in range(2):
                    sp.wait_ge(v_stored[n], 16 * (NG // 2))
                sp.wait_ge(slots_cleared, 48)
                sums_sync(sp, 0)

            run(sp, step, -3, TICKS + 1, loops, {0: lambda: leaders_sync(sp), MEET: meet})
            for n in range(2):
                sp.wait_ge(y_stored[n], 16 * (ND // 2))
            sp.wait_ge(h1_stored[0], stores(NQ, SRC, DST))
            sp.wait_ge(zh_stored[0], stores(NQ, DST))
            messages_sync(sp)
            sp.wait_ge(seg_done, NG)
            sp.wait_ge(eq_done, NG)
            sums_sync(sp, 1)
            update_sync(sp)

        @block.gpsimd
        def _(pool):
            for t in (0, 1):
                pool.memset(ST[t][:], 1.0)
            pool.memset(FARI[:], FAR)
            pool.memset(Z[0][:, 0, :], 0.0)
            pool.memset(ONE3[:], 1.0)
            pool.memset(ZERO[:], 0.0)
            pool.memset(ONES[:], 1.0).then_inc(filled, 1)
            pool.wait_ge(ready, 1)
            last_node = pool.to_reg(N - 1)
            last_edge = pool.to_reg(NE - 1)

            def step(t):
                s = t.s
                if exists(s - 1):
                    wait_x(pool, t, x_loaded, x_gathered, 1)
                    if s >= 5:
                        pool.wait_ge(z_done, t.at(lambda q: q - 3, 1))
                    pool.tensor_tensor(XB[(s - 1) % 4][:], X[(s - 1) % 4][:], each(BT), ALU.add).then_inc(x_beta, 1)
                if is_kind(s + 3, SRC, DST):
                    n = count(s + 3, SRC, DST) - 1
                    index = SRCI if kinds[s + 3] == SRC else DGI
                    pool.tensor_copy(IX[n % 2][:], index[:, bass.ds(t.at(lambda q: number(q) * G, -3), G)]).then_inc(index_done, 1)
                    if s >= 1:
                        pool.wait_ge(h_done, t.at(lambda q: q + 1, 1))
                        pool.wait_ge(x_beta, t.at(lambda q: q + 1, 1))
                    pool.wait_ge(index_done, t.at(lambda q: count(q, SRC, DST), -3))
                    take_waits(pool)
                    for u in range(G):
                        pool.indirect_dma_start(
                            out=X[(s + 3) % 4][:, u, :], out_offset=None, in_=x,
                            in_offset=bass.IndirectOffsetOnAxis(ap=IX[n % 2][:, u:u + 1], axis=0),
                            bounds_check=last_node, oob_is_err=False).then_inc(x_gathered[n % 2], 16)
                if is_kind(s - 5, DST, DENSE):
                    q = s - 5
                    pool.wait_ge(h1_done, t.at(lambda q: q + 1, 5))
                    if is_kind(q - 2, DENSE):
                        pool.wait_ge(y_done, t.at(lambda q: number(q) + 1, 7))
                    if is_kind(q - 2, DST):
                        pool.wait_ge(zh_stored[q % 2], t.at(lambda q: stores(q, DST), 7))
                    pool.tensor_tensor(ZH[q % 2][:], Z[q % 4][:], H1[q % 2][:], ALU.add).then_inc(zh_done, 1)
                if is_kind(s, SRC):
                    n = number(s)
                    if s == 0:
                        pool.wait_ge(slots_cleared, 48)
                    if n >= 2:
                        pool.wait_ge(slots_set[n % 2], t.at(lambda q: ring(q, 16 * G) - 16 * G))
                    pool.tensor_copy(MX[n % 2][:], LIX[:, bass.ds(t.at(lambda q: number(q) * G), G)]).then_inc(map_index_done, 1)
                    pool.tensor_copy(MV[n % 2][:], ENO[:, bass.ds(t.at(lambda q: number(q) * G), G)]).then_inc(map_index_done, 1)
                    pool.wait_ge(map_index_done, t.at(lambda q: 2 * count(q, SRC)))
                    take_waits(pool)
                    for u in range(G):
                        pool.indirect_dma_start(
                            out=slot_d, out_offset=bass.IndirectOffsetOnAxis(ap=MX[n % 2][:, u:u + 1], axis=0),
                            in_=MV[n % 2][:, u:u + 1], in_offset=None,
                            bounds_check=last_node, oob_is_err=False).then_inc(slots_set[n % 2], 16)
                if is_kind(s, DST):
                    n = number(s)
                    if n == 0:
                        for k in range(2):
                            pool.wait_ge(slots_set[k], 16 * G * (NG // 2))
                    pool.tensor_copy(MX[n % 2][:], SRCI[:, bass.ds(t.at(lambda q: number(q) * G), G)]).then_inc(map_index_done, 1)
                    if n >= 2:
                        pool.wait_ge(slot_kept, t.at(lambda q: number(q) - 1))
                    pool.wait_ge(map_index_done, t.at(lambda q: 2 * NG + count(q, DST)))
                    take_waits(pool)
                    for u in range(G):
                        pool.indirect_dma_start(
                            out=MV[n % 2][:, u:u + 1], out_offset=None, in_=slot_d,
                            in_offset=bass.IndirectOffsetOnAxis(ap=MX[n % 2][:, u:u + 1], axis=0),
                            bounds_check=last_node, oob_is_err=False).then_inc(slots_got[n % 2], 16)
                if is_kind(s - 1, DST):
                    n = number(s - 1)
                    pool.wait_ge(slots_got[n % 2], t.at(lambda q: ring(q, 16 * G), 1))
                    pool.tensor_copy(SLOT[:, bass.ds(t.at(lambda q: number(q) * G, 1), G)], MV[n % 2][:]).then_inc(slot_kept, 1)

            run(pool, step, -3, TICKS, loops)
            messages_pool(pool, last_edge)
            update_pool(pool, last_node)

        @block.scalar
        def _(act):
            act.wait_ge(ready, 1)

            def step(t):
                s = t.s
                if 0 <= s < NQ + 4:
                    act.wait_ge(chain_done, t.at(lambda q: CHAIN * (q + 1)))
                    rs, nb = RS[s % 2], NB[s % 2]
                if exists(s):
                    if s >= 4:
                        act.wait_ge(z_done, t.at(lambda q: q - 3))
                    for u in range(G):
                        ins = act.activation(W[s % 4][:, u, :], X[s % 4][:, u, :], ACT.Relu,
                                             bias=nb[:, 0, u:u + 1], scale=rs[:, 0, u:u + 1])
                    ins.then_inc(h_done, 1)
                if is_kind(s - 5, DENSE):
                    n = number(s - 5)
                    act.wait_ge(t_done, t.at(lambda q: number(q) + 1, 5))
                    if n >= 2:
                        act.wait_ge(u_done, t.at(lambda q: number(q) - 1, 5))
                    act.copy(flat(HT[n % 2]), PS[0][:, 0:GR]).then_inc(ht_done, 1)
                if is_kind(s + 1, DST):
                    act.wait_ge(seg_done, t.at(lambda q: number(q) + 1, -1))
                    if number(s + 1) >= 1:
                        act.wait_ge(hid_mm, t.at(lambda q: number(q) * HC, -1))
                    act.copy(UT[:], PS[1][:, 0:GR]).then_inc(ut_done, 1)
                if exists(s - 2):
                    act.wait_ge(g_done, t.at(lambda q: q + 1, 2))
                    for u in range(G):
                        ins = act.activation(W[(s - 2) % 4][:, u, :], W[(s - 2) % 4][:, u, :], ACT.Identity,
                                             bias=nb[:, 1, u:u + 1], scale=rs[:, 1, u:u + 1])
                    ins.then_inc(n_done, 1)

                def hidden(c):
                    act.wait_ge(hid_mm, t.at(lambda q: number(q) * HC + c + 1, -1))
                    if c == 0 and number(s + 1) >= 1:
                        act.wait_ge(m_done, t.at(lambda q: number(q), -1))
                    act.activation(HD[:, c, :], PS[c % 2 ^ 1][:, 0:GR], ACT.Relu,
                                   bias=B1[:, c:c + 1], scale=1.0).then_inc(hid_act, 1)

                if is_kind(s + 1, DST):
                    hidden(0)
                    hidden(1)
                if is_kind(s - 5, DENSE):
                    n = number(s - 5)
                    act.wait_ge(u_done, t.at(lambda q: number(q) + 1, 5))
                    if n >= 2:
                        act.wait_ge(y_mm, t.at(lambda q: number(q) - 1, 5))
                    act.activation(flat(S1[n % 2]), PS[2][:, 0:GR], ACT.Silu, bias=UB[:, 0:1], scale=1.0).then_inc(silu_done, 1)
                if is_kind(s + 1, DST):
                    hidden(2)
                    hidden(3)
                if exists(s - 4):
                    q = s - 4
                    act.wait_ge(z_done, t.at(lambda q: q + 1, 4))
                    if is_kind(q - 2, DST, DENSE):
                        act.wait_ge(zh_done, t.at(lambda q: count(q, DST, DENSE), 6))
                    if is_kind(q - 2, DENSE):
                        act.wait_ge(t_done, t.at(lambda q: number(q) + 1, 6))
                    if is_kind(q - 2, SRC, DST):
                        act.wait_ge(h1_stored[q % 2], t.at(lambda q: stores(q, SRC, DST), 6))
                    for u in range(G):
                        ins = act.activation(H1[q % 2][:, u, :], Z[q % 4][:, u, :], ACT.Relu,
                                             bias=nb[:, 2, u:u + 1], scale=rs[:, 2, u:u + 1])
                    ins.then_inc(h1_done, 1)

            run(act, step, -1, TICKS, loops)
            messages_act(act)
            update_act(act)

        @block.tensor
        def _(pe):
            pe.wait_ge(prep, SETUP_STEPS)
            pe.matmul(PS[1][:, 0:1], ONES[:], BAD[:, 0:1], start=True, stop=True)
            pe.matmul(PS[2][:, 0:D], ONE3[:], B3[:, 0, 0, :], start=True, stop=False)
            for c in range(HC):
                ins = pe.matmul(PS[2][:, 0:D], RB[:, c, :], W2[:, c, :], start=False, stop=(c == HC - 1))
            ins.then_inc(prep_pe, 1)
            pe.wait_ge(ready, 1)

            def step(t):
                s = t.s
                dst, dense = is_kind(s + 1, DST), is_kind(s - 5, DENSE)
                if dense:
                    pe.wait_ge(h1_done, t.at(lambda q: q + 1, 5))
                    if number(s - 5) >= 1:
                        pe.wait_ge(ht_done, t.at(lambda q: number(q), 5))
                    if count(s, DST):
                        pe.wait_ge(hid_act, t.at(lambda q: HC * count(q, DST)))
                    for u in range(G):
                        ins = pe.transpose(PS[0][:, u * P:(u + 1) * P], H1[(s - 5) % 2][:, u, :], ID[:])
                    ins.then_inc(t_done, 1)
                if dst:
                    n = number(s + 1)
                    pe.wait_ge(window_loaded[n % 2], t.at(lambda q: ring(q, 32), -1))
                    pe.wait_ge(eq_done, t.at(lambda q: number(q) + 1, -1))
                    if n >= 1:
                        pe.wait_ge(hid_act, t.at(lambda q: number(q) * HC, -1))
                    ins = neighbour_sums(pe, PS[1], VG[n % 2])
                    ins.then_inc(seg_done, 1)
                if dense:
                    if number(s - 5) >= 1:
                        pe.wait_ge(silu_done, t.at(lambda q: number(q), 5))
                    pe.wait_ge(ht_done, t.at(lambda q: number(q) + 1, 5))
                    for lo, hi in HALVES:
                        ins = pe.matmul(PS[2][:, lo:hi], UW[:, 0, :], flat(HT[number(s - 5) % 2])[:, lo:hi], start=True, stop=True)
                    ins.then_inc(u_done, 1)

                def hidden(c):
                    if c == 0:
                        pe.wait_ge(ut_done, t.at(lambda q: number(q) + 1, -1))
                    if c == 1 and count(s - 5, DENSE):
                        pe.wait_ge(ht_done, t.at(lambda q: count(q, DENSE), 5))
                    if c == 1 and number(s + 1) >= 1:
                        pe.wait_ge(hid_act, t.at(lambda q: number(q) * HC, -1))
                    if c >= 2:
                        pe.wait_ge(hid_act, t.at(lambda q: number(q) * HC + c - 1, -1))
                    for lo, hi in HALVES:
                        ins = pe.matmul(PS[c % 2 ^ 1][:, lo:hi], W1[:, c * P:(c + 1) * P], UT[:, lo:hi], start=True, stop=True)
                    ins.then_inc(hid_mm, 1)

                def aggregate(c):
                    if c == 0:
                        if count(s - 5, DENSE):
                            pe.wait_ge(y_done, t.at(lambda q: count(q, DENSE), 5))
                        if through_dst(s):
                            pe.wait_ge(g_done, t.at(through_dst))
                        bias(pe, PS[3], 0)
                    pe.wait_ge(hid_act, t.at(lambda q: number(q) * HC + c + 1, -1))
                    for u in range(G):
                        ins = pe.matmul(PS[3][:, u * P:(u + 1) * P], HD[:, c, u * P:(u + 1) * P], W2[:, c, :],
                                        start=False, stop=(c == HC - 1), skip_group_check=True)
                    if c == HC - 1:
                        ins.then_inc(m_done, 1)

                if dst:
                    hidden(0)
                    hidden(1)
                if dense:
                    n = number(s - 5)
                    if n >= 1:
                        pe.wait_ge(y_done, t.at(lambda q: number(q), 5))
                    if through_dst(s):
                        pe.wait_ge(g_done, t.at(through_dst))
                    bias(pe, PS[3], 2)
                    pe.wait_ge(silu_done, t.at(lambda q: number(q) + 1, 5))
                    for u in range(G):
                        ins = pe.matmul(PS[3][:, u * P:(u + 1) * P], S1[n % 2][:, u, :], U2[:],
                                        start=False, stop=True, skip_group_check=True)
                    ins.then_inc(y_mm, 1)
                if dst:
                    aggregate(0)
                    hidden(2)
                    aggregate(1)
                    hidden(3)
                    aggregate(2)
                    aggregate(3)

            run(pe, step, -1, TICKS, loops, {MEET: lambda: sums_pe(pe, 0)})
            messages_pe(pe)
            for sem_, n in ((me_done, NG), (msg_done, NG)):
                pe.wait_ge(sem_, n)
            sums_pe(pe, 1)
            update_pe(pe)

        @block.vector
        def _(dve):
            setup_vector(dve)

            def chain(t, k):
                s = t.s
                if not 0 <= s - 1 < NQ + 4:
                    return
                st, rs, nb = ST[(s - 1) % 2], RS[(s - 1) % 2], NB[(s - 1) % 2]
                total, diff, m2, sq, var, r, a, b = (CS[:, i] for i in range(8))
                need = {0: 0, 1: 0, 2: 0, 3: 2, 4: 4, 5: 5}.get(k, k)
                if need:
                    dve.wait_ge(chain_done, t.at(lambda q: CHAIN * q + need, 1))
                if k == 0:
                    if s >= 2:
                        dve.wait_ge(chain_done, t.at(lambda q: CHAIN * q, 1))
                    dve.wait_ge(st_done, t.at(lambda q: q + 1, 1))
                    if s >= 3:
                        last = 7 if exists(s - 7) else 5 if exists(s - 5) else 3
                        dve.wait_ge({7: h1_done, 5: n_done, 3: h_done}[last], t.at(lambda q: q + 1, last))
                if k == 0:
                    ins = dve.tensor_tensor(total, st[:, :, :, 1], st[:, :, :, 4], ALU.add)
                elif k == 1:
                    ins = dve.tensor_tensor(diff, st[:, :, :, 1], st[:, :, :, 4], ALU.subtract)
                elif k == 2:
                    ins = dve.scalar_tensor_tensor(out=m2, in0=st[:, :, :, 2], scalar=EPS * D, in1=st[:, :, :, 5],
                                                   op0=ALU.add, op1=ALU.add)
                elif k == 3:
                    ins = dve.scalar_tensor_tensor(out=sq, in0=diff, scalar=0.25, in1=diff, op0=ALU.mult, op1=ALU.mult)
                elif k == 4:
                    ins = dve.scalar_tensor_tensor(out=var, in0=m2, scalar=1.0 / D, in1=sq, op0=ALU.mult, op1=ALU.add)
                elif k == 5:
                    ins = dve.tensor_scalar(r.bitcast(I32), var.bitcast(I32), -0.5, MAGIC, ALU.mult, ALU.add)
                elif k < 15:
                    if k % 3 == 0:
                        ins = dve.tensor_tensor(a, r, r, ALU.mult)
                    elif k % 3 == 1:
                        ins = dve.scalar_tensor_tensor(out=b, in0=var, scalar=-0.5, in1=a, op0=ALU.mult, op1=ALU.mult)
                    else:
                        ins = dve.scalar_tensor_tensor(out=rs[:] if k == 14 else r, in0=b, scalar=1.5, in1=r,
                                                       op0=ALU.add, op1=ALU.mult)
                else:
                    ins = dve.scalar_tensor_tensor(out=nb[:], in0=total, scalar=-0.5, in1=rs[:], op0=ALU.mult, op1=ALU.mult)
                ins.then_inc(chain_done, 1)

            def step(t):
                s = t.s
                stats = None
                chain(t, 0)
                chain(t, 1)
                chain(t, 2)
                if exists(s):
                    wait_x(dve, t, x_loaded, x_gathered)
                for u in range(G):
                    if exists(s):
                        stats = dve.bn_stats(ST[s % 2][:, 0, u, :], X[s % 4][:, u, :])
                    chain(t, 3 + u)
                if is_kind(s + 1, DST):
                    n = number(s + 1)
                    dve.tensor_copy(KC[:], KCF[:, bass.ds(t.at(lambda q: number(q) * G, -1), G + 1)]).then_inc(kc_done, 1)
                    dve.wait_ge(window_loaded[n % 2], t.at(lambda q: ring(q, 32), -1))
                    if n >= 1:
                        dve.wait_ge(seg_done, t.at(lambda q: number(q), -1))
                    dve.wait_ge(kc_done, t.at(lambda q: number(q) + 1, -1))
                    ins = equal_tiles(dve, KR[n % 2])
                    ins.then_inc(eq_done, 1)
                if exists(s - 2):
                    w = W[(s - 2) % 4]
                    dve.wait_ge(h_done, t.at(lambda q: q + 1, 2))
                    if is_kind(s - 2, SRC):
                        n = number(s - 2)
                        dve.wait_ge(e_loaded[n % 2], t.at(ring, 2))
                        if n >= 2:
                            dve.wait_ge(v_stored[n % 2], t.at(lambda q: ring(q) - 16, 2))
                        dve.tensor_tensor(V[n % 2][:], w[:], E[n % 2][:], ALU.add).then_inc(v_done, 1)
                    if is_kind(s - 2, DST):
                        dve.wait_ge(m_done, t.at(lambda q: number(q) + 1, 2))
                        dve.tensor_tensor(flat(w), flat(w), PS[3][:, 0:GR], ALU.add).then_inc(g_done, 1)
                    else:
                        dve.tensor_tensor(w[:], w[:], each(CR), ALU.add).then_inc(g_done, 1)
                chain(t, 10)
                if exists(s - 4):
                    dve.wait_ge(n_done, t.at(lambda q: q + 1, 4))
                    dve.tensor_tensor(W[s % 4][:], W[s % 4][:], each(GM), ALU.mult).then_inc(mul_done, 1)
                chain(t, 11)
                if exists(s - 2):
                    dve.wait_ge(g_done, t.at(lambda q: q + 1, 2))
                for u in range(G):
                    if exists(s - 2):
                        stats = dve.bn_stats(ST[s % 2][:, 1, u, :], W[(s - 2) % 4][:, u, :])
                    if u < 4:
                        chain(t, 12 + u)
                    if u == 4 and exists(s - 4):
                        dve.wait_ge(mul_done, t.at(lambda q: q + 1, 4))
                        dve.wait_ge(x_beta, t.at(lambda q: q + 1, 4))
                        if s >= 8:
                            dve.wait_ge(h1_done, t.at(lambda q: q + 1, 8))
                            if is_kind(s - 8, DST, DENSE):
                                dve.wait_ge(zh_done, t.at(lambda q: count(q, DST, DENSE), 8))
                        dve.tensor_tensor(Z[s % 4][:], W[s % 4][:], XB[s % 4][:], ALU.add).then_inc(z_done, 1)
                if exists(s - 4):
                    dve.wait_ge(z_done, t.at(lambda q: q + 1, 4))
                    for u in range(G):
                        stats = dve.bn_stats(ST[s % 2][:, 2, u, :], Z[s % 4][:, u, :])
                if stats is not None:
                    stats.then_inc(st_done, 1)
                if is_kind(s - 7, DENSE):
                    n = number(s - 7)
                    dve.wait_ge(y_mm, t.at(lambda q: number(q) + 1, 7))
                    dve.wait_ge(zh_done, t.at(lambda q: count(q, DST, DENSE), 7))
                    if n >= 2:
                        dve.wait_ge(y_stored[n % 2], t.at(lambda q: ring(q) - 16, 7))
                    dve.tensor_tensor(flat(Y[n % 2]), PS[3][:, 0:GR], flat(ZH[(s - 7) % 2]), ALU.add).then_inc(y_done, 1)

            run(dve, step, -1, TICKS, loops, {MEET + 1: lambda: sums_vector(dve, 0)})
            messages_vector(dve)
            dve.wait_ge(m_done, NG)
            sums_vector(dve, 1)
            update_vector(dve)


def kernel(x, src, dst, edge_attr_128, L0_gnn_W1, L0_gnn_b1, L0_gnn_W2, L0_gnn_b2, L0_gnn_gamma, L0_gnn_beta,
           L1_gnn_mw1, L1_gnn_mb1, L1_gnn_uw1, L1_gnn_ub1, L1_gnn_uw2, L1_gnn_ub2):
    import numpy as np
    import concourse.bacc as bacc
    from concourse.bass_utils import run_bass_kernel_spmd

    n, d = x.shape
    edges = src.shape[0]
    tiles_ = -(-edges // GR) * G
    padded = tiles_ * P
    src_p = np.zeros(padded, np.int32)
    src_p[:edges] = np.asarray(src)
    keys = np.arange(n - edges, n - edges + padded + P, dtype=np.int32)
    keys[:edges] = np.asarray(dst)
    prev = np.concatenate([np.full(1, -1, np.int32), keys[:padded - 1]])
    e_p = np.zeros((padded, d), np.float32)
    e_p[:edges] = np.asarray(edge_attr_128)

    def by_tile(a):
        return np.ascontiguousarray(a.reshape(-1, P).T)

    arrays = {
        "x": x, "e": e_p, "src_t": by_tile(src_p), "dst_t": by_tile(keys), "prev_t": by_tile(prev), "keys": keys,
        "after": np.arange(padded, 0, -1, dtype=np.float32), "ident": np.eye(P, dtype=np.float32), "edge_no": by_tile(np.arange(padded, dtype=np.int32)),
        "w1": L0_gnn_W1, "b1": np.asarray(L0_gnn_b1).reshape(-1, P).T, "w2": L0_gnn_W2, "b2": L0_gnn_b2, "gamma": L0_gnn_gamma, "beta": L0_gnn_beta,
        "mw1": L1_gnn_mw1, "mb1": L1_gnn_mb1, "uw1": L1_gnn_uw1, "ub1": L1_gnn_ub1, "uw2": L1_gnn_uw2, "ub2": L1_gnn_ub2,
    }
    arrays = {f"in_{k}": np.ascontiguousarray(a) for k, a in arrays.items()}
    nc = bacc.Bacc("TRN2", target_bir_lowering=False, num_devices=1)
    aps = [nc.dram_tensor(k, a.shape, mybir.dt.from_np(a.dtype), kind="ExternalInput").ap() for k, a in arrays.items()]
    out = nc.dram_tensor("out", (n, d), F32, kind="ExternalOutput").ap()
    gnn_program(nc, *aps, out)
    r = run_bass_kernel_spmd(nc, [arrays], core_ids=[0])
    return r.results[0]["out"]
```

```python
from contextlib import ExitStack

import concourse.bass as bass
from concourse import mybir

F32 = mybir.dt.float32
I32 = mybir.dt.int32
BF16 = mybir.dt.bfloat16
ALU = mybir.AluOpType
ACT = mybir.ActivationFunctionType
AX_X = mybir.AxisListType.X

P = 128
G = 7
GR = G * P
BODY = 4
EPS = 1e-5
FAR = 1 << 17
MAGIC = 1597463007.0
CHAIN = 16

SRC, DST, DENSE = "src", "dst", "dense"


def plan(n_edge_groups, n_dense_groups):
    first = [SRC, DENSE] * n_edge_groups
    gap = [DENSE] * 4
    second = [DST, DENSE] * n_edge_groups
    rest = [DENSE] * (n_dense_groups - 2 * n_edge_groups - 4)
    kinds = first + gap + second + rest
    lag, ahead = 8, 3
    loops = []
    start = 0
    for part in (first, gap, second, rest):
        lo, hi = start + lag + (BODY if start == 0 else 0), start + len(part) - ahead
        if part is rest:
            lo, hi = max(lo, start + 4 + 4), min(hi, start + 4 + n_edge_groups)
        if hi - lo >= 2 * BODY:
            lo += (start - lo) % BODY
            loops.append((lo, lo + (hi - lo) // BODY * BODY))
        start += len(part)
    return kinds, loops, len(first), len(first + gap + second) + 4


class Tick:

    def __init__(self, s, body=None, bodies=1):
        self.s, self.body, self.bodies = s, body, bodies

    def at(self, f, back=0):
        q = self.s - back
        if self.body is None:
            return f(q)
        step = f(q + BODY) - f(q)
        assert f(q + (self.bodies - 1) * BODY) == f(q) + (self.bodies - 1) * step
        return f(q) + (self.body * step if step else 0)


def gnn_program(nc, x, e, src_t, dst_t, prev_t, keys, after, ident, edge_no, w1, b1, w2, b2, gamma, beta,
                mw1, mb1, uw1, ub1, uw2, ub2, out):
    N, D = x.shape
    NT = src_t.shape[1]
    NE = NT * P
    NG = NT // G
    HID = w1.shape[1]
    HC = HID // P
    ND = -(-N // GR)
    assert D == P and NT % G == 0 and NG % 2 == 0

    kinds, loops, src_span, MSG0 = plan(NG, ND)
    NQ = len(kinds)
    MEET = src_span + 1
    TICKS = NQ + 8
    LAST_DST = max(q for q in range(NQ) if kinds[q] == DST)

    def is_kind(q, *which):
        return 0 <= q < NQ and kinds[q] in which

    def exists(q):
        return 0 <= q < NQ

    def count(q, *which):
        return sum(k in which for k in kinds[:max(q + 1, 0)])

    def number(q):
        return count(q, kinds[q]) - 1

    def x_loads(q):
        return sum(16 for i in range(q % 4, q + 1, 4) if kinds[i] == DENSE)

    def x_gathers(q):
        return 16 * G * ((count(q, SRC, DST) - 1) // 2 + 1)

    def wait_x(eng, t, x_loaded, x_gathered, back=0):
        q = t.s - back
        if kinds[q] == DENSE:
            eng.wait_ge(x_loaded[q % 4], t.at(x_loads, back))
        else:
            eng.wait_ge(x_gathered[(count(q, SRC, DST) - 1) % 2], t.at(x_gathers, back))

    def ring(q, each=16):
        return (number(q) // 2 + 1) * each

    def stores(q, *which):
        return sum(16 for i in range(q % 2, min(q + 1, NQ), 2) if kinds[i] in which)

    def mul_on_pool(q):
        return kinds[q] == DENSE and q >= src_span

    def pool_muls(q):
        return sum(mul_on_pool(i) for i in range(q + 1))

    def dense_row(q):
        n = number(q)
        return 0 if n == 0 else N - GR * (ND - n)

    def run(eng, step, first, ticks, loops, meets={}):
        s = first
        for lo, hi in [*loops, (ticks, ticks)]:
            for s in range(s, lo):
                if s in meets:
                    meets[s]()
                step(Tick(s))
            if hi > lo:
                with eng.Fori(0, (hi - lo) // BODY) as body:
                    for u in range(BODY):
                        step(Tick(lo + u, body, (hi - lo) // BODY))
            s = hi

    ctx = ExitStack()
    with ctx:
        def sb(name, shape, dt=F32):
            return ctx.enter_context(nc.sbuf_tensor(name, shape, dt))

        def sem(name):
            return ctx.enter_context(nc.semaphore(name))

        def sems(name, n):
            return [sem(f"{name}_{i}") for i in range(n)]

        def tiles(name, n):
            return [sb(f"{name}_{i}", [P, G, D]) for i in range(n)]

        v_d = nc.dram_tensor("v_scratch", (NE + P, D), F32).ap()
        q_d = nc.dram_tensor("edge_part_scratch", (NE, D), F32).ap()
        m_d = nc.dram_tensor("msg_scratch", (NE + P, D), F32).ap()
        fix_d = nc.dram_tensor("sum_scratch", (NE, D), F32).ap()
        hs_d = nc.dram_tensor("h1_src_scratch", (NE, D), F32).ap()
        hd_d = nc.dram_tensor("h1_dst_scratch", (NE, D), F32).ap()
        zd_d = nc.dram_tensor("x1_h1_dst_scratch", (NE, D), F32).ap()
        slot_d = nc.dram_tensor("slot_of_node_scratch", (N, 1), I32).ap()

        X = tiles("x_in", 4)
        XB = tiles("x_beta", 4)
        W = tiles("work", 4)
        Z = tiles("x1", 4)
        H1 = tiles("h1", 2)
        ZH = tiles("x1_h1", 2)
        Y = tiles("y", 2)
        HT = tiles("h1T", 2)
        S1 = tiles("silu", 2)
        E = tiles("e_in", 2)
        V = tiles("v", 2)
        VG = [sb(f"v_window_{i}", [P, G + 1, D]) for i in range(2)]
        KR = [sb(f"key_row_{i}", [P, GR], I32) for i in range(2)]
        EQ = sb("equal", [P, G + 1, 2 * P])
        KC = sb("key_col_group", [P, G + 1])
        UT = sb("uT", [P, GR])
        HD = sb("hidden", [P, HC, GR])
        IX = [sb(f"gather_index_{i}", [P, G], I32) for i in range(2)]
        MX = [sb(f"map_index_{i}", [P, G], I32) for i in range(2)]
        MV = [sb(f"map_value_{i}", [P, G], I32) for i in range(2)]
        ST = [sb(f"stats_{i}", [P, 3, G, 6]) for i in range(2)]
        RS = [sb(f"rstd_{i}", [P, 3, G]) for i in range(2)]
        NB = [sb(f"minus_mean_rstd_{i}", [P, 3, G]) for i in range(2)]
        CS = sb("chain", [P, 8, 3, G])

        W1 = sb("W1", [P, HID])
        W2 = sb("W2", [P, HC, D])
        B1 = sb("B1", [P, HC])
        RB = sb("relu_b1", [P, HC, P])
        CR = sb("c_row", [P, D])
        GM = sb("gamma_row", [P, D])
        BT = sb("beta_row", [P, D])
        MW = sb("MW1", [P, 2, D])
        UW = sb("UW1", [P, 2, D])
        U2 = sb("UW2", [P, D])
        UB = sb("UB1", [P, 1])
        ID = sb("ident", [P, P])
        BR = sb("bias_rows", [3, 3, D])
        BS = sb("bias_rest", [3, 3, 3, D])
        BH = sb("bias_high", [3, 3, 3, D], BF16)
        B3 = sb("bias_parts", [3, 3, 4, D], BF16)
        ONE3 = sb("ones3", [3, P], BF16)
        ONES = sb("ones", [P, P])
        SRCI = sb("src_index", [P, NT], I32)
        DSTI = sb("dst_key", [P, NT + 1], I32)
        PRVI = sb("prev_key", [P, NT], I32)
        ENO = sb("edge_number", [P, NT], I32)
        KCF = sb("key_col", [P, NT + 1])
        PKF = sb("prev_key_f", [P, NT])
        ENF = sb("edge_number_f", [P, NT])
        LEAD = sb("leader", [P, NT])
        DGI = sb("dst_gather_index", [P, NT], I32)
        LIX = sb("leader_index", [P, NT], I32)
        SLOT = sb("slot_of_src", [P, NT], I32)
        BAD = sb("bad", [P, 4])
        FST = sb("first_of_key", [P, NT])
        FM = sb("first_in_chunk", [P, 1])
        AFT = sb("edges_to_the_end", [P, NT])
        ZERO = sb("zeros", [3, 512], BF16)
        SINK = sb("sink", [1, 1])
        BADI = sb("bad_i", [1, 1], I32)
        FARI = sb("far", [80, N // 80], I32)

        PS = [ctx.enter_context(nc.psum_tensor(f"ps{i}", [P, 1024], F32)) for i in range(4)]
        HALVES = ((0, 512), (512, GR))
        MH = [VG[0][:, 0:G, :], VG[1][:, 0:G, :], *(sb(f"msg_h_{i}", [P, G, D])[:] for i in range(2))]
        MQ = [E[0], E[1], ZH[0], ZH[1]]

        def message(t, back=0):
            return t.at(lambda q: q - MSG0, back), t.s - back - MSG0, 0 <= t.s - back - MSG0 < NG

        def as_tiles(rows):
            return rows.rearrange("p (t d) -> p t d", d=D)

        def flat(t):
            return t[:].rearrange("p t d -> p (t d)")

        def each(row):
            return row[:].unsqueeze(1).broadcast_to([P, G, D])

        def edge_rows(d, row, n=G):
            return d[bass.ds(row, n * P), :].rearrange("(t p) d -> p t d", p=P)

        def node_rows(d, row):
            return d[bass.ds(row, GR), :].rearrange("(p t) d -> p t d", t=G)

        consts_in = sem("consts_in")
        tables_in = sem("tables_in")
        filled = sem("filled")
        prep = sem("prep")
        prep_pe = sem("prep_pe")
        slots_cleared = sem("slots_cleared")
        ready = sem("ready")
        flag_ready = sem("order_flag_ready")
        first_in = sem("first_keys_loaded")
        first_key = sem("first_key_col_done")
        first_done = sem("first_of_key_steps")
        first_ends = sem("first_of_key_ends")
        targets = sems("sums_keys_loaded_and_sums_stored", 2)
        source_in = sems("sums_source_loaded", 2)
        sums_mm = sems("sums_mm", 2)
        sums_equal = sems("sums_equal_done", 2)
        sums_key = sems("sums_key_col_done", 2)
        sums_done = sems("sums_done", 2)
        sums_moved = sems("sums_moved", 2)
        x_loaded = sems("x_loaded", 4)
        x_gathered = sems("x_gathered", 2)
        x_beta = sem("x_beta_done")
        h_done = sem("h_done")
        g_done = sem("g_done")
        n_done = sem("n_done")
        mul_done = sem("mul_done")
        dve_mul_done = sem("dve_mul_done")
        z_done = sem("z_done")
        st_done = sem("st_done")
        chain_done = sem("chain_done")
        h1_done = sem("h1_done")
        zh_done = sem("zh_done")
        e_loaded = sems("e_loaded", 2)
        v_done = sem("v_done")
        v_stored = sems("v_stored", 2)
        window_loaded = sems("window_loaded", 2)
        kc_done = sem("kc_done")
        eq_done = sem("eq_done")
        seg_done = sem("seg_done")
        ut_done = sem("ut_done")
        hid_mm = sem("hid_mm")
        hid_act = sem("hid_act")
        agg_mm = sem("agg_mm")
        t_done = sem("t_done")
        ht_done = sem("ht_done")
        u_done = sem("u_done")
        silu_done = sem("silu_done")
        y_mm = sem("y_mm")
        y_done = sem("y_done")
        y_stored = sems("y_stored", 2)
        h1_stored = sems("h1_stored", 2)
        zh_stored = sems("zh_stored", 2)
        index_done = sem("index_done")
        map_index_done = sem("map_index_done")
        slots_set = sems("slots_set", 2)
        slots_got = sems("slots_got", 2)
        slot_kept = sem("slot_kept")

        et_done = sem("eT_transposed")
        et_out = sem("eT_done")
        qe_mm = sem("edge_part_mm")
        qe_done = sem("edge_part_done")
        qe_stored = sems("edge_part_stored", 2)
        hs_in = sems("msg_h_loaded", 4)
        qm_in = sems("msg_edge_part_loaded", 4)
        over = sems("msg_h_replaced", 4)
        mi_done = sem("msg_index_done")
        mt_done = sem("msg_transposed")
        mh_done = sem("msg_hT_done")
        mm_done = sem("msg_mm")
        msg_done = sem("msg_done")
        msg_stored = sems("msg_stored", 2)
        up_in = sems("upd_window_loaded", 2)
        uh_in = sems("upd_h1_loaded", 2)
        uz_in = sems("upd_x1_h1_loaded", 4)
        uk_done = sem("upd_key_col_done")
        uq_done = sem("upd_equal_done")
        us_done = sem("upd_sums")
        ut2_done = sem("upd_transposed")
        ua_done = sem("upd_aT_done")
        uh_done = sem("upd_hT_done")
        um_done = sem("upd_u_mm")
        usilu_done = sem("upd_silu_done")
        uy_mm = sem("upd_y_mm")
        uy_done = sem("upd_y_done")
        ui_done = sem("upd_index_done")
        scattered = sems("upd_scattered", 2)

        def equal_tiles(dve, row):
            for j in range(G + 1):
                lo, hi = max(j - 1, 0) * P, min(j + 1, G) * P
                at = P if j == 0 else 0
                ins = dve.tensor_scalar(EQ[:, j, at:at + hi - lo], row[:, lo:hi], KC[:, j:j + 1], None, ALU.is_equal)
            return ins

        def neighbour_sums(pe, ps, rows):
            for u in range(G):
                own = u * P, (u + 1) * P
                pe.matmul(ps[:, own[0]:own[1]], rows[:, u, :], EQ[:, u, P:2 * P],
                          start=(u * P % 512 == 0), stop=False, skip_group_check=True)
                ins = pe.matmul(ps[:, own[0]:own[1]], rows[:, u + 1, :], EQ[:, u + 1, 0:P],
                                start=False, stop=True, skip_group_check=True)
            return ins

        def bias(pe, ps, which):
            for lo, hi in HALVES:
                pe.matmul(ps[:, lo:hi], ONE3[:], B3[:, which].rearrange("k t d -> k (t d)")[:, 0:hi - lo],
                          start=True, stop=False, skip_group_check=True)

        def take_waits(pool):
            pool.tensor_tensor(SINK[:], ONES[0:1, 0:1], ONES[0:1, 0:1], ALU.mult)

        EDGE_TICKS = NG + 3
        edge_loops = [(4, 4 + (NG - 4) // BODY * BODY)]

        def group(t, back=0):
            return t.at(lambda q: q, back), 0 <= t.s - back < NG

        def update_sync(sp):
            sp.wait_ge(seg_done, NG)
            sp.wait_ge(eq_done, NG)
            sp.wait_ge(h1_done, NQ)

            def step(t):
                s = t.s
                i, there = group(t)
                if there:
                    k = s % 2
                    if s >= 2:
                        sp.wait_ge(us_done, i - 1)
                        sp.wait_ge(ut2_done, i - 1)
                    sp.dma_start(VG[k][:], edge_rows(m_d, i * GR, G + 1)).then_inc(up_in[k], 16)
                    sp.dma_start(KR[k][:], keys[bass.ds(i * GR, GR)].partition_broadcast(P)).then_inc(up_in[k], 16)
                    sp.dma_start(X[2 + k][:], edge_rows(hd_d, i * GR)).then_inc(uh_in[k], 16)
                    if s >= 4:
                        sp.wait_ge(uy_done, i - 3)
                    sp.dma_start(Z[s % 4][:], edge_rows(zd_d, i * GR)).then_inc(uz_in[s % 4], 16)

            run(sp, step, 0, EDGE_TICKS, edge_loops)

        def update_vector(dve):
            dve.wait_ge(u_done, ND)
            for k in range(2):
                dve.wait_ge(y_stored[k], 16 * (ND // 2))

            def step(t):
                s = t.s
                i, there = group(t)
                if there:
                    k = s % 2
                    if s >= 1:
                        dve.wait_ge(uq_done, i)
                    dve.tensor_copy(KC[:], KCF[:, bass.ds(i * G, G + 1)]).then_inc(uk_done, 1)
                    dve.wait_ge(up_in[k], t.at(lambda q: 32 * (q // 2 + 1)))
                    if s >= 1:
                        dve.wait_ge(us_done, i)
                    dve.wait_ge(uk_done, i + 1)
                    equal_tiles(dve, KR[k]).then_inc(uq_done, 1)
                    dve.wait_ge(ut2_done, i + 1)
                    if s >= 2:
                        dve.wait_ge(um_done, i - 1)
                    dve.tensor_copy(flat(HT[k]), PS[1][:, 0:GR]).then_inc(uh_done, 1)
                i, there = group(t, 2)
                if there:
                    k = s % 2
                    dve.wait_ge(uy_mm, i + 1)
                    dve.wait_ge(uz_in[(s - 2) % 4], t.at(lambda q: 16 * (q // 4 + 1), 2))
                    if s >= 4:
                        dve.wait_ge(scattered[k], t.at(lambda q: 16 * G * (q // 2), 2))
                    dve.tensor_tensor(flat(Y[k]), PS[3][:, 0:GR], flat(Z[(s - 2) % 4]), ALU.add).then_inc(uy_done, 1)

            run(dve, step, 0, EDGE_TICKS, edge_loops)

        def update_act(act):
            act.wait_ge(u_done, ND)
            act.wait_ge(y_mm, ND)
            act.wait_ge(z_done, NQ)

            def step(t):
                s = t.s
                i, there = group(t)
                if there:
                    k = s % 2
                    act.wait_ge(us_done, i + 1)
                    if s >= 2:
                        act.wait_ge(um_done, i - 1)
                    act.copy(flat(W[k]), PS[0][:, 0:GR]).then_inc(ua_done, 1)
                i, there = group(t, 1)
                if there:
                    k = (s - 1) % 2
                    act.wait_ge(um_done, i + 1)
                    if s >= 3:
                        act.wait_ge(uy_mm, i - 1)
                    act.activation(flat(S1[k]), PS[2][:, 0:GR], ACT.Silu, bias=UB[:, 0:1], scale=1.0).then_inc(usilu_done, 1)

            run(act, step, 0, EDGE_TICKS, edge_loops)

        def update_pe(pe):
            def step(t):
                s = t.s
                i, there = group(t)
                if there:
                    k = s % 2
                    pe.wait_ge(up_in[k], t.at(lambda q: 32 * (q // 2 + 1)))
                    pe.wait_ge(uq_done, i + 1)
                    if s >= 1:
                        pe.wait_ge(ua_done, i)
                    neighbour_sums(pe, PS[0], VG[k]).then_inc(us_done, 1)
                    pe.wait_ge(uh_in[k], t.at(lambda q: 16 * (q // 2 + 1)))
                    if s >= 1:
                        pe.wait_ge(uh_done, i)
                    for u in range(G):
                        ins = pe.transpose(PS[1][:, u * P:(u + 1) * P], X[2 + k][:, u, :], ID[:])
                    ins.then_inc(ut2_done, 1)
                i, there = group(t, 2)
                if there:
                    k = s % 2
                    if s >= 3:
                        pe.wait_ge(uy_done, i)
                    bias(pe, PS[3], 2)
                    pe.wait_ge(usilu_done, i + 1)
                    for u in range(G):
                        ins = pe.matmul(PS[3][:, u * P:(u + 1) * P], S1[k][:, u, :], U2[:],
                                        start=False, stop=True, skip_group_check=True)
                    ins.then_inc(uy_mm, 1)
                i, there = group(t, 1)
                if there:
                    k = (s - 1) % 2
                    if s >= 2:
                        pe.wait_ge(usilu_done, i)
                    pe.wait_ge(uh_done, i + 1)
                    pe.wait_ge(ua_done, i + 1)
                    for lo, hi in HALVES:
                        pe.matmul(PS[2][:, lo:hi], UW[:, 0, :], flat(HT[k])[:, lo:hi], start=True, stop=False)
                        ins = pe.matmul(PS[2][:, lo:hi], UW[:, 1, :], flat(W[k])[:, lo:hi], start=False, stop=True)
                    ins.then_inc(um_done, 1)

            run(pe, step, 0, EDGE_TICKS, edge_loops)

        def update_pool(pool, last_node):
            for k in range(4):
                pool.wait_ge(over[k], 16 * G * ((NG - k + 3) // 4))
            for k in range(2):
                pool.wait_ge(y_stored[k], 16 * (ND // 2))

            def step(t):
                s = t.s
                i, there = group(t, 2)
                if there:
                    k = s % 2
                    if s >= 4:
                        pool.wait_ge(scattered[k], t.at(lambda q: 16 * G * (q // 2), 2))
                    pool.tensor_copy(IX[k][:], LIX[:, bass.ds(i * G, G)]).then_inc(ui_done, 1)
                    pool.wait_ge(ui_done, i + 1)
                    pool.wait_ge(uy_done, i + 1)
                    take_waits(pool)
                    for u in range(G):
                        pool.indirect_dma_start(
                            out=out, out_offset=bass.IndirectOffsetOnAxis(ap=IX[k][:, u:u + 1], axis=0),
                            in_=Y[k][:, u, :], in_offset=None,
                            bounds_check=last_node, oob_is_err=False).then_inc(scattered[k], 16)

            run(pool, step, 0, EDGE_TICKS, edge_loops)
            for k in range(2):
                pool.wait_ge(scattered[k], 16 * G * (NG // 2))


        def flagged(eng):
            return eng.value_load(BADI[0:1, 0:1])

        SETS = 1 + NT

        def leaders_sync(sp):
            sp.wait_ge(flag_ready, 1)
            with sp.If(flagged(sp)):
                with sp.Fori(0, NG) as c:
                    sp.wait_ge(first_done, c * (3 * NT) + 1)
                    sp.dma_start(KR[0][:], keys[bass.ds(c * GR, GR)].partition_broadcast(P)).then_inc(first_in, 16)
                    sp.dma_start(UT[:], after[bass.ds(c * GR, GR)].partition_broadcast(P)).then_inc(first_in, 16)

        def leaders_vector(dve):
            product = flat(EQ)[:, 0:GR]
            with dve.If(flagged(dve)):
                dve.memset(FST[:], 0.0).then_inc(first_done, 1)
                dve.wait_ge(first_done, 1)
                with dve.Fori(0, NG) as c:
                    with dve.Fori(0, NT) as i:
                        n = c * (3 * NT) + i * 3 + 1
                        dve.wait_ge(first_in, (c + 1) * 32)
                        dve.tensor_copy(KC[:, 0:1], KCF[:, bass.ds(i, 1)]).then_inc(first_key, 1)
                        dve.wait_ge(first_key, c * NT + i + 1)
                        dve.scalar_tensor_tensor(out=product, in0=KR[0][:], scalar=KC[:, 0:1], in1=UT[:],
                                                 op0=ALU.is_equal, op1=ALU.mult).then_inc(first_done, 1)
                        dve.wait_ge(first_done, n + 1)
                        dve.tensor_reduce(out=FM[:], in_=product, axis=AX_X, op=ALU.max).then_inc(first_done, 1)
                        dve.wait_ge(first_done, n + 2)
                        dve.tensor_tensor(FST[:, bass.ds(i, 1)], FST[:, bass.ds(i, 1)], FM[:], ALU.max).then_inc(first_done, 1)
                        dve.wait_ge(first_done, n + 3)
                dve.tensor_scalar(AFT[:], ENO[:], -1.0, float(NE), ALU.mult, ALU.add).then_inc(first_ends, 1)
                dve.wait_ge(first_ends, 1)
                dve.tensor_tensor(LEAD[:], AFT[:], FST[:], ALU.is_equal).then_inc(first_ends, 1)
                dve.wait_ge(first_ends, 2)

        def sums_sync(sp, layer):
            rows = (v_d, m_d)[layer]
            with sp.If(flagged(sp)):
                with sp.Fori(0, NG) as i:
                    sp.dma_start(KR[0][:], keys[bass.ds(i * GR, GR)].partition_broadcast(P)).then_inc(targets[layer], 16)
                    with sp.Fori(0, NG) as j:
                        sp.wait_ge(targets[layer], i * 32 + 16)
                        sp.wait_ge(sums_mm[layer], i * SETS + j * G + 1)
                        sp.dma_start(VG[0][:, 0:G, :], edge_rows(rows, j * GR)).then_inc(source_in[layer], 16)
                    sp.wait_ge(sums_done[layer], i + 1)
                    sp.dma_start(edge_rows(fix_d, i * GR), V[0][:]).then_inc(targets[layer], 16)
                sp.wait_ge(targets[layer], NG * 32)
                sp.dma_start(rows[0:NE, :], fix_d).then_inc(sums_moved[layer], 16)
                sp.wait_ge(sums_moved[layer], 16)

        def sums_pe(pe, layer):
            with pe.If(flagged(pe)):
                if layer == 0:
                    pe.wait_ge(et_out, NG)
                with pe.Fori(0, NG) as i:
                    pe.wait_ge(targets[layer], i * 32 + 16)
                    for lo, hi in HALVES:
                        ins = pe.matmul(PS[1][:, lo:hi], ONE3[:], ZERO[:, 0:hi - lo], start=True, stop=False,
                                        skip_group_check=True)
                    ins.then_inc(sums_mm[layer], 1)
                    with pe.Fori(0, NG) as j:
                        pe.wait_ge(source_in[layer], (i * NG + j + 1) * 16)
                        for v in range(G):
                            pe.wait_ge(sums_equal[layer], i * NT + j * G + v + 1)
                            for u in range(G):
                                ins = pe.matmul(PS[1][:, u * P:(u + 1) * P], HD[:, 0, u * P:(u + 1) * P], VG[0][:, v, :],
                                                start=False, stop=True, skip_group_check=True)
                            ins.then_inc(sums_mm[layer], 1)
                    pe.wait_ge(sums_done[layer], i + 1)

        def sums_vector(dve, layer):
            with dve.If(flagged(dve)):
                if layer == 0:
                    dve.wait_ge(qe_mm, NG)
                with dve.Fori(0, NG) as i:
                    with dve.Fori(0, NG) as j:
                        dve.wait_ge(targets[layer], i * 32 + 16)
                        dve.wait_ge(sums_mm[layer], i * SETS + j * G + 1)
                        dve.tensor_copy(KC[:], KCF[:, bass.ds(j * G, G + 1)]).then_inc(sums_key[layer], 1)
                        dve.wait_ge(sums_key[layer], i * (NG + 1) + j + 1)
                        for v in range(G):
                            dve.wait_ge(sums_mm[layer], i * SETS + j * G + v + 1)
                            dve.tensor_scalar(HD[:, 0, :], KR[0][:], KC[:, v:v + 1], None,
                                              ALU.is_equal).then_inc(sums_equal[layer], 1)
                    dve.wait_ge(sums_mm[layer], (i + 1) * SETS)
                    dve.wait_ge(sums_equal[layer], (i + 1) * NT)
                    dve.tensor_copy(KC[:, 0:G], LEAD[:, bass.ds(i * G, G)]).then_inc(sums_key[layer], 1)
                    dve.wait_ge(sums_key[layer], (i + 1) * (NG + 1))
                    for u in range(G):
                        ins = dve.tensor_scalar(V[0][:, u, :], PS[1][:, u * P:(u + 1) * P], KC[:, u:u + 1], None, ALU.mult)
                    ins.then_inc(sums_done[layer], 1)
                dve.wait_ge(sums_done[layer], NG)

        def setup_vector(dve):
            done = [0]

            def then(ins):
                done[0] += 1
                ins.then_inc(prep, 1)
                dve.wait_ge(prep, done[0])

            dve.wait_ge(tables_in, 16 * len(TABLES))
            dve.wait_ge(filled, 1)
            dve.tensor_copy(KCF[:], DSTI[:])
            then(dve.tensor_copy(PKF[:], PRVI[:]))
            key = KCF[:, 0:NT]
            tmp = flat(W[0])[:, 0:NT]
            tmp2 = flat(W[1])[:, 0:NT]
            dve.tensor_scalar(DGI[:], key, float(N - 1), None, ALU.min)
            dve.tensor_tensor(LEAD[:], PKF[:], key, ALU.not_equal)
            dve.tensor_tensor(tmp, PKF[:], key, ALU.is_gt)
            then(dve.tensor_tensor(tmp2, KCF[:, 1:NT + 1], key, ALU.is_le))
            then(dve.tensor_tensor(tmp, tmp, tmp2, ALU.add))
            then(dve.reduce_sum(BAD[:, 0:1], tmp, AX_X))
            dve.wait_ge(consts_in, 16 * len(CONSTS))
            for c in range(HC):
                dve.tensor_scalar(RB[:, c, :], ONES[:], B1[:, c:c + 1], 0.0, ALU.mult, ALU.max)
            then(dve.tensor_copy(BH[:, 0], BR[:]))
            then(dve.tensor_tensor(BS[:, 0], BR[:], BH[:, 0], ALU.subtract))
            then(dve.tensor_copy(BH[:, 1], BS[:, 0]))
            then(dve.tensor_tensor(BS[:, 1], BS[:, 0], BH[:, 1], ALU.subtract))
            then(dve.tensor_copy(BH[:, 2], BS[:, 1]))
            then(dve.tensor_scalar(BS[:, 0], BH[:, 0], ID[0:3, 0:1], None, ALU.mult))
            then(dve.scalar_tensor_tensor(out=BS[:, 1], in0=BH[:, 1], scalar=ID[0:3, 1:2], in1=BS[:, 0],
                                          op0=ALU.mult, op1=ALU.add))
            then(dve.scalar_tensor_tensor(out=BS[:, 2], in0=BH[:, 2], scalar=ID[0:3, 2:3], in1=BS[:, 1],
                                          op0=ALU.mult, op1=ALU.add))
            then(dve.tensor_copy(B3[:], BS[:, 2].unsqueeze(2).broadcast_to([3, 3, 4, D])))
            assert done[0] == SETUP_STEPS
            dve.wait_ge(prep_pe, 1)
            dve.tensor_copy(CR[:], PS[2][:, 0:D])
            dve.tensor_copy(BADI[:], PS[1][0:1, 0:1]).then_inc(flag_ready, 1)
            dve.wait_ge(flag_ready, 1)
            leaders_vector(dve)
            tmp3 = flat(W[2])[:, 0:NT]
            then(dve.tensor_scalar(tmp3, LEAD[:], -float(FAR), float(FAR), ALU.mult, ALU.add))
            dve.tensor_tensor(LIX[:], tmp3, KCF[:, 0:NT], ALU.add).then_inc(ready, 1)

        SETUP_STEPS = 13

        block = ctx.enter_context(nc.Block())
        CONSTS = [(W1[:], w1), (W2[:], w2.rearrange("(c p) d -> p c d", p=P)),
                  (B1[:], b1),
                  (GM[:], gamma.partition_broadcast(P)), (BT[:], beta.partition_broadcast(P)),
                  (MW[:], mw1.rearrange("(c p) d -> p c d", p=P)), (UW[:], uw1.rearrange("(c p) d -> p c d", p=P)),
                  (U2[:], uw2), (UB[:], ub1.rearrange("(p a) -> p a", a=1)), (ID[:], ident),
                  (BR[:, 0, :], b2.partition_broadcast(3)), (BR[:, 1, :], mb1.partition_broadcast(3)),
                  (BR[:, 2, :], ub2.partition_broadcast(3))]
        TABLES = [(DSTI[:], dst_t), (PRVI[:], prev_t), (SRCI[:], src_t), (ENO[:], edge_no)]

        @block.sync
        def _(sp):
            for t, a in TABLES:
                sp.dma_start(t, a).then_inc(tables_in, 16)
            for t, a in CONSTS:
                sp.dma_start(t, a).then_inc(consts_in, 16)
            sp.wait_ge(filled, 1)
            sp.dma_start(slot_d.rearrange("(p n) a -> p (n a)", p=80), FARI[:]).then_inc(slots_cleared, 16)
            sp.dma_start(v_d[NE:NE + P, :], Z[0][:, 0, :]).then_inc(slots_cleared, 16)
            sp.dma_start(m_d[NE:NE + P, :], Z[0][:, 0, :]).then_inc(slots_cleared, 16)

            def step(t):
                s = t.s
                if is_kind(s + 3, DENSE):
                    if s >= 1:
                        sp.wait_ge(h_done, t.at(lambda q: q + 1, 1))
                        sp.wait_ge(x_beta, t.at(lambda q: q + 1, 1))
                    sp.dma_start(X[(s + 3) % 4][:], node_rows(x, t.at(dense_row, -3))).then_inc(x_loaded[(s + 3) % 4], 16)
                if is_kind(s + 3, SRC):
                    n = number(s + 3)
                    if n >= 2:
                        sp.wait_ge(v_done, t.at(lambda q: number(q) - 1, -3))
                        sp.wait_ge(et_done, t.at(lambda q: number(q) - 1, -3))
                    sp.dma_start(E[n % 2][:], edge_rows(e, t.at(lambda q: number(q) * GR, -3))).then_inc(e_loaded[n % 2], 16)
                if is_kind(s + 3, DST):
                    n = number(s + 3)
                    if n >= 2:
                        sp.wait_ge(seg_done, t.at(lambda q: number(q) - 1, -3))
                    row = t.at(lambda q: number(q) * GR, -3)
                    sp.dma_start(VG[n % 2][:], edge_rows(v_d, row, G + 1)).then_inc(window_loaded[n % 2], 16)
                    sp.dma_start(KR[n % 2][:], keys[bass.ds(row, GR)].partition_broadcast(P)).then_inc(window_loaded[n % 2], 16)
                if is_kind(s - 2, SRC):
                    n = number(s - 2)
                    sp.wait_ge(v_done, t.at(lambda q: number(q) + 1, 2))
                    sp.dma_start(edge_rows(v_d, t.at(lambda q: number(q) * GR, 2)), V[n % 2][:]).then_inc(v_stored[n % 2], 16)
                if is_kind(s - 3, SRC):
                    n = number(s - 3)
                    sp.wait_ge(qe_done, t.at(lambda q: number(q) + 1, 3))
                    sp.dma_start(edge_rows(q_d, t.at(lambda q: number(q) * GR, 3)),
                                 as_tiles(HD[:, 2 + n % 2, :])).then_inc(qe_stored[n % 2], 16)
                if is_kind(s - 5, SRC, DST):
                    sp.wait_ge(h1_done, t.at(lambda q: q + 1, 5))
                    to = hs_d if kinds[s - 5] == SRC else hd_d
                    sp.dma_start(edge_rows(to, t.at(lambda q: number(q) * GR, 5)), H1[(s - 5) % 2][:]).then_inc(h1_stored[(s - 5) % 2], 16)
                if is_kind(s - 6, DST):
                    n = number(s - 6)
                    sp.wait_ge(zh_done, t.at(lambda q: number(q) + 1, 6))
                    sp.dma_start(edge_rows(zd_d, t.at(lambda q: number(q) * GR, 6)), ZH[n % 2][:]).then_inc(zh_stored[n % 2], 16)
                if is_kind(s - 8, DENSE):
                    n = number(s - 8)
                    sp.wait_ge(y_done, t.at(lambda q: number(q) + 1, 8))
                    if n == 1:
                        sp.wait_ge(y_stored[0], 16)
                    sp.dma_start(node_rows(out, t.at(dense_row, 8)), Y[n % 2][:]).then_inc(y_stored[n % 2], 16)
                i, n, there = message(t)
                if there:
                    if n == 0:
                        sp.wait_ge(h1_stored[0], stores(NQ, SRC))
                        for k in range(2):
                            sp.wait_ge(qe_stored[k], 16 * (NG // 2))
                            sp.wait_ge(zh_stored[k], 16 * (NG // 2))
                        sp.wait_ge(v_done, NG)
                        sp.wait_ge(et_done, NG)
                        sp.wait_ge(seg_done, NG)
                    if n >= 4:
                        sp.wait_ge(mm_done, i - 3)
                    sp.dma_start(MH[n % 4], edge_rows(hs_d, i * GR)).then_inc(hs_in[n % 4], 16)
                    sp.dma_start(MQ[n % 4][:], edge_rows(q_d, i * GR)).then_inc(qm_in[n % 4], 16)
                i, n, there = message(t, 4)
                if there:
                    sp.wait_ge(msg_done, i + 1)
                    sp.dma_start(edge_rows(m_d, i * GR), V[n % 2][:]).then_inc(msg_stored[n % 2], 16)

            def meet():
                for n in range(2):
                    sp.wait_ge(v_stored[n], 16 * (NG // 2))
                sp.wait_ge(slots_cleared, 48)
                sums_sync(sp, 0)

            run(sp, step, -3, TICKS + 1, loops, {0: lambda: leaders_sync(sp), MEET: meet})
            for n in range(2):
                sp.wait_ge(y_stored[n], 16 * (ND // 2))
            for n in range(2):
                sp.wait_ge(msg_stored[n], 16 * (NG // 2))
            sp.wait_ge(mt_done, NG)
            sp.wait_ge(eq_done, NG)
            sp.wait_ge(h_done, NQ)
            sp.wait_ge(x_beta, NQ)
            sp.wait_ge(h1_done, NQ)
            sums_sync(sp, 1)
            update_sync(sp)

        @block.gpsimd
        def _(pool):
            for t in (0, 1):
                pool.memset(ST[t][:], 1.0)
            pool.memset(FARI[:], FAR)
            pool.memset(Z[0][:, 0, :], 0.0)
            pool.memset(ONE3[:], 1.0)
            pool.memset(ZERO[:], 0.0)
            pool.memset(ONES[:], 1.0).then_inc(filled, 1)
            pool.wait_ge(ready, 1)
            last_node = pool.to_reg(N - 1)
            last_edge = pool.to_reg(NE - 1)

            def step(t):
                s = t.s
                if exists(s - 1):
                    wait_x(pool, t, x_loaded, x_gathered, 1)
                    if s >= 5:
                        pool.wait_ge(z_done, t.at(lambda q: q - 3, 1))
                    pool.tensor_tensor(XB[(s - 1) % 4][:], X[(s - 1) % 4][:], each(BT), ALU.add).then_inc(x_beta, 1)
                if exists(s - 3) and mul_on_pool(s - 3):
                    pool.wait_ge(n_done, t.at(lambda q: q + 1, 3))
                    pool.tensor_tensor(W[(s - 3) % 4][:], W[(s - 3) % 4][:], each(GM), ALU.mult).then_inc(mul_done, 1)
                if is_kind(s + 3, SRC, DST):
                    n = count(s + 3, SRC, DST) - 1
                    index = SRCI if kinds[s + 3] == SRC else DGI
                    pool.tensor_copy(IX[n % 2][:], index[:, bass.ds(t.at(lambda q: number(q) * G, -3), G)]).then_inc(index_done, 1)
                    if s >= 1:
                        pool.wait_ge(h_done, t.at(lambda q: q + 1, 1))
                        pool.wait_ge(x_beta, t.at(lambda q: q + 1, 1))
                    pool.wait_ge(index_done, t.at(lambda q: count(q, SRC, DST), -3))
                    take_waits(pool)
                    for u in range(G):
                        pool.indirect_dma_start(
                            out=X[(s + 3) % 4][:, u, :], out_offset=None, in_=x,
                            in_offset=bass.IndirectOffsetOnAxis(ap=IX[n % 2][:, u:u + 1], axis=0),
                            bounds_check=last_node, oob_is_err=False).then_inc(x_gathered[n % 2], 16)
                if is_kind(s - 5, DST):
                    n = number(s - 5)
                    pool.wait_ge(h1_done, t.at(lambda q: q + 1, 5))
                    if n >= 2:
                        pool.wait_ge(zh_stored[n % 2], t.at(lambda q: ring(q) - 16, 5))
                    pool.tensor_tensor(ZH[n % 2][:], Z[(s - 5) % 4][:], H1[(s - 5) % 2][:], ALU.add).then_inc(zh_done, 1)
                if is_kind(s, SRC):
                    n = number(s)
                    if s == 0:
                        pool.wait_ge(slots_cleared, 48)
                    if n >= 2:
                        pool.wait_ge(slots_set[n % 2], t.at(lambda q: ring(q, 16 * G) - 16 * G))
                    pool.tensor_copy(MX[n % 2][:], LIX[:, bass.ds(t.at(lambda q: number(q) * G), G)]).then_inc(map_index_done, 1)
                    pool.tensor_copy(MV[n % 2][:], ENO[:, bass.ds(t.at(lambda q: number(q) * G), G)]).then_inc(map_index_done, 1)
                    pool.wait_ge(map_index_done, t.at(lambda q: 2 * count(q, SRC)))
                    take_waits(pool)
                    for u in range(G):
                        pool.indirect_dma_start(
                            out=slot_d, out_offset=bass.IndirectOffsetOnAxis(ap=MX[n % 2][:, u:u + 1], axis=0),
                            in_=MV[n % 2][:, u:u + 1], in_offset=None,
                            bounds_check=last_node, oob_is_err=False).then_inc(slots_set[n % 2], 16)
                if is_kind(s, DST):
                    n = number(s)
                    if n == 0:
                        for k in range(2):
                            pool.wait_ge(slots_set[k], 16 * G * (NG // 2))
                    pool.tensor_copy(MX[n % 2][:], SRCI[:, bass.ds(t.at(lambda q: number(q) * G), G)]).then_inc(map_index_done, 1)
                    if n >= 2:
                        pool.wait_ge(slot_kept, t.at(lambda q: number(q) - 1))
                    pool.wait_ge(map_index_done, t.at(lambda q: 2 * NG + count(q, DST)))
                    take_waits(pool)
                    for u in range(G):
                        pool.indirect_dma_start(
                            out=MV[n % 2][:, u:u + 1], out_offset=None, in_=slot_d,
                            in_offset=bass.IndirectOffsetOnAxis(ap=MX[n % 2][:, u:u + 1], axis=0),
                            bounds_check=last_node, oob_is_err=False).then_inc(slots_got[n % 2], 16)
                i, n, there = message(t, 1)
                if there:
                    if n == 0:
                        pool.wait_ge(h1_stored[0], stores(NQ, SRC, DST))
                        pool.wait_ge(slot_kept, NG)
                        for k in range(2):
                            pool.wait_ge(x_gathered[k], 16 * G * NG)
                    if n >= 2:
                        pool.wait_ge(over[(n - 2) % 4], t.at(lambda q: 16 * G * ((q - MSG0 - 2) // 4 + 1), 1))
                    pool.tensor_copy(IX[n % 2][:], SLOT[:, bass.ds(i * G, G)]).then_inc(mi_done, 1)
                    pool.wait_ge(mi_done, i + 1)
                    pool.wait_ge(hs_in[n % 4], t.at(lambda q: 16 * ((q - MSG0) // 4 + 1), 1))
                    take_waits(pool)
                    for u in range(G):
                        pool.indirect_dma_start(
                            out=MH[n % 4][:, u, :], out_offset=None, in_=hd_d,
                            in_offset=bass.IndirectOffsetOnAxis(ap=IX[n % 2][:, u:u + 1], axis=0),
                            bounds_check=last_edge, oob_is_err=False).then_inc(over[n % 4], 16)
                if is_kind(s - 1, DST):
                    n = number(s - 1)
                    pool.wait_ge(slots_got[n % 2], t.at(lambda q: ring(q, 16 * G), 1))
                    pool.tensor_copy(SLOT[:, bass.ds(t.at(lambda q: number(q) * G, 1), G)], MV[n % 2][:]).then_inc(slot_kept, 1)

            run(pool, step, -3, TICKS, loops)
            update_pool(pool, last_node)

        @block.scalar
        def _(act):
            act.wait_ge(ready, 1)

            def step(t):
                s = t.s
                if 0 <= s < NQ + 4:
                    act.wait_ge(chain_done, t.at(lambda q: CHAIN * (q + 1)))
                    rs, nb = RS[s % 2], NB[s % 2]
                if exists(s):
                    if s >= 4:
                        act.wait_ge(z_done, t.at(lambda q: q - 3))
                    for u in range(G):
                        ins = act.activation(W[s % 4][:, u, :], X[s % 4][:, u, :], ACT.Relu,
                                             bias=nb[:, 0, u:u + 1], scale=rs[:, 0, u:u + 1])
                    ins.then_inc(h_done, 1)
                if exists(s - 2):
                    act.wait_ge(g_done, t.at(lambda q: q + 1, 2))
                    for u in range(G):
                        ins = act.activation(W[(s - 2) % 4][:, u, :], W[(s - 2) % 4][:, u, :], ACT.Identity,
                                             bias=nb[:, 1, u:u + 1], scale=rs[:, 1, u:u + 1])
                    ins.then_inc(n_done, 1)

                if is_kind(s, SRC):
                    n = number(s)
                    act.wait_ge(et_done, t.at(lambda q: number(q) + 1))
                    if n >= 2:
                        act.wait_ge(qe_mm, t.at(lambda q: number(q) - 1))
                    act.copy(HD[:, n % 2, :], PS[1][:, 0:GR]).then_inc(et_out, 1)
                if is_kind(s - 1, SRC):
                    n = number(s - 1)
                    act.wait_ge(qe_mm, t.at(lambda q: number(q) + 1, 1))
                    if n >= 2:
                        act.wait_ge(qe_stored[n % 2], t.at(lambda q: ring(q) - 16, 1))
                    act.copy(HD[:, 2 + n % 2, :], PS[3][:, 0:GR]).then_inc(qe_done, 1)
                i, n, there = message(t, 2)
                if there:
                    act.wait_ge(mt_done, i + 1)
                    if n < 2:
                        act.wait_ge(agg_mm, HC * NG)
                    else:
                        act.wait_ge(mm_done, i - 1)
                    act.copy(HD[:, n % 2, :], PS[1][:, 0:GR]).then_inc(mh_done, 1)

                def hidden(c, back):
                    if number(s - back) == 0:
                        act.wait_ge(qe_mm, NG)
                        for k in range(2):
                            act.wait_ge(qe_stored[k], 16 * (NG // 2))
                    act.wait_ge(hid_mm, t.at(lambda q: number(q) * HC + c + 1, back))
                    if number(s - back) >= 1:
                        act.wait_ge(agg_mm, t.at(lambda q: (number(q) - 1) * HC + c + 1, back))
                    act.activation(HD[:, c, :], PS[1][:, 0:GR], ACT.Relu, bias=B1[:, c:c + 1], scale=1.0).then_inc(hid_act, 1)

                if is_kind(s + 1, DST):
                    hidden(2, -1)
                if is_kind(s - 5, DENSE):
                    n = number(s - 5)
                    act.wait_ge(u_done, t.at(lambda q: number(q) + 1, 5))
                    if n >= 2:
                        act.wait_ge(y_mm, t.at(lambda q: number(q) - 1, 5))
                    act.activation(flat(S1[n % 2]), PS[0][:, 0:GR], ACT.Silu, bias=UB[:, 0:1], scale=1.0).then_inc(silu_done, 1)
                if is_kind(s + 2, DST):
                    act.wait_ge(seg_done, t.at(lambda q: number(q) + 1, -2))
                    if number(s + 2) >= 1:
                        act.wait_ge(hid_mm, t.at(lambda q: number(q) * HC, -2))
                    act.copy(UT[:], PS[1][:, 0:GR]).then_inc(ut_done, 1)
                    hidden(0, -2)
                if is_kind(s + 1, DST):
                    hidden(3, -1)
                if exists(s - 4):
                    q = s - 4
                    act.wait_ge(z_done, t.at(lambda q: q + 1, 4))
                    if is_kind(q - 2, DST):
                        act.wait_ge(zh_done, t.at(lambda q: number(q) + 1, 6))
                    if is_kind(q - 2, DENSE):
                        act.wait_ge(y_mm, t.at(lambda q: number(q) + 1, 6))
                    if is_kind(q - 2, SRC, DST):
                        act.wait_ge(h1_stored[q % 2], t.at(lambda q: stores(q, SRC, DST), 6))
                    for u in range(G):
                        ins = act.activation(H1[q % 2][:, u, :], Z[q % 4][:, u, :], ACT.Relu,
                                             bias=nb[:, 2, u:u + 1], scale=rs[:, 2, u:u + 1])
                    ins.then_inc(h1_done, 1)
                if is_kind(s + 2, DST):
                    hidden(1, -2)
                i, n, there = message(t, 3)
                if there:
                    act.wait_ge(mm_done, i + 1)
                    if n < 2:
                        act.wait_ge(v_stored[n % 2], 16 * (NG // 2))
                    else:
                        act.wait_ge(msg_stored[n % 2], t.at(lambda q: 16 * ((q - MSG0) // 2), 3))
                    act.activation(flat(V[n % 2]), PS[3][:, 0:GR], ACT.Silu).then_inc(msg_done, 1)

            run(act, step, -1, TICKS, loops)
            update_act(act)

        @block.tensor
        def _(pe):
            pe.wait_ge(prep, SETUP_STEPS)
            pe.matmul(PS[1][:, 0:1], ONES[:], BAD[:, 0:1], start=True, stop=True)
            pe.matmul(PS[2][:, 0:D], ONE3[:], B3[:, 0, 0, :], start=True, stop=False)
            for c in range(HC):
                ins = pe.matmul(PS[2][:, 0:D], RB[:, c, :], W2[:, c, :], start=False, stop=(c == HC - 1))
            ins.then_inc(prep_pe, 1)
            pe.wait_ge(ready, 1)

            def step(t):
                s = t.s

                def hidden(c, back):
                    if c == 0:
                        pe.wait_ge(ut_done, t.at(lambda q: number(q) + 1, back))
                    else:
                        pe.wait_ge(hid_act, t.at(lambda q: number(q) * HC + c, back))
                    for lo, hi in HALVES:
                        ins = pe.matmul(PS[1][:, lo:hi], W1[:, c * P:(c + 1) * P], UT[:, lo:hi], start=True, stop=True)
                    ins.then_inc(hid_mm, 1)

                def aggregate(c, back):
                    if c == 0:
                        if number(s - back) >= 1:
                            pe.wait_ge(g_done, t.at(lambda q: q - 1, back))
                        else:
                            pe.wait_ge(qe_done, NG)
                        bias(pe, PS[3], 0)
                    pe.wait_ge(hid_act, t.at(lambda q: number(q) * HC + c + 1, back))
                    for u in range(G):
                        ins = pe.matmul(PS[3][:, u * P:(u + 1) * P], HD[:, c, u * P:(u + 1) * P], W2[:, c, :],
                                        start=False, stop=(c == HC - 1), skip_group_check=True)
                    ins.then_inc(agg_mm, 1)

                if is_kind(s + 1, DST):
                    hidden(2, -1)
                if is_kind(s - 6, DENSE):
                    n = number(s - 6)
                    if n >= 1:
                        pe.wait_ge(y_done, t.at(lambda q: number(q), 6))
                    bias(pe, PS[2], 2)
                    for rows in (Z[(s - 6) % 4], H1[(s - 6) % 2]):
                        for lo, hi in HALVES:
                            pe.matmul(PS[2][:, lo:hi], ID[:], flat(rows)[:, lo:hi], start=False, stop=False,
                                      skip_group_check=True)
                    pe.wait_ge(silu_done, t.at(lambda q: number(q) + 1, 6))
                    for u in range(G):
                        ins = pe.matmul(PS[2][:, u * P:(u + 1) * P], S1[n % 2][:, u, :], U2[:],
                                        start=False, stop=True, skip_group_check=True)
                    ins.then_inc(y_mm, 1)
                if is_kind(s, DST):
                    aggregate(2, 0)
                if is_kind(s - 5, DENSE):
                    pe.wait_ge(h1_done, t.at(lambda q: q + 1, 5))
                    if number(s - 5) >= 1:
                        pe.wait_ge(silu_done, t.at(lambda q: number(q), 5))
                    for u in range(G):
                        ins = pe.transpose(PS[0][:, u * P:(u + 1) * P], H1[(s - 5) % 2][:, u, :], ID[:])
                    ins.then_inc(t_done, 1)
                if is_kind(s, SRC):
                    n = number(s)
                    pe.wait_ge(e_loaded[n % 2], t.at(ring))
                    if n >= 1:
                        pe.wait_ge(et_out, t.at(number))
                    for u in range(G):
                        ins = pe.transpose(PS[1][:, u * P:(u + 1) * P], E[n % 2][:, u, :], ID[:])
                    ins.then_inc(et_done, 1)
                i, n, there = message(t, 2)
                if there:
                    pe.wait_ge(over[n % 4], t.at(lambda q: 16 * G * ((q - MSG0) // 4 + 1), 2))
                    if n == 0:
                        pe.wait_ge(hid_act, HC * NG)
                    else:
                        pe.wait_ge(mh_done, i)
                    for u in range(G):
                        ins = pe.transpose(PS[1][:, u * P:(u + 1) * P], MH[n % 4][:, u, :], ID[:])
                    ins.then_inc(mt_done, 1)
                if is_kind(s + 1, DST):
                    hidden(3, -1)
                if is_kind(s, DST):
                    aggregate(3, 0)
                if is_kind(s - 5, DENSE):
                    pe.wait_ge(ht_done, t.at(lambda q: number(q) + 1, 5))
                    for lo, hi in HALVES:
                        ins = pe.matmul(PS[0][:, lo:hi], UW[:, 0, :], flat(HT[number(s - 5) % 2])[:, lo:hi], start=True, stop=True)
                    ins.then_inc(u_done, 1)
                if is_kind(s - 1, SRC):
                    n = number(s - 1)
                    if n >= 1:
                        pe.wait_ge(qe_done, t.at(number, 1))
                    bias(pe, PS[3], 1)
                    pe.wait_ge(et_out, t.at(lambda q: number(q) + 1, 1))
                    for u in range(G):
                        ins = pe.matmul(PS[3][:, u * P:(u + 1) * P], HD[:, n % 2, u * P:(u + 1) * P], MW[:, 1, :],
                                        start=False, stop=True, skip_group_check=True)
                    ins.then_inc(qe_mm, 1)
                i, n, there = message(t, 3)
                if there:
                    if n == 0:
                        pe.wait_ge(g_done, LAST_DST + 1)
                    else:
                        pe.wait_ge(msg_done, i)
                    pe.wait_ge(qm_in[n % 4], t.at(lambda q: 16 * ((q - MSG0) // 4 + 1), 3))
                    for lo, hi in HALVES:
                        pe.matmul(PS[3][:, lo:hi], ID[:], flat(MQ[n % 4])[:, lo:hi], start=True, stop=False,
                                  skip_group_check=True)
                    pe.wait_ge(mh_done, i + 1)
                    for u in range(G):
                        ins = pe.matmul(PS[3][:, u * P:(u + 1) * P], HD[:, n % 2, u * P:(u + 1) * P], MW[:, 0, :],
                                        start=False, stop=True, skip_group_check=True)
                    ins.then_inc(mm_done, 1)
                if is_kind(s + 1, DST):
                    aggregate(0, -1)
                    aggregate(1, -1)
                if is_kind(s + 2, DST):
                    n = number(s + 2)
                    pe.wait_ge(window_loaded[n % 2], t.at(lambda q: ring(q, 32), -2))
                    pe.wait_ge(eq_done, t.at(lambda q: number(q) + 1, -2))
                    if n >= 1:
                        pe.wait_ge(hid_act, t.at(lambda q: number(q) * HC, -2))
                    else:
                        pe.wait_ge(et_out, NG)
                    neighbour_sums(pe, PS[1], VG[n % 2]).then_inc(seg_done, 1)
                    hidden(0, -2)
                    hidden(1, -2)

            run(pe, step, -1, TICKS, loops, {MEET: lambda: sums_pe(pe, 0)})
            pe.wait_ge(mh_done, NG)
            pe.wait_ge(msg_done, NG)
            pe.wait_ge(silu_done, ND)
            pe.wait_ge(y_done, ND)
            sums_pe(pe, 1)
            update_pe(pe)

        @block.vector
        def _(dve):
            setup_vector(dve)

            def chain(t, k):
                s = t.s
                if not 0 <= s - 1 < NQ + 4:
                    return
                st, rs, nb = ST[(s - 1) % 2], RS[(s - 1) % 2], NB[(s - 1) % 2]
                total, diff, m2, sq, var, r, a, b = (CS[:, i] for i in range(8))
                need = {0: 0, 1: 0, 2: 0, 3: 2, 4: 4, 5: 5}.get(k, k)
                if need:
                    dve.wait_ge(chain_done, t.at(lambda q: CHAIN * q + need, 1))
                if k == 0:
                    if s >= 2:
                        dve.wait_ge(chain_done, t.at(lambda q: CHAIN * q, 1))
                    dve.wait_ge(st_done, t.at(lambda q: q + 1, 1))
                    if s >= 3:
                        last = 7 if exists(s - 7) else 5 if exists(s - 5) else 3
                        dve.wait_ge({7: h1_done, 5: n_done, 3: h_done}[last], t.at(lambda q: q + 1, last))
                if k == 0:
                    ins = dve.tensor_tensor(total, st[:, :, :, 1], st[:, :, :, 4], ALU.add)
                elif k == 1:
                    ins = dve.tensor_tensor(diff, st[:, :, :, 1], st[:, :, :, 4], ALU.subtract)
                elif k == 2:
                    ins = dve.scalar_tensor_tensor(out=m2, in0=st[:, :, :, 2], scalar=EPS * D, in1=st[:, :, :, 5],
                                                   op0=ALU.add, op1=ALU.add)
                elif k == 3:
                    ins = dve.scalar_tensor_tensor(out=sq, in0=diff, scalar=0.25, in1=diff, op0=ALU.mult, op1=ALU.mult)
                elif k == 4:
                    ins = dve.scalar_tensor_tensor(out=var, in0=m2, scalar=1.0 / D, in1=sq, op0=ALU.mult, op1=ALU.add)
                elif k == 5:
                    ins = dve.tensor_scalar(r.bitcast(I32), var.bitcast(I32), -0.5, MAGIC, ALU.mult, ALU.add)
                elif k < 15:
                    if k % 3 == 0:
                        ins = dve.tensor_tensor(a, r, r, ALU.mult)
                    elif k % 3 == 1:
                        ins = dve.scalar_tensor_tensor(out=b, in0=var, scalar=-0.5, in1=a, op0=ALU.mult, op1=ALU.mult)
                    else:
                        ins = dve.scalar_tensor_tensor(out=rs[:] if k == 14 else r, in0=b, scalar=1.5, in1=r,
                                                       op0=ALU.add, op1=ALU.mult)
                else:
                    ins = dve.scalar_tensor_tensor(out=nb[:], in0=total, scalar=-0.5, in1=rs[:], op0=ALU.mult, op1=ALU.mult)
                ins.then_inc(chain_done, 1)

            def step(t):
                s = t.s
                stats = None
                chain(t, 0)
                chain(t, 1)
                chain(t, 2)
                if exists(s):
                    wait_x(dve, t, x_loaded, x_gathered)
                for u in range(G):
                    if exists(s):
                        stats = dve.bn_stats(ST[s % 2][:, 0, u, :], X[s % 4][:, u, :])
                    chain(t, 3 + u)
                if exists(s - 2):
                    w = W[(s - 2) % 4]
                    dve.wait_ge(h_done, t.at(lambda q: q + 1, 2))
                    if is_kind(s - 2, SRC):
                        n = number(s - 2)
                        dve.wait_ge(e_loaded[n % 2], t.at(ring, 2))
                        if n >= 2:
                            dve.wait_ge(v_stored[n % 2], t.at(lambda q: ring(q) - 16, 2))
                        dve.tensor_tensor(V[n % 2][:], w[:], E[n % 2][:], ALU.add).then_inc(v_done, 1)
                    if is_kind(s - 2, DST):
                        dve.wait_ge(agg_mm, t.at(lambda q: (number(q) + 1) * HC, 2))
                        dve.tensor_tensor(flat(w), flat(w), PS[3][:, 0:GR], ALU.add).then_inc(g_done, 1)
                    else:
                        dve.tensor_tensor(w[:], w[:], each(CR), ALU.add).then_inc(g_done, 1)
                chain(t, 10)
                if exists(s - 4) and not mul_on_pool(s - 4):
                    dve.wait_ge(n_done, t.at(lambda q: q + 1, 4))
                    dve.tensor_tensor(W[s % 4][:], W[s % 4][:], each(GM), ALU.mult).then_inc(dve_mul_done, 1)
                chain(t, 11)
                if exists(s - 2):
                    dve.wait_ge(g_done, t.at(lambda q: q + 1, 2))
                for u in range(G):
                    if exists(s - 2):
                        stats = dve.bn_stats(ST[s % 2][:, 1, u, :], W[(s - 2) % 4][:, u, :])
                    if u < 4:
                        chain(t, 12 + u)
                    if u == 4 and exists(s - 4):
                        if mul_on_pool(s - 4):
                            dve.wait_ge(mul_done, t.at(pool_muls, 4))
                        else:
                            dve.wait_ge(dve_mul_done, t.at(lambda q: q + 1 - pool_muls(q), 4))
                        dve.wait_ge(x_beta, t.at(lambda q: q + 1, 4))
                        if s >= 8:
                            dve.wait_ge(h1_done, t.at(lambda q: q + 1, 8))
                            if is_kind(s - 8, DST):
                                dve.wait_ge(zh_done, t.at(lambda q: number(q) + 1, 8))
                            if is_kind(s - 8, DENSE):
                                dve.wait_ge(y_mm, t.at(lambda q: number(q) + 1, 8))
                        dve.tensor_tensor(Z[s % 4][:], W[s % 4][:], XB[s % 4][:], ALU.add).then_inc(z_done, 1)
                if exists(s - 4):
                    dve.wait_ge(z_done, t.at(lambda q: q + 1, 4))
                    for u in range(G):
                        stats = dve.bn_stats(ST[s % 2][:, 2, u, :], Z[s % 4][:, u, :])
                if stats is not None:
                    stats.then_inc(st_done, 1)
                if is_kind(s + 2, DST):
                    n = number(s + 2)
                    dve.tensor_copy(KC[:], KCF[:, bass.ds(t.at(lambda q: number(q) * G, -2), G + 1)]).then_inc(kc_done, 1)
                    dve.wait_ge(window_loaded[n % 2], t.at(lambda q: ring(q, 32), -2))
                    if n >= 1:
                        dve.wait_ge(seg_done, t.at(lambda q: number(q), -2))
                    dve.wait_ge(kc_done, t.at(lambda q: number(q) + 1, -2))
                    ins = equal_tiles(dve, KR[n % 2])
                    ins.then_inc(eq_done, 1)
                if is_kind(s - 7, DENSE):
                    n = number(s - 7)
                    dve.wait_ge(y_mm, t.at(lambda q: number(q) + 1, 7))
                    if n >= 2:
                        dve.wait_ge(y_stored[n % 2], t.at(lambda q: ring(q) - 16, 7))
                    dve.tensor_copy(flat(Y[n % 2]), PS[2][:, 0:GR]).then_inc(y_done, 1)
                if is_kind(s - 6, DENSE):
                    n = number(s - 6)
                    dve.wait_ge(t_done, t.at(lambda q: number(q) + 1, 6))
                    if n >= 2:
                        dve.wait_ge(u_done, t.at(lambda q: number(q) - 1, 6))
                    dve.tensor_copy(flat(HT[n % 2]), PS[0][:, 0:GR]).then_inc(ht_done, 1)

            run(dve, step, -1, TICKS, loops, {MEET + 1: lambda: sums_vector(dve, 0)})
            dve.wait_ge(mm_done, NG)
            sums_vector(dve, 1)
            update_vector(dve)


def kernel(x, src, dst, edge_attr_128, L0_gnn_W1, L0_gnn_b1, L0_gnn_W2, L0_gnn_b2, L0_gnn_gamma, L0_gnn_beta,
           L1_gnn_mw1, L1_gnn_mb1, L1_gnn_uw1, L1_gnn_ub1, L1_gnn_uw2, L1_gnn_ub2):
    import numpy as np
    import concourse.bacc as bacc
    from concourse.bass_utils import run_bass_kernel_spmd

    n, d = x.shape
    edges = src.shape[0]
    tiles_ = -(-edges // GR) * G
    padded = tiles_ * P
    src_p = np.zeros(padded, np.int32)
    src_p[:edges] = np.asarray(src)
    keys = np.arange(n - edges, n - edges + padded + P, dtype=np.int32)
    keys[:edges] = np.asarray(dst)
    prev = np.concatenate([np.full(1, -1, np.int32), keys[:padded - 1]])
    e_p = np.zeros((padded, d), np.float32)
    e_p[:edges] = np.asarray(edge_attr_128)

    def by_tile(a):
        return np.ascontiguousarray(a.reshape(-1, P).T)

    arrays = {
        "x": x, "e": e_p, "src_t": by_tile(src_p), "dst_t": by_tile(keys), "prev_t": by_tile(prev), "keys": keys,
        "after": np.arange(padded, 0, -1, dtype=np.float32), "ident": np.eye(P, dtype=np.float32), "edge_no": by_tile(np.arange(padded, dtype=np.int32)),
        "w1": L0_gnn_W1, "b1": np.asarray(L0_gnn_b1).reshape(-1, P).T, "w2": L0_gnn_W2, "b2": L0_gnn_b2, "gamma": L0_gnn_gamma, "beta": L0_gnn_beta,
        "mw1": L1_gnn_mw1, "mb1": L1_gnn_mb1, "uw1": L1_gnn_uw1, "ub1": L1_gnn_ub1, "uw2": L1_gnn_uw2, "ub2": L1_gnn_ub2,
    }
    arrays = {f"in_{k}": np.ascontiguousarray(a) for k, a in arrays.items()}
    nc = bacc.Bacc("TRN2", target_bir_lowering=False, num_devices=1)
    aps = [nc.dram_tensor(k, a.shape, mybir.dt.from_np(a.dtype), kind="ExternalInput").ap() for k, a in arrays.items()]
    out = nc.dram_tensor("out", (n, d), F32, kind="ExternalOutput").ap()
    gnn_program(nc, *aps, out)
    r = run_bass_kernel_spmd(nc, [arrays], core_ids=[0])
    return r.results[0]["out"]
```

```python
from contextlib import ExitStack

import concourse.bass as bass
from concourse import mybir

F32 = mybir.dt.float32
I32 = mybir.dt.int32
BF16 = mybir.dt.bfloat16
ALU = mybir.AluOpType
ACT = mybir.ActivationFunctionType
AX_X = mybir.AxisListType.X

P = 128
G = 7
GR = G * P
BODY = 4
EPS = 1e-5
FAR = 1 << 17
MAGIC = 1597463007.0
CHAIN = 16

SRC, DST, DENSE = "src", "dst", "dense"


def plan(n_edge_groups, n_dense_groups):
    first = [SRC, DENSE] * n_edge_groups
    gap = [DENSE] * 4
    second = [DST, DENSE] * n_edge_groups
    rest = [DENSE] * (n_dense_groups - 2 * n_edge_groups - 4)
    kinds = first + gap + second + rest
    lag, ahead = 8, 3
    loops = []
    start = 0
    for part in (first, gap, second, rest):
        lo, hi = start + lag + (BODY if start == 0 else 0), start + len(part) - ahead
        if part is rest:
            lo, hi = max(lo, start + 4 + 4), min(hi, start + 4 + n_edge_groups)
        if hi - lo >= 2 * BODY:
            lo += (start - lo) % BODY
            loops.append((lo, lo + (hi - lo) // BODY * BODY))
        start += len(part)
    upd = len(kinds) + 3
    lo = upd + 6
    loops.append((lo, lo + (upd + n_edge_groups - lo) // BODY * BODY))
    return kinds, loops, len(first), len(first + gap + second) + 4, upd


class Tick:

    def __init__(self, s, body=None, bodies=1):
        self.s, self.body, self.bodies = s, body, bodies

    def at(self, f, back=0):
        q = self.s - back
        if self.body is None:
            return f(q)
        step = f(q + BODY) - f(q)
        assert f(q + (self.bodies - 1) * BODY) == f(q) + (self.bodies - 1) * step
        return f(q) + (self.body * step if step else 0)


def gnn_program(nc, x, e, src_t, dst_t, prev_t, keys, after, ident, edge_no, w1, b1, w2, b2, gamma, beta,
                mw1, mb1, uw1, ub1, uw2, ub2, out):
    N, D = x.shape
    NT = src_t.shape[1]
    NE = NT * P
    NG = NT // G
    HID = w1.shape[1]
    HC = HID // P
    ND = -(-N // GR)
    assert D == P and NT % G == 0 and NG % 2 == 0

    kinds, loops, src_span, MSG0, UPD0 = plan(NG, ND)
    NQ = len(kinds)
    MEET = src_span + 1
    MEET1 = MSG0 + NG + 6
    TICKS = UPD0 + NG + 4
    LAST_DST = max(q for q in range(NQ) if kinds[q] == DST)

    def is_kind(q, *which):
        return 0 <= q < NQ and kinds[q] in which

    def exists(q):
        return 0 <= q < NQ

    def count(q, *which):
        return sum(k in which for k in kinds[:max(q + 1, 0)])

    def number(q):
        return count(q, kinds[q]) - 1

    def x_loads(q):
        return sum(16 for i in range(q % 4, q + 1, 4) if kinds[i] == DENSE)

    def x_gathers(q):
        return 16 * G * ((count(q, SRC, DST) - 1) // 2 + 1)

    def wait_x(eng, t, x_loaded, x_gathered, back=0):
        q = t.s - back
        if kinds[q] == DENSE:
            eng.wait_ge(x_loaded[q % 4], t.at(x_loads, back))
        else:
            eng.wait_ge(x_gathered[(count(q, SRC, DST) - 1) % 2], t.at(x_gathers, back))

    def ring(q, each=16):
        return (number(q) // 2 + 1) * each

    def stores(q, *which):
        return sum(16 for i in range(q % 2, min(q + 1, NQ), 2) if kinds[i] in which)

    def mul_on_pool(q):
        return kinds[q] == DENSE and q >= src_span and (q % 2 == 1 or q < MSG0 - 2)

    def pool_muls(q):
        return sum(mul_on_pool(i) for i in range(q + 1))

    def dense_row(q):
        n = number(q)
        return 0 if n == 0 else N - GR * (ND - n)

    def run(eng, step, first, ticks, loops, meets={}):
        s = first
        for lo, hi in [*loops, (ticks, ticks)]:
            for s in range(s, lo):
                if s in meets:
                    meets[s]()
                step(Tick(s))
            if hi > lo:
                with eng.Fori(0, (hi - lo) // BODY) as body:
                    for u in range(BODY):
                        step(Tick(lo + u, body, (hi - lo) // BODY))
            s = hi

    ctx = ExitStack()
    with ctx:
        def sb(name, shape, dt=F32):
            return ctx.enter_context(nc.sbuf_tensor(name, shape, dt))

        def sem(name):
            return ctx.enter_context(nc.semaphore(name))

        def sems(name, n):
            return [sem(f"{name}_{i}") for i in range(n)]

        def tiles(name, n):
            return [sb(f"{name}_{i}", [P, G, D]) for i in range(n)]

        v_d = nc.dram_tensor("v_scratch", (NE + P, D), F32).ap()
        q_d = nc.dram_tensor("edge_part_scratch", (NE, D), F32).ap()
        m_d = nc.dram_tensor("msg_scratch", (NE + P, D), F32).ap()
        fix_d = nc.dram_tensor("sum_scratch", (NE, D), F32).ap()
        hs_d = nc.dram_tensor("h1_src_scratch", (NE, D), F32).ap()
        hd_d = nc.dram_tensor("h1_dst_scratch", (NE, D), F32).ap()
        zd_d = nc.dram_tensor("x1_h1_dst_scratch", (NE, D), F32).ap()
        slot_d = nc.dram_tensor("slot_of_node_scratch", (N, 1), I32).ap()

        X = tiles("x_in", 4)
        XB = tiles("x_beta", 4)
        W = tiles("work", 4)
        Z = tiles("x1", 4)
        H1 = tiles("h1", 2)
        ZH = tiles("x1_h1", 2)
        Y = tiles("y", 2)
        HT = tiles("h1T", 2)
        S1 = tiles("silu", 2)
        E = tiles("e_in", 2)
        V = tiles("v", 2)
        VG = [sb(f"v_window_{i}", [P, G + 1, D]) for i in range(2)]
        KR = [sb(f"key_row_{i}", [P, GR], I32) for i in range(2)]
        EQ = sb("equal", [P, G + 1, 2 * P])
        KC = sb("key_col_group", [P, G + 1])
        UT = sb("uT", [P, GR])
        HD = sb("hidden", [P, HC, GR])
        IX = [sb(f"gather_index_{i}", [P, G], I32) for i in range(2)]
        MX = [sb(f"map_index_{i}", [P, G], I32) for i in range(2)]
        MV = [sb(f"map_value_{i}", [P, G], I32) for i in range(2)]
        ST = [sb(f"stats_{i}", [P, 3, G, 6]) for i in range(2)]
        RS = [sb(f"rstd_{i}", [P, 3, G]) for i in range(2)]
        NB = [sb(f"minus_mean_rstd_{i}", [P, 3, G]) for i in range(2)]
        CS = sb("chain", [P, 8, 3, G])

        W1 = sb("W1", [P, HID])
        W2 = sb("W2", [P, HC, D])
        B1 = sb("B1", [P, HC])
        RB = sb("relu_b1", [P, HC, P])
        CR = sb("c_row", [P, D])
        GM = sb("gamma_row", [P, D])
        BT = sb("beta_row", [P, D])
        MW = sb("MW1", [P, 2, D])
        UW = sb("UW1", [P, 2, D])
        U2 = sb("UW2", [P, D])
        UB = sb("UB1", [P, 1])
        ID = sb("ident", [P, P])
        BR = sb("bias_rows", [3, 3, D])
        BS = sb("bias_rest", [3, 3, 3, D])
        BH = sb("bias_high", [3, 3, 3, D], BF16)
        B3 = sb("bias_parts", [3, 3, 4, D], BF16)
        ONE3 = sb("ones3", [3, P], BF16)
        ONES = sb("ones", [P, P])
        SRCI = sb("src_index", [P, NT], I32)
        DSTI = sb("dst_key", [P, NT + 1], I32)
        PRVI = sb("prev_key", [P, NT], I32)
        ENO = sb("edge_number", [P, NT], I32)
        KCF = sb("key_col", [P, NT + 1])
        PKF = sb("prev_key_f", [P, NT])
        ENF = sb("edge_number_f", [P, NT])
        LEAD = sb("leader", [P, NT])
        DGI = sb("dst_gather_index", [P, NT], I32)
        LIX = sb("leader_index", [P, NT], I32)
        SLOT = sb("slot_of_src", [P, NT], I32)
        BAD = sb("bad", [P, 4])
        FST = sb("first_of_key", [P, NT])
        FM = sb("first_in_chunk", [P, 1])
        AFT = sb("edges_to_the_end", [P, NT])
        ZERO = sb("zeros", [3, 512], BF16)
        SINK = sb("sink", [1, 1])
        BADI = sb("bad_i", [1, 1], I32)
        FARI = sb("far", [80, N // 80], I32)

        PS = [ctx.enter_context(nc.psum_tensor(f"ps{i}", [P, 1024], F32)) for i in range(4)]
        HALVES = ((0, 512), (512, GR))
        MH = [VG[0][:, 0:G, :], VG[1][:, 0:G, :], *(sb(f"msg_h_{i}", [P, G, D])[:] for i in range(2))]
        MQ = [E[0], E[1], ZH[0], ZH[1]]

        def message(t, back=0):
            return t.at(lambda q: q - MSG0, back), t.s - back - MSG0, 0 <= t.s - back - MSG0 < NG

        def as_tiles(rows):
            return rows.rearrange("p (t d) -> p t d", d=D)

        def flat(t):
            return t[:].rearrange("p t d -> p (t d)")

        def each(row):
            return row[:].unsqueeze(1).broadcast_to([P, G, D])

        def edge_rows(d, row, n=G):
            return d[bass.ds(row, n * P), :].rearrange("(t p) d -> p t d", p=P)

        def node_rows(d, row):
            return d[bass.ds(row, GR), :].rearrange("(p t) d -> p t d", t=G)

        consts_in = sem("consts_in")
        tables_in = sem("tables_in")
        filled = sem("filled")
        prep = sem("prep")
        prep_pe = sem("prep_pe")
        slots_cleared = sem("slots_cleared")
        ready = sem("ready")
        flag_ready = sem("order_flag_ready")
        first_in = sem("first_keys_loaded")
        first_key = sem("first_key_col_done")
        first_done = sem("first_of_key_steps")
        first_ends = sem("first_of_key_ends")
        targets = sems("sums_keys_loaded_and_sums_stored", 2)
        source_in = sems("sums_source_loaded", 2)
        sums_mm = sems("sums_mm", 2)
        sums_equal = sems("sums_equal_done", 2)
        sums_key = sems("sums_key_col_done", 2)
        sums_done = sems("sums_done", 2)
        sums_moved = sems("sums_moved", 2)
        x_loaded = sems("x_loaded", 4)
        x_gathered = sems("x_gathered", 2)
        x_beta = sem("x_beta_done")
        h_done = sem("h_done")
        g_done = sem("g_done")
        n_done = sem("n_done")
        mul_done = sem("mul_done")
        dve_mul_done = sem("dve_mul_done")
        z_done = sem("z_done")
        st_done = sem("st_done")
        chain_done = sem("chain_done")
        h1_done = sem("h1_done")
        zh_done = sem("zh_done")
        e_loaded = sems("e_loaded", 2)
        v_done = sem("v_done")
        v_stored = sems("v_stored", 2)
        window_loaded = sems("window_loaded", 2)
        kc_done = sem("kc_done")
        eq_done = sem("eq_done")
        seg_done = sem("seg_done")
        ut_done = sem("ut_done")
        hid_mm = sem("hid_mm")
        hid_act = sem("hid_act")
        agg_mm = sem("agg_mm")
        t_done = sem("t_done")
        ht_done = sem("ht_done")
        u_done = sem("u_done")
        silu_done = sem("silu_done")
        y_mm = sem("y_mm")
        y_done = sem("y_done")
        y_stored = sems("y_stored", 2)
        h1_stored = sems("h1_stored", 2)
        zh_stored = sems("zh_stored", 2)
        index_done = sem("index_done")
        map_index_done = sem("map_index_done")
        slots_set = sems("slots_set", 2)
        slots_got = sems("slots_got", 2)
        slot_kept = sem("slot_kept")

        et_done = sem("eT_transposed")
        et_out = sem("eT_done")
        qe_mm = sem("edge_part_mm")
        qe_done = sem("edge_part_done")
        qe_stored = sems("edge_part_stored", 2)
        hs_in = sems("msg_h_loaded", 4)
        qm_in = sems("msg_edge_part_loaded", 4)
        over = sems("msg_h_replaced", 4)
        mi_done = sem("msg_index_done")
        mt_done = sem("msg_transposed")
        mh_done = sem("msg_hT_done")
        mm_done = sem("msg_mm")
        msg_done = sem("msg_done")
        msg_stored = sems("msg_stored", 2)
        up_in = sems("upd_window_loaded", 2)
        uh_in = sems("upd_h1_loaded", 4)
        uz_in = sems("upd_x1_h1_loaded", 4)
        uk_done = sem("upd_key_col_done")
        uq_done = sem("upd_equal_done")
        us_done = sem("upd_sums")
        ut2_done = sem("upd_transposed")
        ua_done = sem("upd_aT_done")
        uh_done = sem("upd_hT_done")
        um_done = sem("upd_u_mm")
        usilu_done = sem("upd_silu_done")
        uy_mm = sem("upd_y_mm")
        uy_done = sem("upd_y_done")
        ui_done = sem("upd_index_done")
        scattered = sems("upd_scattered", 2)

        def equal_tiles(dve, row):
            for j in range(G + 1):
                lo, hi = max(j - 1, 0) * P, min(j + 1, G) * P
                at = P if j == 0 else 0
                ins = dve.tensor_scalar(EQ[:, j, at:at + hi - lo], row[:, lo:hi], KC[:, j:j + 1], None, ALU.is_equal)
            return ins

        def neighbour_sums(pe, ps, rows):
            for u in range(G):
                own = u * P, (u + 1) * P
                pe.matmul(ps[:, own[0]:own[1]], rows[:, u, :], EQ[:, u, P:2 * P],
                          start=(u * P % 512 == 0), stop=False, skip_group_check=True)
                ins = pe.matmul(ps[:, own[0]:own[1]], rows[:, u + 1, :], EQ[:, u + 1, 0:P],
                                start=False, stop=True, skip_group_check=True)
            return ins

        def bias(pe, ps, which):
            for lo, hi in HALVES:
                pe.matmul(ps[:, lo:hi], ONE3[:], B3[:, which].rearrange("k t d -> k (t d)")[:, 0:hi - lo],
                          start=True, stop=False, skip_group_check=True)

        def take_waits(pool):
            pool.tensor_tensor(SINK[:], ONES[0:1, 0:1], ONES[0:1, 0:1], ALU.mult)

        def update(t, back=0):
            return t.at(lambda q: q - UPD0, back), t.s - back - UPD0, 0 <= t.s - back - UPD0 < NG

        UH, UHT, UAT = X, [HD[:, 2, :], HD[:, 3, :]], [HD[:, 0, :], HD[:, 1, :]]
        US, UY = V, MH[2:4]
        UPS = [(PS[1], PS[3]), (PS[0], PS[2])]

        def update_sync(sp, t):
            i, n, there = update(t)
            if not there:
                return
            if n == 0:
                sp.wait_ge(mt_done, NG)
                sp.wait_ge(mm_done, NG)
                sp.wait_ge(eq_done, NG)
                sp.wait_ge(h_done, NQ)
                sp.wait_ge(x_beta, NQ)
                for k in range(2):
                    sp.wait_ge(msg_stored[k], 16 * (NG // 2))
            if n >= 2:
                sp.wait_ge(us_done, i - 1)
            sp.dma_start(VG[n % 2][:], edge_rows(m_d, i * GR, G + 1)).then_inc(up_in[n % 2], 16)
            sp.dma_start(KR[n % 2][:], keys[bass.ds(i * GR, GR)].partition_broadcast(P)).then_inc(up_in[n % 2], 16)
            if n >= 4:
                sp.wait_ge(ut2_done, i - 3)
            sp.dma_start(UH[n % 4][:], edge_rows(hd_d, i * GR)).then_inc(uh_in[n % 4], 16)
            if n >= 4:
                sp.wait_ge(uy_done, i - 3)
            sp.dma_start(MQ[n % 4][:], edge_rows(zd_d, i * GR)).then_inc(uz_in[n % 4], 16)

        def ring_of(t, size, back):
            return t.at(lambda q: (q - UPD0) // size + 1, back)

        def update_vector(dve, t):
            i, n, there = update(t, 2)
            if there:
                dve.wait_ge(ut2_done, i + 1)
                if n == 0:
                    for k in range(2):
                        dve.wait_ge(mm_done, NG)
                else:
                    dve.wait_ge(um_done, i)
                dve.tensor_copy(UHT[n % 2], UPS[n % 2][1][:, 0:GR]).then_inc(uh_done, 1)
            i, n, there = update(t, 1)
            if there:
                if n >= 1:
                    dve.wait_ge(uq_done, i)
                else:
                    dve.wait_ge(eq_done, NG)
                dve.tensor_copy(KC[:], KCF[:, bass.ds(i * G, G + 1)]).then_inc(uk_done, 1)
                dve.wait_ge(up_in[n % 2], ring_of(t, 2, 1) * 32)
                if n >= 1:
                    dve.wait_ge(us_done, i)
                dve.wait_ge(uk_done, i + 1)
                equal_tiles(dve, KR[n % 2]).then_inc(uq_done, 1)
            i, n, there = update(t, 3)
            if there:
                dve.wait_ge(uy_mm, i + 1)
                dve.wait_ge(uz_in[n % 4], ring_of(t, 4, 3) * 16)
                if n >= 2:
                    dve.wait_ge(scattered[n % 2], t.at(lambda q: 16 * G * ((q - UPD0) // 2), 3))
                dve.tensor_tensor(UY[n % 2].rearrange("p t d -> p (t d)"), UPS[n % 2][1][:, 0:GR], flat(MQ[n % 4]),
                                  ALU.add).then_inc(uy_done, 1)

        def update_act(act, t):
            i, n, there = update(t, 2)
            if there:
                act.wait_ge(um_done, i + 1)
                if n >= 2:
                    act.wait_ge(uy_mm, i - 1)
                else:
                    act.wait_ge(msg_stored[n % 2], 16 * (NG // 2))
                act.activation(flat(US[n % 2]), UPS[n % 2][0][:, 0:GR], ACT.Silu, bias=UB[:, 0:1], scale=1.0).then_inc(usilu_done, 1)
            i, n, there = update(t, 1)
            if there:
                act.wait_ge(us_done, i + 1)
                if n >= 2:
                    act.wait_ge(um_done, i - 1)
                else:
                    act.wait_ge(mm_done, NG)
                act.copy(UAT[n % 2], UPS[n % 2][0][:, 0:GR]).then_inc(ua_done, 1)

        def update_pe(pe, t):
            i, n, there = update(t, 3)
            if there:
                ps = UPS[n % 2][1]
                pe.wait_ge(uh_done, i + 1)
                bias(pe, ps, 2)
                pe.wait_ge(usilu_done, i + 1)
                for u in range(G):
                    ins = pe.matmul(ps[:, u * P:(u + 1) * P], US[n % 2][:, u, :], U2[:],
                                    start=False, stop=True, skip_group_check=True)
                ins.then_inc(uy_mm, 1)
            i, n, there = update(t, 2)
            if there:
                pe.wait_ge(uh_done, i + 1)
                pe.wait_ge(ua_done, i + 1)
                for lo, hi in HALVES:
                    pe.matmul(UPS[n % 2][0][:, lo:hi], UW[:, 0, :], UHT[n % 2][:, lo:hi], start=True, stop=False)
                    ins = pe.matmul(UPS[n % 2][0][:, lo:hi], UW[:, 1, :], UAT[n % 2][:, lo:hi], start=False, stop=True)
                ins.then_inc(um_done, 1)
            i, n, there = update(t, 1)
            if there:
                if n == 0:
                    pe.wait_ge(mh_done, NG)
                    pe.wait_ge(msg_done, NG)
                elif n == 1:
                    pe.wait_ge(silu_done, ND)
                else:
                    pe.wait_ge(usilu_done, i - 1)
                pe.wait_ge(up_in[n % 2], ring_of(t, 2, 1) * 32)
                pe.wait_ge(uq_done, i + 1)
                neighbour_sums(pe, UPS[n % 2][0], VG[n % 2]).then_inc(us_done, 1)
                pe.wait_ge(uh_in[n % 4], ring_of(t, 4, 1) * 16)
                if n == 1:
                    pe.wait_ge(y_done, ND)
                if n >= 2:
                    pe.wait_ge(uy_done, i - 1)
                for u in range(G):
                    ins = pe.transpose(UPS[n % 2][1][:, u * P:(u + 1) * P], UH[n % 4][:, u, :], ID[:])
                ins.then_inc(ut2_done, 1)

        def update_pool(pool, t, last_node):
            i, n, there = update(t, 4)
            if not there:
                return
            if n == 0:
                for k in range(4):
                    pool.wait_ge(over[k], 16 * G * ((NG - k + 3) // 4))
                for k in range(2):
                    pool.wait_ge(y_stored[k], 16 * (ND // 2))
            if n >= 2:
                pool.wait_ge(scattered[n % 2], t.at(lambda q: 16 * G * ((q - UPD0) // 2), 4))
            pool.tensor_copy(IX[n % 2][:], LIX[:, bass.ds(i * G, G)]).then_inc(ui_done, 1)
            pool.wait_ge(ui_done, i + 1)
            pool.wait_ge(uy_done, i + 1)
            take_waits(pool)
            for u in range(G):
                pool.indirect_dma_start(
                    out=out, out_offset=bass.IndirectOffsetOnAxis(ap=IX[n % 2][:, u:u + 1], axis=0),
                    in_=UY[n % 2][:, u, :], in_offset=None,
                    bounds_check=last_node, oob_is_err=False).then_inc(scattered[n % 2], 16)


        def flagged(eng):
            return eng.value_load(BADI[0:1, 0:1])

        SETS = 1 + NT

        def leaders_sync(sp):
            sp.wait_ge(flag_ready, 1)
            with sp.If(flagged(sp)):
                with sp.Fori(0, NG) as c:
                    sp.wait_ge(first_done, c * (3 * NT) + 1)
                    sp.dma_start(KR[0][:], keys[bass.ds(c * GR, GR)].partition_broadcast(P)).then_inc(first_in, 16)
                    sp.dma_start(UT[:], after[bass.ds(c * GR, GR)].partition_broadcast(P)).then_inc(first_in, 16)

        def leaders_vector(dve):
            product = flat(EQ)[:, 0:GR]
            with dve.If(flagged(dve)):
                dve.memset(FST[:], 0.0).then_inc(first_done, 1)
                dve.wait_ge(first_done, 1)
                with dve.Fori(0, NG) as c:
                    with dve.Fori(0, NT) as i:
                        n = c * (3 * NT) + i * 3 + 1
                        dve.wait_ge(first_in, (c + 1) * 32)
                        dve.tensor_copy(KC[:, 0:1], KCF[:, bass.ds(i, 1)]).then_inc(first_key, 1)
                        dve.wait_ge(first_key, c * NT + i + 1)
                        dve.scalar_tensor_tensor(out=product, in0=KR[0][:], scalar=KC[:, 0:1], in1=UT[:],
                                                 op0=ALU.is_equal, op1=ALU.mult).then_inc(first_done, 1)
                        dve.wait_ge(first_done, n + 1)
                        dve.tensor_reduce(out=FM[:], in_=product, axis=AX_X, op=ALU.max).then_inc(first_done, 1)
                        dve.wait_ge(first_done, n + 2)
                        dve.tensor_tensor(FST[:, bass.ds(i, 1)], FST[:, bass.ds(i, 1)], FM[:], ALU.max).then_inc(first_done, 1)
                        dve.wait_ge(first_done, n + 3)
                dve.tensor_scalar(AFT[:], ENO[:], -1.0, float(NE), ALU.mult, ALU.add).then_inc(first_ends, 1)
                dve.wait_ge(first_ends, 1)
                dve.tensor_tensor(LEAD[:], AFT[:], FST[:], ALU.is_equal).then_inc(first_ends, 1)
                dve.wait_ge(first_ends, 2)

        def sums_sync(sp, layer):
            rows = (v_d, m_d)[layer]
            with sp.If(flagged(sp)):
                with sp.Fori(0, NG) as i:
                    sp.dma_start(KR[0][:], keys[bass.ds(i * GR, GR)].partition_broadcast(P)).then_inc(targets[layer], 16)
                    with sp.Fori(0, NG) as j:
                        sp.wait_ge(targets[layer], i * 32 + 16)
                        sp.wait_ge(sums_mm[layer], i * SETS + j * G + 1)
                        sp.dma_start(VG[0][:, 0:G, :], edge_rows(rows, j * GR)).then_inc(source_in[layer], 16)
                    sp.wait_ge(sums_done[layer], i + 1)
                    sp.dma_start(edge_rows(fix_d, i * GR), V[0][:]).then_inc(targets[layer], 16)
                sp.wait_ge(targets[layer], NG * 32)
                sp.dma_start(rows[0:NE, :], fix_d).then_inc(sums_moved[layer], 16)
                sp.wait_ge(sums_moved[layer], 16)

        def sums_pe(pe, layer):
            with pe.If(flagged(pe)):
                if layer == 0:
                    pe.wait_ge(et_out, NG)
                with pe.Fori(0, NG) as i:
                    pe.wait_ge(targets[layer], i * 32 + 16)
                    for lo, hi in HALVES:
                        ins = pe.matmul(PS[1][:, lo:hi], ONE3[:], ZERO[:, 0:hi - lo], start=True, stop=False,
                                        skip_group_check=True)
                    ins.then_inc(sums_mm[layer], 1)
                    with pe.Fori(0, NG) as j:
                        pe.wait_ge(source_in[layer], (i * NG + j + 1) * 16)
                        for v in range(G):
                            pe.wait_ge(sums_equal[layer], i * NT + j * G + v + 1)
                            for u in range(G):
                                ins = pe.matmul(PS[1][:, u * P:(u + 1) * P], HD[:, 0, u * P:(u + 1) * P], VG[0][:, v, :],
                                                start=False, stop=True, skip_group_check=True)
                            ins.then_inc(sums_mm[layer], 1)
                    pe.wait_ge(sums_done[layer], i + 1)

        def sums_vector(dve, layer):
            with dve.If(flagged(dve)):
                if layer == 0:
                    dve.wait_ge(qe_mm, NG)
                with dve.Fori(0, NG) as i:
                    with dve.Fori(0, NG) as j:
                        dve.wait_ge(targets[layer], i * 32 + 16)
                        dve.wait_ge(sums_mm[layer], i * SETS + j * G + 1)
                        dve.tensor_copy(KC[:], KCF[:, bass.ds(j * G, G + 1)]).then_inc(sums_key[layer], 1)
                        dve.wait_ge(sums_key[layer], i * (NG + 1) + j + 1)
                        for v in range(G):
                            dve.wait_ge(sums_mm[layer], i * SETS + j * G + v + 1)
                            dve.tensor_scalar(HD[:, 0, :], KR[0][:], KC[:, v:v + 1], None,
                                              ALU.is_equal).then_inc(sums_equal[layer], 1)
                    dve.wait_ge(sums_mm[layer], (i + 1) * SETS)
                    dve.wait_ge(sums_equal[layer], (i + 1) * NT)
                    dve.tensor_copy(KC[:, 0:G], LEAD[:, bass.ds(i * G, G)]).then_inc(sums_key[layer], 1)
                    dve.wait_ge(sums_key[layer], (i + 1) * (NG + 1))
                    for u in range(G):
                        ins = dve.tensor_scalar(V[0][:, u, :], PS[1][:, u * P:(u + 1) * P], KC[:, u:u + 1], None, ALU.mult)
                    ins.then_inc(sums_done[layer], 1)
                dve.wait_ge(sums_done[layer], NG)

        def setup_vector(dve):
            done = [0]

            def then(ins):
                done[0] += 1
                ins.then_inc(prep, 1)
                dve.wait_ge(prep, done[0])

            dve.wait_ge(tables_in, 16 * len(TABLES))
            dve.wait_ge(filled, 1)
            dve.tensor_copy(KCF[:], DSTI[:])
            then(dve.tensor_copy(PKF[:], PRVI[:]))
            key = KCF[:, 0:NT]
            tmp = flat(W[0])[:, 0:NT]
            tmp2 = flat(W[1])[:, 0:NT]
            dve.tensor_scalar(DGI[:], key, float(N - 1), None, ALU.min)
            dve.tensor_tensor(LEAD[:], PKF[:], key, ALU.not_equal)
            dve.tensor_tensor(tmp, PKF[:], key, ALU.is_gt)
            then(dve.tensor_tensor(tmp2, KCF[:, 1:NT + 1], key, ALU.is_le))
            then(dve.tensor_tensor(tmp, tmp, tmp2, ALU.add))
            then(dve.reduce_sum(BAD[:, 0:1], tmp, AX_X))
            dve.wait_ge(consts_in, 16 * len(CONSTS))
            for c in range(HC):
                dve.tensor_scalar(RB[:, c, :], ONES[:], B1[:, c:c + 1], 0.0, ALU.mult, ALU.max)
            then(dve.tensor_copy(BH[:, 0], BR[:]))
            then(dve.tensor_tensor(BS[:, 0], BR[:], BH[:, 0], ALU.subtract))
            then(dve.tensor_copy(BH[:, 1], BS[:, 0]))
            then(dve.tensor_tensor(BS[:, 1], BS[:, 0], BH[:, 1], ALU.subtract))
            then(dve.tensor_copy(BH[:, 2], BS[:, 1]))
            then(dve.tensor_scalar(BS[:, 0], BH[:, 0], ID[0:3, 0:1], None, ALU.mult))
            then(dve.scalar_tensor_tensor(out=BS[:, 1], in0=BH[:, 1], scalar=ID[0:3, 1:2], in1=BS[:, 0],
                                          op0=ALU.mult, op1=ALU.add))
            then(dve.scalar_tensor_tensor(out=BS[:, 2], in0=BH[:, 2], scalar=ID[0:3, 2:3], in1=BS[:, 1],
                                          op0=ALU.mult, op1=ALU.add))
            then(dve.tensor_copy(B3[:], BS[:, 2].unsqueeze(2).broadcast_to([3, 3, 4, D])))
            assert done[0] == SETUP_STEPS
            dve.wait_ge(prep_pe, 1)
            dve.tensor_copy(CR[:], PS[2][:, 0:D])
            dve.tensor_copy(BADI[:], PS[1][0:1, 0:1]).then_inc(flag_ready, 1)
            dve.wait_ge(flag_ready, 1)
            leaders_vector(dve)
            tmp3 = flat(W[2])[:, 0:NT]
            then(dve.tensor_scalar(tmp3, LEAD[:], -float(FAR), float(FAR), ALU.mult, ALU.add))
            dve.tensor_tensor(LIX[:], tmp3, KCF[:, 0:NT], ALU.add).then_inc(ready, 1)

        SETUP_STEPS = 13

        block = ctx.enter_context(nc.Block())
        CONSTS = [(W1[:], w1), (W2[:], w2.rearrange("(c p) d -> p c d", p=P)),
                  (B1[:], b1),
                  (GM[:], gamma.partition_broadcast(P)), (BT[:], beta.partition_broadcast(P)),
                  (MW[:], mw1.rearrange("(c p) d -> p c d", p=P)), (UW[:], uw1.rearrange("(c p) d -> p c d", p=P)),
                  (U2[:], uw2), (UB[:], ub1.rearrange("(p a) -> p a", a=1)), (ID[:], ident),
                  (BR[:, 0, :], b2.partition_broadcast(3)), (BR[:, 1, :], mb1.partition_broadcast(3)),
                  (BR[:, 2, :], ub2.partition_broadcast(3))]
        TABLES = [(DSTI[:], dst_t), (PRVI[:], prev_t), (SRCI[:], src_t), (ENO[:], edge_no)]

        @block.sync
        def _(sp):
            for t, a in TABLES:
                sp.dma_start(t, a).then_inc(tables_in, 16)
            for t, a in CONSTS:
                sp.dma_start(t, a).then_inc(consts_in, 16)
            sp.wait_ge(filled, 1)
            sp.dma_start(slot_d.rearrange("(p n) a -> p (n a)", p=80), FARI[:]).then_inc(slots_cleared, 16)
            sp.dma_start(v_d[NE:NE + P, :], Z[0][:, 0, :]).then_inc(slots_cleared, 16)
            sp.dma_start(m_d[NE:NE + P, :], Z[0][:, 0, :]).then_inc(slots_cleared, 16)

            def step(t):
                s = t.s
                if is_kind(s + 3, DENSE):
                    if s >= 1:
                        sp.wait_ge(h_done, t.at(lambda q: q + 1, 1))
                        sp.wait_ge(x_beta, t.at(lambda q: q + 1, 1))
                    sp.dma_start(X[(s + 3) % 4][:], node_rows(x, t.at(dense_row, -3))).then_inc(x_loaded[(s + 3) % 4], 16)
                if is_kind(s + 3, SRC):
                    n = number(s + 3)
                    if n >= 2:
                        sp.wait_ge(v_done, t.at(lambda q: number(q) - 1, -3))
                        sp.wait_ge(et_done, t.at(lambda q: number(q) - 1, -3))
                    sp.dma_start(E[n % 2][:], edge_rows(e, t.at(lambda q: number(q) * GR, -3))).then_inc(e_loaded[n % 2], 16)
                if is_kind(s + 3, DST):
                    n = number(s + 3)
                    if n >= 2:
                        sp.wait_ge(seg_done, t.at(lambda q: number(q) - 1, -3))
                    row = t.at(lambda q: number(q) * GR, -3)
                    sp.dma_start(VG[n % 2][:], edge_rows(v_d, row, G + 1)).then_inc(window_loaded[n % 2], 16)
                    sp.dma_start(KR[n % 2][:], keys[bass.ds(row, GR)].partition_broadcast(P)).then_inc(window_loaded[n % 2], 16)
                if is_kind(s - 2, SRC):
                    n = number(s - 2)
                    sp.wait_ge(v_done, t.at(lambda q: number(q) + 1, 2))
                    sp.dma_start(edge_rows(v_d, t.at(lambda q: number(q) * GR, 2)), V[n % 2][:]).then_inc(v_stored[n % 2], 16)
                if is_kind(s - 3, SRC):
                    n = number(s - 3)
                    sp.wait_ge(qe_done, t.at(lambda q: number(q) + 1, 3))
                    sp.dma_start(edge_rows(q_d, t.at(lambda q: number(q) * GR, 3)),
                                 as_tiles(HD[:, 2 + n % 2, :])).then_inc(qe_stored[n % 2], 16)
                if is_kind(s - 5, SRC, DST):
                    sp.wait_ge(h1_done, t.at(lambda q: q + 1, 5))
                    to = hs_d if kinds[s - 5] == SRC else hd_d
                    sp.dma_start(edge_rows(to, t.at(lambda q: number(q) * GR, 5)), H1[(s - 5) % 2][:]).then_inc(h1_stored[(s - 5) % 2], 16)
                if is_kind(s - 6, DST):
                    n = number(s - 6)
                    sp.wait_ge(zh_done, t.at(lambda q: number(q) + 1, 6))
                    sp.dma_start(edge_rows(zd_d, t.at(lambda q: number(q) * GR, 6)), ZH[n % 2][:]).then_inc(zh_stored[n % 2], 16)
                if is_kind(s - 8, DENSE):
                    n = number(s - 8)
                    sp.wait_ge(y_done, t.at(lambda q: number(q) + 1, 8))
                    if n == 1:
                        sp.wait_ge(y_stored[0], 16)
                    sp.dma_start(node_rows(out, t.at(dense_row, 8)), Y[n % 2][:]).then_inc(y_stored[n % 2], 16)
                i, n, there = message(t)
                if there:
                    if n == 0:
                        sp.wait_ge(h1_stored[0], stores(NQ, SRC))
                        for k in range(2):
                            sp.wait_ge(qe_stored[k], 16 * (NG // 2))
                            sp.wait_ge(zh_stored[k], 16 * (NG // 2))
                        sp.wait_ge(v_done, NG)
                        sp.wait_ge(et_done, NG)
                        sp.wait_ge(seg_done, NG)
                    if n >= 4:
                        sp.wait_ge(mm_done, i - 3)
                    sp.dma_start(MH[n % 4], edge_rows(hs_d, i * GR)).then_inc(hs_in[n % 4], 16)
                    sp.dma_start(MQ[n % 4][:], edge_rows(q_d, i * GR)).then_inc(qm_in[n % 4], 16)
                i, n, there = message(t, 4)
                if there:
                    sp.wait_ge(msg_done, i + 1)
                    sp.dma_start(edge_rows(m_d, i * GR), V[n % 2][:]).then_inc(msg_stored[n % 2], 16)
                update_sync(sp, t)

            def meet():
                for n in range(2):
                    sp.wait_ge(v_stored[n], 16 * (NG // 2))
                sp.wait_ge(slots_cleared, 48)
                sums_sync(sp, 0)

            def meet1():
                for n in range(2):
                    sp.wait_ge(msg_stored[n], 16 * (NG // 2))
                sp.wait_ge(mt_done, NG)
                sp.wait_ge(eq_done, NG)
                sums_sync(sp, 1)

            run(sp, step, -3, TICKS, loops, {0: lambda: leaders_sync(sp), MEET: meet, MEET1: meet1})

        @block.gpsimd
        def _(pool):
            for t in (0, 1):
                pool.memset(ST[t][:], 1.0)
            pool.memset(FARI[:], FAR)
            pool.memset(Z[0][:, 0, :], 0.0)
            pool.memset(ONE3[:], 1.0)
            pool.memset(ZERO[:], 0.0)
            pool.memset(ONES[:], 1.0).then_inc(filled, 1)
            pool.wait_ge(tables_in, 16 * len(TABLES))
            last_node = pool.to_reg(N - 1)
            last_edge = pool.to_reg(NE - 1)

            def step(t):
                s = t.s
                if s == 1:
                    pool.wait_ge(consts_in, 16 * len(CONSTS))
                if exists(s - 1):
                    wait_x(pool, t, x_loaded, x_gathered, 1)
                    if s >= 5:
                        pool.wait_ge(z_done, t.at(lambda q: q - 3, 1))
                    pool.tensor_tensor(XB[(s - 1) % 4][:], X[(s - 1) % 4][:], each(BT), ALU.add).then_inc(x_beta, 1)
                if exists(s - 3) and mul_on_pool(s - 3):
                    pool.wait_ge(n_done, t.at(lambda q: q + 1, 3))
                    pool.tensor_tensor(W[(s - 3) % 4][:], W[(s - 3) % 4][:], each(GM), ALU.mult).then_inc(mul_done, 1)
                if is_kind(s + 3, SRC, DST):
                    n = count(s + 3, SRC, DST) - 1
                    index = SRCI if kinds[s + 3] == SRC else DGI
                    pool.tensor_copy(IX[n % 2][:], index[:, bass.ds(t.at(lambda q: number(q) * G, -3), G)]).then_inc(index_done, 1)
                    if s >= 1:
                        pool.wait_ge(h_done, t.at(lambda q: q + 1, 1))
                        pool.wait_ge(x_beta, t.at(lambda q: q + 1, 1))
                    pool.wait_ge(index_done, t.at(lambda q: count(q, SRC, DST), -3))
                    take_waits(pool)
                    for u in range(G):
                        pool.indirect_dma_start(
                            out=X[(s + 3) % 4][:, u, :], out_offset=None, in_=x,
                            in_offset=bass.IndirectOffsetOnAxis(ap=IX[n % 2][:, u:u + 1], axis=0),
                            bounds_check=last_node, oob_is_err=False).then_inc(x_gathered[n % 2], 16)
                if is_kind(s - 5, DST):
                    n = number(s - 5)
                    pool.wait_ge(h1_done, t.at(lambda q: q + 1, 5))
                    if n >= 2:
                        pool.wait_ge(zh_stored[n % 2], t.at(lambda q: ring(q) - 16, 5))
                    pool.tensor_tensor(ZH[n % 2][:], Z[(s - 5) % 4][:], H1[(s - 5) % 2][:], ALU.add).then_inc(zh_done, 1)
                if is_kind(s, SRC):
                    n = number(s)
                    if s == 0:
                        pool.wait_ge(ready, 1)
                        pool.wait_ge(slots_cleared, 48)
                    if n >= 2:
                        pool.wait_ge(slots_set[n % 2], t.at(lambda q: ring(q, 16 * G) - 16 * G))
                    pool.tensor_copy(MX[n % 2][:], LIX[:, bass.ds(t.at(lambda q: number(q) * G), G)]).then_inc(map_index_done, 1)
                    pool.tensor_copy(MV[n % 2][:], ENO[:, bass.ds(t.at(lambda q: number(q) * G), G)]).then_inc(map_index_done, 1)
                    pool.wait_ge(map_index_done, t.at(lambda q: 2 * count(q, SRC)))
                    take_waits(pool)
                    for u in range(G):
                        pool.indirect_dma_start(
                            out=slot_d, out_offset=bass.IndirectOffsetOnAxis(ap=MX[n % 2][:, u:u + 1], axis=0),
                            in_=MV[n % 2][:, u:u + 1], in_offset=None,
                            bounds_check=last_node, oob_is_err=False).then_inc(slots_set[n % 2], 16)
                if is_kind(s, DST):
                    n = number(s)
                    if n == 0:
                        for k in range(2):
                            pool.wait_ge(slots_set[k], 16 * G * (NG // 2))
                    pool.tensor_copy(MX[n % 2][:], SRCI[:, bass.ds(t.at(lambda q: number(q) * G), G)]).then_inc(map_index_done, 1)
                    if n >= 2:
                        pool.wait_ge(slot_kept, t.at(lambda q: number(q) - 1))
                    pool.wait_ge(map_index_done, t.at(lambda q: 2 * NG + count(q, DST)))
                    take_waits(pool)
                    for u in range(G):
                        pool.indirect_dma_start(
                            out=MV[n % 2][:, u:u + 1], out_offset=None, in_=slot_d,
                            in_offset=bass.IndirectOffsetOnAxis(ap=MX[n % 2][:, u:u + 1], axis=0),
                            bounds_check=last_node, oob_is_err=False).then_inc(slots_got[n % 2], 16)
                i, n, there = message(t, 1)
                if there:
                    if n == 0:
                        pool.wait_ge(h1_stored[0], stores(NQ, SRC, DST))
                        pool.wait_ge(slot_kept, NG)
                        for k in range(2):
                            pool.wait_ge(x_gathered[k], 16 * G * NG)
                    if n >= 2:
                        pool.wait_ge(over[(n - 2) % 4], t.at(lambda q: 16 * G * ((q - MSG0 - 2) // 4 + 1), 1))
                    pool.tensor_copy(IX[n % 2][:], SLOT[:, bass.ds(i * G, G)]).then_inc(mi_done, 1)
                    pool.wait_ge(mi_done, i + 1)
                    pool.wait_ge(hs_in[n % 4], t.at(lambda q: 16 * ((q - MSG0) // 4 + 1), 1))
                    take_waits(pool)
                    for u in range(G):
                        pool.indirect_dma_start(
                            out=MH[n % 4][:, u, :], out_offset=None, in_=hd_d,
                            in_offset=bass.IndirectOffsetOnAxis(ap=IX[n % 2][:, u:u + 1], axis=0),
                            bounds_check=last_edge, oob_is_err=False).then_inc(over[n % 4], 16)
                if is_kind(s - 1, DST):
                    n = number(s - 1)
                    pool.wait_ge(slots_got[n % 2], t.at(lambda q: ring(q, 16 * G), 1))
                    pool.tensor_copy(SLOT[:, bass.ds(t.at(lambda q: number(q) * G, 1), G)], MV[n % 2][:]).then_inc(slot_kept, 1)
                update_pool(pool, t, last_node)

            run(pool, step, -3, TICKS, loops)
            for k in range(2):
                pool.wait_ge(scattered[k], 16 * G * (NG // 2))

        @block.scalar
        def _(act):
            act.wait_ge(ready, 1)

            def step(t):
                s = t.s
                if 0 <= s < NQ + 4:
                    act.wait_ge(chain_done, t.at(lambda q: CHAIN * (q + 1)))
                    rs, nb = RS[s % 2], NB[s % 2]
                if exists(s):
                    if s >= 4:
                        act.wait_ge(z_done, t.at(lambda q: q - 3))
                    for u in range(G):
                        ins = act.activation(W[s % 4][:, u, :], X[s % 4][:, u, :], ACT.Relu,
                                             bias=nb[:, 0, u:u + 1], scale=rs[:, 0, u:u + 1])
                    ins.then_inc(h_done, 1)
                def hidden(c, back):
                    if number(s - back) == 0:
                        act.wait_ge(qe_mm, NG)
                        for k in range(2):
                            act.wait_ge(qe_stored[k], 16 * (NG // 2))
                    act.wait_ge(hid_mm, t.at(lambda q: number(q) * HC + c + 1, back))
                    if number(s - back) >= 1:
                        act.wait_ge(agg_mm, t.at(lambda q: (number(q) - 1) * HC + c + 1, back))
                    act.activation(HD[:, c, :], PS[1][:, 0:GR], ACT.Relu, bias=B1[:, c:c + 1], scale=1.0).then_inc(hid_act, 1)

                if is_kind(s + 2, DST):
                    act.wait_ge(seg_done, t.at(lambda q: number(q) + 1, -2))
                    if number(s + 2) >= 1:
                        act.wait_ge(hid_mm, t.at(lambda q: number(q) * HC, -2))
                    act.copy(UT[:], PS[1][:, 0:GR]).then_inc(ut_done, 1)
                if is_kind(s + 1, DST):
                    hidden(2, -1)
                if exists(s - 2):
                    act.wait_ge(g_done, t.at(lambda q: q + 1, 2))
                    for u in range(G):
                        ins = act.activation(W[(s - 2) % 4][:, u, :], W[(s - 2) % 4][:, u, :], ACT.Identity,
                                             bias=nb[:, 1, u:u + 1], scale=rs[:, 1, u:u + 1])
                    ins.then_inc(n_done, 1)

                if is_kind(s, SRC):
                    n = number(s)
                    act.wait_ge(et_done, t.at(lambda q: number(q) + 1))
                    if n >= 2:
                        act.wait_ge(qe_mm, t.at(lambda q: number(q) - 1))
                    act.copy(HD[:, n % 2, :], PS[1][:, 0:GR]).then_inc(et_out, 1)
                if is_kind(s - 1, SRC):
                    n = number(s - 1)
                    act.wait_ge(qe_mm, t.at(lambda q: number(q) + 1, 1))
                    if n >= 2:
                        act.wait_ge(qe_stored[n % 2], t.at(lambda q: ring(q) - 16, 1))
                    act.copy(HD[:, 2 + n % 2, :], PS[3][:, 0:GR]).then_inc(qe_done, 1)
                i, n, there = message(t, 2)
                if there:
                    act.wait_ge(mt_done, i + 1)
                    if n < 2:
                        act.wait_ge(agg_mm, HC * NG)
                    else:
                        act.wait_ge(mm_done, i - 1)
                    act.copy(HD[:, n % 2, :], PS[1][:, 0:GR]).then_inc(mh_done, 1)

                if is_kind(s + 2, DST):
                    hidden(0, -2)
                if is_kind(s - 5, DENSE):
                    n = number(s - 5)
                    act.wait_ge(u_done, t.at(lambda q: number(q) + 1, 5))
                    if n >= 2:
                        act.wait_ge(y_mm, t.at(lambda q: number(q) - 1, 5))
                    act.activation(flat(S1[n % 2]), PS[0][:, 0:GR], ACT.Silu, bias=UB[:, 0:1], scale=1.0).then_inc(silu_done, 1)
                if is_kind(s + 1, DST):
                    hidden(3, -1)
                if is_kind(s + 2, DST):
                    hidden(1, -2)
                if exists(s - 4):
                    q = s - 4
                    act.wait_ge(z_done, t.at(lambda q: q + 1, 4))
                    if is_kind(q - 2, DST):
                        act.wait_ge(zh_done, t.at(lambda q: number(q) + 1, 6))
                    if is_kind(q - 2, DENSE):
                        act.wait_ge(y_mm, t.at(lambda q: number(q) + 1, 6))
                    if is_kind(q - 2, SRC, DST):
                        act.wait_ge(h1_stored[q % 2], t.at(lambda q: stores(q, SRC, DST), 6))
                    for u in range(G):
                        ins = act.activation(H1[q % 2][:, u, :], Z[q % 4][:, u, :], ACT.Relu,
                                             bias=nb[:, 2, u:u + 1], scale=rs[:, 2, u:u + 1])
                    ins.then_inc(h1_done, 1)
                i, n, there = message(t, 3)
                if there:
                    act.wait_ge(mm_done, i + 1)
                    if n < 2:
                        act.wait_ge(v_stored[n % 2], 16 * (NG // 2))
                    else:
                        act.wait_ge(msg_stored[n % 2], t.at(lambda q: 16 * ((q - MSG0) // 2), 3))
                    act.activation(flat(V[n % 2]), PS[3][:, 0:GR], ACT.Silu).then_inc(msg_done, 1)
                update_act(act, t)

            run(act, step, -1, TICKS, loops)

        @block.tensor
        def _(pe):
            pe.wait_ge(prep, SETUP_STEPS)
            pe.matmul(PS[1][:, 0:1], ONES[:], BAD[:, 0:1], start=True, stop=True)
            pe.matmul(PS[2][:, 0:D], ONE3[:], B3[:, 0, 0, :], start=True, stop=False)
            for c in range(HC):
                ins = pe.matmul(PS[2][:, 0:D], RB[:, c, :], W2[:, c, :], start=False, stop=(c == HC - 1))
            ins.then_inc(prep_pe, 1)
            pe.wait_ge(ready, 1)

            def step(t):
                s = t.s

                def hidden(c, back):
                    if c == 0:
                        pe.wait_ge(ut_done, t.at(lambda q: number(q) + 1, back))
                    else:
                        pe.wait_ge(hid_act, t.at(lambda q: number(q) * HC + c, back))
                    for lo, hi in HALVES:
                        ins = pe.matmul(PS[1][:, lo:hi], W1[:, c * P:(c + 1) * P], UT[:, lo:hi], start=True, stop=True)
                    ins.then_inc(hid_mm, 1)

                def aggregate(c, back):
                    if c == 0:
                        if number(s - back) >= 1:
                            pe.wait_ge(g_done, t.at(lambda q: q - 1, back))
                        else:
                            pe.wait_ge(qe_done, NG)
                        bias(pe, PS[3], 0)
                    pe.wait_ge(hid_act, t.at(lambda q: number(q) * HC + c + 1, back))
                    for u in range(G):
                        ins = pe.matmul(PS[3][:, u * P:(u + 1) * P], HD[:, c, u * P:(u + 1) * P], W2[:, c, :],
                                        start=False, stop=(c == HC - 1), skip_group_check=True)
                    ins.then_inc(agg_mm, 1)

                if is_kind(s, DST):
                    aggregate(2, 0)
                if is_kind(s + 2, DST):
                    n = number(s + 2)
                    pe.wait_ge(window_loaded[n % 2], t.at(lambda q: ring(q, 32), -2))
                    pe.wait_ge(eq_done, t.at(lambda q: number(q) + 1, -2))
                    if n >= 1:
                        pe.wait_ge(hid_act, t.at(lambda q: number(q) * HC, -2))
                    else:
                        pe.wait_ge(et_out, NG)
                    neighbour_sums(pe, PS[1], VG[n % 2]).then_inc(seg_done, 1)
                if is_kind(s + 1, DST):
                    hidden(2, -1)
                if is_kind(s - 6, DENSE):
                    n = number(s - 6)
                    if n >= 1:
                        pe.wait_ge(y_done, t.at(lambda q: number(q), 6))
                    bias(pe, PS[2], 2)
                    for lo, hi in HALVES:
                        pe.matmul(PS[2][:, lo:hi], ID[:], flat(H1[(s - 6) % 2])[:, lo:hi], start=False, stop=False,
                                  skip_group_check=True)
                    pe.wait_ge(silu_done, t.at(lambda q: number(q) + 1, 6))
                    for u in range(G):
                        ins = pe.matmul(PS[2][:, u * P:(u + 1) * P], S1[n % 2][:, u, :], U2[:],
                                        start=False, stop=True, skip_group_check=True)
                    ins.then_inc(y_mm, 1)
                if is_kind(s - 5, DENSE):
                    pe.wait_ge(h1_done, t.at(lambda q: q + 1, 5))
                    if number(s - 5) >= 1:
                        pe.wait_ge(silu_done, t.at(lambda q: number(q), 5))
                    for u in range(G):
                        ins = pe.transpose(PS[0][:, u * P:(u + 1) * P], H1[(s - 5) % 2][:, u, :], ID[:])
                    ins.then_inc(t_done, 1)
                if is_kind(s, SRC):
                    n = number(s)
                    pe.wait_ge(e_loaded[n % 2], t.at(ring))
                    if n >= 1:
                        pe.wait_ge(et_out, t.at(number))
                    for u in range(G):
                        ins = pe.transpose(PS[1][:, u * P:(u + 1) * P], E[n % 2][:, u, :], ID[:])
                    ins.then_inc(et_done, 1)
                i, n, there = message(t, 2)
                if there:
                    pe.wait_ge(over[n % 4], t.at(lambda q: 16 * G * ((q - MSG0) // 4 + 1), 2))
                    if n == 0:
                        pe.wait_ge(hid_act, HC * NG)
                    else:
                        pe.wait_ge(mh_done, i)
                    for u in range(G):
                        ins = pe.transpose(PS[1][:, u * P:(u + 1) * P], MH[n % 4][:, u, :], ID[:])
                    ins.then_inc(mt_done, 1)
                if is_kind(s + 1, DST):
                    hidden(3, -1)
                if is_kind(s, DST):
                    aggregate(3, 0)
                if is_kind(s + 2, DST):
                    hidden(0, -2)
                if is_kind(s - 5, DENSE):
                    pe.wait_ge(ht_done, t.at(lambda q: number(q) + 1, 5))
                    for lo, hi in HALVES:
                        ins = pe.matmul(PS[0][:, lo:hi], UW[:, 0, :], flat(HT[number(s - 5) % 2])[:, lo:hi], start=True, stop=True)
                    ins.then_inc(u_done, 1)
                if is_kind(s - 1, SRC):
                    n = number(s - 1)
                    if n >= 1:
                        pe.wait_ge(qe_done, t.at(number, 1))
                    bias(pe, PS[3], 1)
                    pe.wait_ge(et_out, t.at(lambda q: number(q) + 1, 1))
                    for u in range(G):
                        ins = pe.matmul(PS[3][:, u * P:(u + 1) * P], HD[:, n % 2, u * P:(u + 1) * P], MW[:, 1, :],
                                        start=False, stop=True, skip_group_check=True)
                    ins.then_inc(qe_mm, 1)
                i, n, there = message(t, 3)
                if there:
                    if n == 0:
                        pe.wait_ge(g_done, LAST_DST + 1)
                    else:
                        pe.wait_ge(msg_done, i)
                    pe.wait_ge(qm_in[n % 4], t.at(lambda q: 16 * ((q - MSG0) // 4 + 1), 3))
                    for lo, hi in HALVES:
                        pe.matmul(PS[3][:, lo:hi], ID[:], flat(MQ[n % 4])[:, lo:hi], start=True, stop=False,
                                  skip_group_check=True)
                    pe.wait_ge(mh_done, i + 1)
                    for u in range(G):
                        ins = pe.matmul(PS[3][:, u * P:(u + 1) * P], HD[:, n % 2, u * P:(u + 1) * P], MW[:, 0, :],
                                        start=False, stop=True, skip_group_check=True)
                    ins.then_inc(mm_done, 1)
                if is_kind(s + 1, DST):
                    aggregate(0, -1)
                    aggregate(1, -1)
                if is_kind(s + 2, DST):
                    hidden(1, -2)
                update_pe(pe, t)

            def meet1():
                pe.wait_ge(mh_done, NG)
                sums_pe(pe, 1)

            run(pe, step, -1, TICKS, loops, {MEET: lambda: sums_pe(pe, 0), MEET1: meet1})

        @block.vector
        def _(dve):
            setup_vector(dve)

            def chain(t, k):
                s = t.s
                if not 0 <= s - 1 < NQ + 4:
                    return
                st, rs, nb = ST[(s - 1) % 2], RS[(s - 1) % 2], NB[(s - 1) % 2]
                total, diff, m2, sq, var, r, a, b = (CS[:, i] for i in range(8))
                need = {0: 0, 1: 0, 2: 0, 3: 2, 4: 4, 5: 5}.get(k, k)
                if need:
                    dve.wait_ge(chain_done, t.at(lambda q: CHAIN * q + need, 1))
                if k == 0:
                    if s >= 2:
                        dve.wait_ge(chain_done, t.at(lambda q: CHAIN * q, 1))
                    dve.wait_ge(st_done, t.at(lambda q: q + 1, 1))
                    if s >= 3:
                        last = 7 if exists(s - 7) else 5 if exists(s - 5) else 3
                        dve.wait_ge({7: h1_done, 5: n_done, 3: h_done}[last], t.at(lambda q: q + 1, last))
                if k == 0:
                    ins = dve.tensor_tensor(total, st[:, :, :, 1], st[:, :, :, 4], ALU.add)
                elif k == 1:
                    ins = dve.tensor_tensor(diff, st[:, :, :, 1], st[:, :, :, 4], ALU.subtract)
                elif k == 2:
                    ins = dve.scalar_tensor_tensor(out=m2, in0=st[:, :, :, 2], scalar=EPS * D, in1=st[:, :, :, 5],
                                                   op0=ALU.add, op1=ALU.add)
                elif k == 3:
                    ins = dve.scalar_tensor_tensor(out=sq, in0=diff, scalar=0.25, in1=diff, op0=ALU.mult, op1=ALU.mult)
                elif k == 4:
                    ins = dve.scalar_tensor_tensor(out=var, in0=m2, scalar=1.0 / D, in1=sq, op0=ALU.mult, op1=ALU.add)
                elif k == 5:
                    ins = dve.tensor_scalar(r.bitcast(I32), var.bitcast(I32), -0.5, MAGIC, ALU.mult, ALU.add)
                elif k < 15:
                    if k % 3 == 0:
                        ins = dve.tensor_tensor(a, r, r, ALU.mult)
                    elif k % 3 == 1:
                        ins = dve.scalar_tensor_tensor(out=b, in0=var, scalar=-0.5, in1=a, op0=ALU.mult, op1=ALU.mult)
                    else:
                        ins = dve.scalar_tensor_tensor(out=rs[:] if k == 14 else r, in0=b, scalar=1.5, in1=r,
                                                       op0=ALU.add, op1=ALU.mult)
                else:
                    ins = dve.scalar_tensor_tensor(out=nb[:], in0=total, scalar=-0.5, in1=rs[:], op0=ALU.mult, op1=ALU.mult)
                ins.then_inc(chain_done, 1)

            def step(t):
                s = t.s
                stats = None
                chain(t, 0)
                chain(t, 1)
                chain(t, 2)
                if exists(s):
                    wait_x(dve, t, x_loaded, x_gathered)
                for u in range(G):
                    if exists(s):
                        stats = dve.bn_stats(ST[s % 2][:, 0, u, :], X[s % 4][:, u, :])
                    chain(t, 3 + u)
                if exists(s - 2):
                    w = W[(s - 2) % 4]
                    dve.wait_ge(h_done, t.at(lambda q: q + 1, 2))
                    if is_kind(s - 2, SRC):
                        n = number(s - 2)
                        dve.wait_ge(e_loaded[n % 2], t.at(ring, 2))
                        if n >= 2:
                            dve.wait_ge(v_stored[n % 2], t.at(lambda q: ring(q) - 16, 2))
                        dve.tensor_tensor(V[n % 2][:], w[:], E[n % 2][:], ALU.add).then_inc(v_done, 1)
                    if is_kind(s - 2, DST):
                        dve.wait_ge(agg_mm, t.at(lambda q: (number(q) + 1) * HC, 2))
                        dve.tensor_tensor(flat(w), flat(w), PS[3][:, 0:GR], ALU.add).then_inc(g_done, 1)
                    else:
                        dve.tensor_tensor(w[:], w[:], each(CR), ALU.add).then_inc(g_done, 1)
                chain(t, 10)
                if exists(s - 4) and not mul_on_pool(s - 4):
                    dve.wait_ge(n_done, t.at(lambda q: q + 1, 4))
                    dve.tensor_tensor(W[s % 4][:], W[s % 4][:], each(GM), ALU.mult).then_inc(dve_mul_done, 1)
                chain(t, 11)
                if exists(s - 2):
                    dve.wait_ge(g_done, t.at(lambda q: q + 1, 2))
                for u in range(G):
                    if exists(s - 2):
                        stats = dve.bn_stats(ST[s % 2][:, 1, u, :], W[(s - 2) % 4][:, u, :])
                    if u < 4:
                        chain(t, 12 + u)
                    if u == 4 and exists(s - 4):
                        if mul_on_pool(s - 4):
                            dve.wait_ge(mul_done, t.at(pool_muls, 4))
                        else:
                            dve.wait_ge(dve_mul_done, t.at(lambda q: q + 1 - pool_muls(q), 4))
                        dve.wait_ge(x_beta, t.at(lambda q: q + 1, 4))
                        if s >= 8:
                            dve.wait_ge(h1_done, t.at(lambda q: q + 1, 8))
                            if is_kind(s - 8, DST):
                                dve.wait_ge(zh_done, t.at(lambda q: number(q) + 1, 8))
                            if is_kind(s - 8, DENSE):
                                dve.wait_ge(y_done, t.at(lambda q: number(q) + 1, 8))
                        dve.tensor_tensor(Z[s % 4][:], W[s % 4][:], XB[s % 4][:], ALU.add).then_inc(z_done, 1)
                if exists(s - 4):
                    dve.wait_ge(z_done, t.at(lambda q: q + 1, 4))
                    for u in range(G):
                        stats = dve.bn_stats(ST[s % 2][:, 2, u, :], Z[s % 4][:, u, :])
                if stats is not None:
                    stats.then_inc(st_done, 1)
                if is_kind(s + 2, DST):
                    n = number(s + 2)
                    dve.tensor_copy(KC[:], KCF[:, bass.ds(t.at(lambda q: number(q) * G, -2), G + 1)]).then_inc(kc_done, 1)
                    dve.wait_ge(window_loaded[n % 2], t.at(lambda q: ring(q, 32), -2))
                    if n >= 1:
                        dve.wait_ge(seg_done, t.at(lambda q: number(q), -2))
                    dve.wait_ge(kc_done, t.at(lambda q: number(q) + 1, -2))
                    ins = equal_tiles(dve, KR[n % 2])
                    ins.then_inc(eq_done, 1)
                if is_kind(s - 7, DENSE):
                    n = number(s - 7)
                    dve.wait_ge(y_mm, t.at(lambda q: number(q) + 1, 7))
                    if n >= 2:
                        dve.wait_ge(y_stored[n % 2], t.at(lambda q: ring(q) - 16, 7))
                    dve.tensor_tensor(flat(Y[n % 2]), PS[2][:, 0:GR], flat(Z[(s - 7) % 4]), ALU.add).then_inc(y_done, 1)
                if is_kind(s - 6, DENSE):
                    n = number(s - 6)
                    dve.wait_ge(t_done, t.at(lambda q: number(q) + 1, 6))
                    if n >= 2:
                        dve.wait_ge(u_done, t.at(lambda q: number(q) - 1, 6))
                    dve.tensor_copy(flat(HT[n % 2]), PS[0][:, 0:GR]).then_inc(ht_done, 1)
                update_vector(dve, t)

            def meet1():
                dve.wait_ge(mm_done, NG)
                sums_vector(dve, 1)

            run(dve, step, -1, TICKS, loops, {MEET + 1: lambda: sums_vector(dve, 0), MEET1 + 1: meet1})


def kernel(x, src, dst, edge_attr_128, L0_gnn_W1, L0_gnn_b1, L0_gnn_W2, L0_gnn_b2, L0_gnn_gamma, L0_gnn_beta,
           L1_gnn_mw1, L1_gnn_mb1, L1_gnn_uw1, L1_gnn_ub1, L1_gnn_uw2, L1_gnn_ub2):
    import numpy as np
    import concourse.bacc as bacc
    from concourse.bass_utils import run_bass_kernel_spmd

    n, d = x.shape
    edges = src.shape[0]
    tiles_ = -(-edges // GR) * G
    padded = tiles_ * P
    src_p = np.zeros(padded, np.int32)
    src_p[:edges] = np.asarray(src)
    keys = np.arange(n - edges, n - edges + padded + P, dtype=np.int32)
    keys[:edges] = np.asarray(dst)
    prev = np.concatenate([np.full(1, -1, np.int32), keys[:padded - 1]])
    e_p = np.zeros((padded, d), np.float32)
    e_p[:edges] = np.asarray(edge_attr_128)

    def by_tile(a):
        return np.ascontiguousarray(a.reshape(-1, P).T)

    arrays = {
        "x": x, "e": e_p, "src_t": by_tile(src_p), "dst_t": by_tile(keys), "prev_t": by_tile(prev), "keys": keys,
        "after": np.arange(padded, 0, -1, dtype=np.float32), "ident": np.eye(P, dtype=np.float32), "edge_no": by_tile(np.arange(padded, dtype=np.int32)),
        "w1": L0_gnn_W1, "b1": np.asarray(L0_gnn_b1).reshape(-1, P).T, "w2": L0_gnn_W2, "b2": L0_gnn_b2, "gamma": L0_gnn_gamma, "beta": L0_gnn_beta,
        "mw1": L1_gnn_mw1, "mb1": L1_gnn_mb1, "uw1": L1_gnn_uw1, "ub1": L1_gnn_ub1, "uw2": L1_gnn_uw2, "ub2": L1_gnn_ub2,
    }
    arrays = {f"in_{k}": np.ascontiguousarray(a) for k, a in arrays.items()}
    nc = bacc.Bacc("TRN2", target_bir_lowering=False, num_devices=1)
    aps = [nc.dram_tensor(k, a.shape, mybir.dt.from_np(a.dtype), kind="ExternalInput").ap() for k, a in arrays.items()]
    out = nc.dram_tensor("out", (n, d), F32, kind="ExternalOutput").ap()
    gnn_program(nc, *aps, out)
    r = run_bass_kernel_spmd(nc, [arrays], core_ids=[0])
    return r.results[0]["out"]
```
